# Optimizing a Trainium2 kernel written in Bass

```python
import numpy as np
import jax
import jax.numpy as jnp

def _softmax(x, axis=-1):
    return jax.nn.softmax(x, axis=axis)

def _gelu(x):
    return jax.nn.gelu(x, approximate=True)

def _silu(x):
    return jax.nn.silu(x)

def _sigmoid(x):
    return jax.nn.sigmoid(x)

def _layernorm(x, axis=-1, eps=1e-05):
    m = jnp.mean(x, axis=axis, keepdims=True)
    v = jnp.var(x, axis=axis, keepdims=True)
    return (x - m) / jnp.sqrt(v + eps)

def _scatter_add(tgt, idx, src, axis=0):
    return tgt.at[idx].add(src)

def _segment_sum(src, seg, n):
    return jax.ops.segment_sum(src, seg, n)
kernel_name = 'mk_decoder_postln_d2_seqx_r4_cca4ea'

def setup_inputs(seed: int=0):
    np.random.seed(seed)
    _w = jnp.asarray

    def _rec_inputs():
        import jax
        import jax.numpy as jnp
        _rk = jax.random.key(seed)
        x = -7.109e-05 + 0.9999 * jax.random.normal(jax.random.fold_in(_rk, 1), (4, 512, 512), jnp.float32)
        _lenS = 512 - jax.random.randint(jax.random.fold_in(_rk, 7), (4,), 0, max(1, 512 // 4) + 1, jnp.int32)
        _lenS2 = 512 - jax.random.randint(jax.random.fold_in(_rk, 8), (4,), 0, max(1, 512 // 4) + 1, jnp.int32)
        _ctx_512P = jax.random.normal(jax.random.fold_in(_rk, 11), (4, 16, 128), jnp.float32)
        _ctx_512c = jax.random.dirichlet(jax.random.fold_in(_rk, 511), 0.3 * jnp.ones((16,), jnp.float32), (4, 512))
        _ctx_512t = jnp.einsum('bsk,bkd->bsd', _ctx_512c, _ctx_512P)
        _ctx_512t = _ctx_512t * jax.lax.rsqrt(jnp.mean(jnp.square(_ctx_512t)) + 1e-12) * 0.953939
        ctx_512 = 2.81802e-05 + 1.00001 * (_ctx_512t + 0.3 * jax.random.normal(jax.random.fold_in(_rk, 611), (4, 512, 128), jnp.float32))
        return (x, ctx_512)
    x, ctx_512 = _rec_inputs()

    def _L0_attn_setup():
        import jax, jax.numpy as jnp
        import numpy as np
        BATCH, SEQ, EMBED, STATE = (4, 512, 512, 16)
        key = jax.random.key(seed)
        ks = jax.random.split(key, 8)
        s = 0.02
        return {'x': jax.random.normal(ks[0], (BATCH, SEQ, EMBED), jnp.float32), 'proj_in_w': jax.random.normal(ks[1], (EMBED, EMBED), jnp.float32) * s, 'proj_in_b': jnp.zeros((EMBED,), jnp.float32), 'proj_out_w': jax.random.normal(ks[2], (EMBED, EMBED), jnp.float32) * s, 'proj_out_b': jnp.zeros((EMBED,), jnp.float32), 'A': jax.random.normal(ks[3], (EMBED, STATE), jnp.float32) * 0.01, 'B_w': jax.random.normal(ks[4], (STATE, EMBED), jnp.float32) * s, 'C_w': jax.random.normal(ks[5], (EMBED, STATE), jnp.float32) * s, 'D_param': jnp.ones((EMBED,), jnp.float32)}
    _L0_attn_all = _L0_attn_setup()
    _L0_attn_in = {k: v for k, v in _L0_attn_all.items() if k in ('proj_in_w', 'proj_in_b', 'proj_out_w', 'proj_out_b', 'A', 'B_w', 'C_w', 'D_param')}
    del _L0_attn_all

    def _L0_xattn_setup():
        import jax, jax.numpy as jnp
        import numpy as np
        EPS = 1e-06
        IMAGE_DIMS = 512
        key = jax.random.key(seed)
        k1, k2, k3 = jax.random.split(key, 3)
        B, I, J, D = (16, 512, 512, 128)
        p = jax.random.normal(k1, (B, I, J), dtype=jnp.float32)
        k_v = jax.random.normal(k2, (B, J, D), dtype=jnp.float32)
        W_k = jax.random.normal(k3, (D, D), dtype=jnp.float32) * (1.0 / np.sqrt(D))
        b_k = jnp.zeros((D,), dtype=jnp.float32)
        ln_gamma = jnp.ones((J,), dtype=jnp.float32)
        ln_beta = jnp.zeros((J,), dtype=jnp.float32)
        return {'p': p, 'k_v': k_v, 'W_k': W_k, 'b_k': b_k, 'ln_gamma': ln_gamma, 'ln_beta': ln_beta}
    _L0_xattn_all = _L0_xattn_setup()
    _L0_xattn_in = {k: v for k, v in _L0_xattn_all.items() if k in ('W_k', 'b_k', 'ln_gamma', 'ln_beta')}
    del _L0_xattn_all

    def _L0_ffn_setup():
        import jax, jax.numpy as jnp
        import numpy as np
        H = 512
        key = jax.random.key(seed)
        ks = jax.random.split(key, 10)
        s = 1.0 / np.sqrt(H)
        x = jax.random.normal(ks[0], (4, 512, H), dtype=jnp.float32)
        Wg = jax.random.uniform(ks[1], (2, H), jnp.float32, -s, s)
        W0a = jax.random.uniform(ks[2], (2 * H, H), jnp.float32, -s, s)
        b0a = jax.random.uniform(ks[3], (2 * H,), jnp.float32, -s, s)
        W0b = jax.random.uniform(ks[4], (H, 2 * H), jnp.float32, -s, s)
        b0b = jax.random.uniform(ks[5], (H,), jnp.float32, -s, s)
        W1a = jax.random.uniform(ks[6], (2 * H, H), jnp.float32, -s, s)
        b1a = jax.random.uniform(ks[7], (2 * H,), jnp.float32, -s, s)
        W1b = jax.random.uniform(ks[8], (H, 2 * H), jnp.float32, -s, s)
        b1b = jax.random.uniform(ks[9], (H,), jnp.float32, -s, s)
        return {'x': x, 'Wg': Wg, 'W0a': W0a, 'b0a': b0a, 'W0b': W0b, 'b0b': b0b, 'W1a': W1a, 'b1a': b1a, 'W1b': W1b, 'b1b': b1b}
    _L0_ffn_all = _L0_ffn_setup()
    _L0_ffn_in = {k: v for k, v in _L0_ffn_all.items() if k in ('Wg', 'W0a', 'b0a', 'W0b', 'b0b', 'W1a', 'b1a', 'W1b', 'b1b')}
    del _L0_ffn_all

    def _L1_attn_setup():
        import jax, jax.numpy as jnp
        import numpy as np
        B, N, E, H = (1, 1024, 512, 16)
        D = E // H
        DEGREE = 4
        LN_EPS = 1e-05
        ROPE_BASE = 10000.0

        def rope_cos_sin(n, d):
            inv_freq = 1.0 / ROPE_BASE ** (jnp.arange(0, d, 2, dtype=jnp.float32) / d)
            t = jnp.arange(n, dtype=jnp.float32)[:, None] * inv_freq[None, :]
            return (jnp.cos(t), jnp.sin(t))

        def apply_rope(x, cos, sin):
            x1, x2 = jnp.split(x, 2, axis=-1)
            c = cos[None, :, None, :]
            s = sin[None, :, None, :]
            return jnp.concatenate([x1 * c - x2 * s, x1 * s + x2 * c], axis=-1)

        def layernorm(x, scale, bias, eps=LN_EPS):
            m = jnp.mean(x, axis=-1, keepdims=True)
            v = jnp.var(x, axis=-1, keepdims=True)
            return (x - m) * jax.lax.rsqrt(v + eps) * scale + bias

        def polynomial_attention(q, k, v, degree, is_causal):
            a = jnp.einsum('bhnd,bhmd->bhnm', q, k) ** degree
            if is_causal:
                a = jnp.tril(a)
            denom = jnp.sum(a, axis=-1, keepdims=True)
            return jnp.einsum('bhnm,bhmd->bhnd', a / denom, v)
        key = jax.random.key(seed)
        k0, k1, k2 = jax.random.split(key, 3)
        x = jax.random.normal(k0, (B, N, E), dtype=jnp.float32)
        w_qkv = jax.random.normal(k1, (E, 3 * E), dtype=jnp.float32) * (1.0 / np.sqrt(E))
        w_out = jax.random.normal(k2, (E, E), dtype=jnp.float32) * (1.0 / np.sqrt(E))
        ln_scale = jnp.ones((D,), dtype=jnp.float32)
        ln_bias = jnp.zeros((D,), dtype=jnp.float32)
        return {'x': x, 'w_qkv': w_qkv, 'w_out': w_out, 'ln_scale': ln_scale, 'ln_bias': ln_bias}
    _L1_attn_all = _L1_attn_setup()
    _L1_attn_in = {k: v for k, v in _L1_attn_all.items() if k in ('w_qkv', 'w_out', 'ln_scale', 'ln_bias')}
    del _L1_attn_all

    def _L1_xattn_setup():
        import jax, jax.numpy as jnp
        import numpy as np
        N_HEADS = 16
        N_KV_HEADS = 4
        ROPE_THETA = 10000.0
        EPS = 1e-05

        def _rms_norm(x, w):
            var = jnp.mean(x * x, axis=-1, keepdims=True)
            return x * jax.lax.rsqrt(var + EPS) * w

        def _rope_sin_cos(T, head_dim, dtype):
            inv_freq = 1.0 / ROPE_THETA ** (jnp.arange(0, head_dim, 2, dtype=jnp.float32) / head_dim)
            t = jnp.arange(T, dtype=jnp.float32)
            freqs = jnp.outer(t, inv_freq)
            emb = jnp.concatenate([freqs, freqs], -1)
            return (jnp.sin(emb).astype(dtype)[None, None], jnp.cos(emb).astype(dtype)[None, None])

        def _rotate_half(x):
            h = x.shape[-1] // 2
            x1, x2 = (x[..., :h], x[..., h:])
            return jnp.concatenate([-x2, x1], axis=-1)
        key = jax.random.key(seed)
        ks = jax.random.split(key, 6)
        B, T, C = (2, 512, 512)
        Ckv = C // N_HEADS * N_KV_HEADS
        return {'q': jax.random.normal(ks[0], (B, T, C), jnp.float32), 'k': jax.random.normal(ks[1], (B, T, Ckv), jnp.float32), 'v': jax.random.normal(ks[2], (B, T, Ckv), jnp.float32), 'q_norm_w': jnp.ones((C,), jnp.float32), 'k_norm_w': jnp.ones((Ckv,), jnp.float32), 'w_out': jax.random.normal(ks[3], (C, C), jnp.float32) * C ** (-0.5)}
    _L1_xattn_all = _L1_xattn_setup()
    _L1_xattn_in = {k: v for k, v in _L1_xattn_all.items() if k in ('q_norm_w', 'k_norm_w', 'w_out')}
    del _L1_xattn_all

    def _L1_ffn_setup():
        import jax, jax.numpy as jnp
        import numpy as np
        B, S, H = (1, 256, 512)
        E = 32
        K = 4
        I = 192
        SI = 1024
        WSCALE = 0.02
        key = jax.random.key(seed)
        ks = jax.random.split(key, 8)
        inp = {'hidden_states': jax.random.normal(ks[0], (B, S, H), jnp.float32), 'router_w': jax.random.normal(ks[1], (H, E), jnp.float32) * WSCALE, 'w_gate': jax.random.normal(ks[2], (E, H, I), jnp.float32) * WSCALE, 'w_up': jax.random.normal(ks[3], (E, H, I), jnp.float32) * WSCALE, 'w_down': jax.random.normal(ks[4], (E, I, H), jnp.float32) * WSCALE, 'ws_gate': jax.random.normal(ks[5], (H, SI), jnp.float32) * WSCALE, 'ws_up': jax.random.normal(ks[6], (H, SI), jnp.float32) * WSCALE, 'ws_down': jax.random.normal(ks[7], (SI, H), jnp.float32) * WSCALE}
        return inp
    _L1_ffn_all = _L1_ffn_setup()
    _L1_ffn_in = {k: v for k, v in _L1_ffn_all.items() if k in ('router_w', 'w_gate', 'w_up', 'w_down', 'ws_gate', 'ws_up', 'ws_down')}
    del _L1_ffn_all
    return {'x': x, 'ctx_512': ctx_512, 'L0_attn_proj_in_w': _L0_attn_in['proj_in_w'], 'L0_attn_proj_in_b': _L0_attn_in['proj_in_b'], 'L0_attn_proj_out_w': _L0_attn_in['proj_out_w'], 'L0_attn_proj_out_b': _L0_attn_in['proj_out_b'], 'L0_attn_A': _L0_attn_in['A'], 'L0_attn_B_w': _L0_attn_in['B_w'], 'L0_attn_C_w': _L0_attn_in['C_w'], 'L0_attn_D_param': _L0_attn_in['D_param'], 'L0_xattn_W_k': _L0_xattn_in['W_k'], 'L0_xattn_b_k': _L0_xattn_in['b_k'], 'L0_xattn_ln_gamma': _L0_xattn_in['ln_gamma'], 'L0_xattn_ln_beta': _L0_xattn_in['ln_beta'], 'L0_ffn_Wg': _L0_ffn_in['Wg'], 'L0_ffn_W0a': _L0_ffn_in['W0a'], 'L0_ffn_b0a': _L0_ffn_in['b0a'], 'L0_ffn_W0b': _L0_ffn_in['W0b'], 'L0_ffn_b0b': _L0_ffn_in['b0b'], 'L0_ffn_W1a': _L0_ffn_in['W1a'], 'L0_ffn_b1a': _L0_ffn_in['b1a'], 'L0_ffn_W1b': _L0_ffn_in['W1b'], 'L0_ffn_b1b': _L0_ffn_in['b1b'], 'L1_attn_w_qkv': _L1_attn_in['w_qkv'], 'L1_attn_w_out': _L1_attn_in['w_out'], 'L1_attn_ln_scale': _L1_attn_in['ln_scale'], 'L1_attn_ln_bias': _L1_attn_in['ln_bias'], 'L1_xattn_q_norm_w': _L1_xattn_in['q_norm_w'], 'L1_xattn_k_norm_w': _L1_xattn_in['k_norm_w'], 'L1_xattn_w_out': _L1_xattn_in['w_out'], 'L1_ffn_router_w': _L1_ffn_in['router_w'], 'L1_ffn_w_gate': _L1_ffn_in['w_gate'], 'L1_ffn_w_up': _L1_ffn_in['w_up'], 'L1_ffn_w_down': _L1_ffn_in['w_down'], 'L1_ffn_ws_gate': _L1_ffn_in['ws_gate'], 'L1_ffn_ws_up': _L1_ffn_in['ws_up'], 'L1_ffn_ws_down': _L1_ffn_in['ws_down']}

def reference(x, ctx_512, L0_attn_proj_in_w, L0_attn_proj_in_b, L0_attn_proj_out_w, L0_attn_proj_out_b, L0_attn_A, L0_attn_B_w, L0_attn_C_w, L0_attn_D_param, L0_xattn_W_k, L0_xattn_b_k, L0_xattn_ln_gamma, L0_xattn_ln_beta, L0_ffn_Wg, L0_ffn_W0a, L0_ffn_b0a, L0_ffn_W0b, L0_ffn_b0b, L0_ffn_W1a, L0_ffn_b1a, L0_ffn_W1b, L0_ffn_b1b, L1_attn_w_qkv, L1_attn_w_out, L1_attn_ln_scale, L1_attn_ln_bias, L1_xattn_q_norm_w, L1_xattn_k_norm_w, L1_xattn_w_out, L1_ffn_router_w, L1_ffn_w_gate, L1_ffn_w_up, L1_ffn_w_down, L1_ffn_ws_gate, L1_ffn_ws_up, L1_ffn_ws_down):
    import jax
    import jax.numpy as jnp

    def _L0_attn_ref(x, proj_in_w, proj_in_b, proj_out_w, proj_out_b, A, B_w, C_w, D_param):
        import jax, jax.numpy as jnp
        import numpy as np
        BATCH, SEQ, EMBED, STATE = (4, 512, 512, 16)
        x_proj = x @ proj_in_w.T + proj_in_b
        delta = jax.nn.softplus(x_proj @ B_w.T)
        sigA = jax.nn.sigmoid(A)
        Bsz, L, D = x.shape
        S = A.shape[1]

        def step(h, inp):
            x_t, d_t = inp
            h = h * sigA + x_t[:, :, None] * d_t[:, None, :]
            y_t = h.sum(axis=1) @ C_w.T + D_param * x_t
            return (h, y_t)
        h0 = jnp.zeros((Bsz, D, S), x.dtype)
        xs = (jnp.swapaxes(x_proj, 0, 1), jnp.swapaxes(delta, 0, 1))
        _, ys = jax.lax.scan(step, h0, xs)
        y = jnp.swapaxes(ys, 0, 1)
        y = y @ proj_out_w.T + proj_out_b
        return y + x

    def _L0_xattn_ref(p, k_v, W_k, b_k, ln_gamma, ln_beta):
        import jax, jax.numpy as jnp
        import numpy as np
        EPS = 1e-06
        IMAGE_DIMS = 512
        kv = k_v @ W_k.T + b_k
        out = jnp.einsum('bij,bjd->bid', p, kv)
        scale = IMAGE_DIMS ** (-0.5)
        sim = jnp.einsum('bid,bjd->bij', out, kv) * scale
        mu = jnp.mean(sim, axis=-1, keepdims=True)
        var = jnp.var(sim, axis=-1, keepdims=True)
        sim = (sim - mu) * jax.lax.rsqrt(var + EPS) * ln_gamma + ln_beta
        attn = jax.nn.softmax(sim, axis=-1)
        return attn

    def _L0_ffn_ref(x, Wg, W0a, b0a, W0b, b0b, W1a, b1a, W1b, b1b):
        import jax, jax.numpy as jnp
        import numpy as np
        H = 512
        scores = jax.nn.softmax(jnp.einsum('bsh,eh->bse', x, Wg), axis=-1)
        top_expert = jnp.argmax(scores, axis=-1)
        h0 = jax.nn.gelu(jnp.einsum('bsh,fh->bsf', x, W0a) + b0a, approximate=False)
        out0 = jnp.einsum('bsf,hf->bsh', h0, W0b) + b0b
        h1 = jax.nn.relu(jnp.einsum('bsh,fh->bsf', x, W1a) + b1a)
        out1 = jnp.einsum('bsf,hf->bsh', h1, W1b) + b1b
        mask0 = (top_expert == 0).astype(x.dtype)[..., None]
        return out0 * mask0 + out1 * (1.0 - mask0)

    def _L1_attn_ref(x, w_qkv, w_out, ln_scale, ln_bias):
        import jax, jax.numpy as jnp
        import numpy as np
        B, N, E, H = (1, 1024, 512, 16)
        D = E // H
        DEGREE = 4
        LN_EPS = 1e-05
        ROPE_BASE = 10000.0

        def rope_cos_sin(n, d):
            inv_freq = 1.0 / ROPE_BASE ** (jnp.arange(0, d, 2, dtype=jnp.float32) / d)
            t = jnp.arange(n, dtype=jnp.float32)[:, None] * inv_freq[None, :]
            return (jnp.cos(t), jnp.sin(t))

        def apply_rope(x, cos, sin):
            x1, x2 = jnp.split(x, 2, axis=-1)
            c = cos[None, :, None, :]
            s = sin[None, :, None, :]
            return jnp.concatenate([x1 * c - x2 * s, x1 * s + x2 * c], axis=-1)

        def layernorm(x, scale, bias, eps=LN_EPS):
            m = jnp.mean(x, axis=-1, keepdims=True)
            v = jnp.var(x, axis=-1, keepdims=True)
            return (x - m) * jax.lax.rsqrt(v + eps) * scale + bias

        def polynomial_attention(q, k, v, degree, is_causal):
            a = jnp.einsum('bhnd,bhmd->bhnm', q, k) ** degree
            if is_causal:
                a = jnp.tril(a)
            denom = jnp.sum(a, axis=-1, keepdims=True)
            return jnp.einsum('bhnm,bhmd->bhnd', a / denom, v)
        b, n, e = x.shape
        proj = x @ w_qkv
        q, k, v = jnp.split(proj, 3, axis=-1)
        q = q.reshape(b, n, H, D)
        k = k.reshape(b, n, H, D)
        v = v.reshape(b, n, H, D)
        cos, sin = rope_cos_sin(n, D)
        q = apply_rope(q, cos, sin)
        k = apply_rope(k, cos, sin)
        q = q.transpose(0, 2, 1, 3)
        k = k.transpose(0, 2, 1, 3)
        v = v.transpose(0, 2, 1, 3)
        q = layernorm(q, ln_scale, ln_bias)
        k = layernorm(k, ln_scale, ln_bias)
        out = polynomial_attention(q, k, v, DEGREE, True)
        out = out.transpose(0, 2, 1, 3).reshape(b, n, e)
        out = out @ w_out
        return out

    def _L1_xattn_ref(q, k, v, q_norm_w, k_norm_w, w_out):
        import jax, jax.numpy as jnp
        import numpy as np
        N_HEADS = 16
        N_KV_HEADS = 4
        ROPE_THETA = 10000.0
        EPS = 1e-05

        def _rms_norm(x, w):
            var = jnp.mean(x * x, axis=-1, keepdims=True)
            return x * jax.lax.rsqrt(var + EPS) * w

        def _rope_sin_cos(T, head_dim, dtype):
            inv_freq = 1.0 / ROPE_THETA ** (jnp.arange(0, head_dim, 2, dtype=jnp.float32) / head_dim)
            t = jnp.arange(T, dtype=jnp.float32)
            freqs = jnp.outer(t, inv_freq)
            emb = jnp.concatenate([freqs, freqs], -1)
            return (jnp.sin(emb).astype(dtype)[None, None], jnp.cos(emb).astype(dtype)[None, None])

        def _rotate_half(x):
            h = x.shape[-1] // 2
            x1, x2 = (x[..., :h], x[..., h:])
            return jnp.concatenate([-x2, x1], axis=-1)
        B, T, C = q.shape
        hd = C // N_HEADS
        g = N_HEADS // N_KV_HEADS
        q = _rms_norm(q, q_norm_w)
        k = _rms_norm(k, k_norm_w)
        q = q.reshape(B, T, N_HEADS, hd).transpose(0, 2, 1, 3)
        k = k.reshape(B, T, N_KV_HEADS, hd).transpose(0, 2, 1, 3)
        v = v.reshape(B, T, N_KV_HEADS, hd).transpose(0, 2, 1, 3)
        sin, cos = _rope_sin_cos(T, hd, q.dtype)
        q = q * cos + _rotate_half(q) * sin
        k = k * cos + _rotate_half(k) * sin
        qg = q.reshape(B, N_KV_HEADS, g, T, hd)
        scale = 1.0 / jnp.sqrt(jnp.asarray(hd, q.dtype))
        scores = jnp.einsum('bgnqd,bgkd->bgnqk', qg, k) * scale
        causal = jnp.tril(jnp.ones((T, T), bool))
        scores = jnp.where(causal, scores, jnp.asarray(-1e+30, scores.dtype))
        attn = jax.nn.softmax(scores, axis=-1)
        out = jnp.einsum('bgnqk,bgkd->bgnqd', attn, v)
        out = out.reshape(B, N_HEADS, T, hd).transpose(0, 2, 1, 3).reshape(B, T, C)
        return out @ w_out.T

    def _L1_ffn_ref(hidden_states, router_w, w_gate, w_up, w_down, ws_gate, ws_up, ws_down):
        import jax, jax.numpy as jnp
        import numpy as np
        B, S, H = (1, 256, 512)
        E = 32
        K = 4
        I = 192
        SI = 1024
        WSCALE = 0.02
        b, s, h = hidden_states.shape
        x = hidden_states.reshape(-1, h)
        T = x.shape[0]
        shared = jax.nn.silu(x @ ws_gate) * (x @ ws_up) @ ws_down
        logits = x @ router_w
        probs = jax.nn.softmax(logits.astype(jnp.float32), axis=-1)
        topw, topi = jax.lax.top_k(probs, K)
        topw = topw / jnp.sum(topw, axis=-1, keepdims=True)
        topw = topw.astype(hidden_states.dtype)
        combine = jnp.zeros((T, E), hidden_states.dtype).at[jnp.arange(T)[:, None], topi].add(topw)
        g = jnp.einsum('th,ehi->eti', x, w_gate)
        u = jnp.einsum('th,ehi->eti', x, w_up)
        hmid = jax.nn.silu(g) * u
        routed = jnp.einsum('eti,te,eih->th', hmid, combine, w_down)
        return (shared + routed).reshape(b, s, h)
    x = _layernorm(x + _L0_attn_ref(x, L0_attn_proj_in_w, L0_attn_proj_in_b, L0_attn_proj_out_w, L0_attn_proj_out_b, L0_attn_A, L0_attn_B_w, L0_attn_C_w, L0_attn_D_param), axis=-1)
    x = _layernorm(x + _L0_xattn_ref(x, ctx_512, L0_xattn_W_k, L0_xattn_b_k, L0_xattn_ln_gamma, L0_xattn_ln_beta), axis=-1)
    x = _layernorm(x + _L0_ffn_ref(x, L0_ffn_Wg, L0_ffn_W0a, L0_ffn_b0a, L0_ffn_W0b, L0_ffn_b0b, L0_ffn_W1a, L0_ffn_b1a, L0_ffn_W1b, L0_ffn_b1b), axis=-1)
    x = _layernorm(x + _L1_attn_ref(x, L1_attn_w_qkv, L1_attn_w_out, L1_attn_ln_scale, L1_attn_ln_bias), axis=-1)
    x = _layernorm(x + _L1_xattn_ref(x, ctx_512, ctx_512, L1_xattn_q_norm_w, L1_xattn_k_norm_w, L1_xattn_w_out), axis=-1)
    x = _layernorm(x + _L1_ffn_ref(x, L1_ffn_router_w, L1_ffn_w_gate, L1_ffn_w_up, L1_ffn_w_down, L1_ffn_ws_gate, L1_ffn_ws_up, L1_ffn_ws_down), axis=-1)
    return x

_drawn_inputs = setup_inputs


def setup_inputs(seed=0):
    import zlib

    import numpy as np

    out = dict(_drawn_inputs(seed))
    spreads = {'L0_attn_proj_in_b': (0.0, 0.1),
     'L0_attn_proj_out_b': (0.0, 0.1),
     'L0_attn_D_param': (1.0, 0.2),
     'L0_xattn_b_k': (0.0, 0.8),
     'L0_xattn_ln_gamma': (1.0, 0.6),
     'L0_xattn_ln_beta': (0.0, 0.8),
     'L1_attn_ln_scale': (1.0, 0.2),
     'L1_attn_ln_bias': (0.0, 0.1),
     'L1_xattn_q_norm_w': (1.0, 0.2),
     'L1_xattn_k_norm_w': (1.0, 0.2)}
    factors = {'L0_attn_A': 8.0,
     'L0_xattn_W_k': 6.853,
     'L0_ffn_b0a': 6.564,
     'L0_ffn_b0b': 3.023,
     'L0_ffn_b1a': 5.044,
     'L0_ffn_b1b': 2.681,
     'L1_ffn_router_w': 3.948,
     'L1_ffn_w_gate': 3.798,
     'L1_ffn_w_up': 3.712,
     'L1_ffn_w_down': 3.717}
    for name, (base, spread) in spreads.items():
        noise = np.random.default_rng([zlib.crc32(name.encode()), seed]).standard_normal(out[name].shape)
        drawn = base * np.exp(spread * noise) if base else spread * noise
        out[name] = jnp.asarray(drawn.astype(out[name].dtype))
    for name, factor in factors.items():
        out[name] = (out[name] * factor).astype(out[name].dtype)
    return out
```

```python
from contextlib import ExitStack

import concourse.bass as bass
from concourse import mybir

F32 = mybir.dt.float32
BF16 = mybir.dt.bfloat16
I32 = mybir.dt.int32
U32 = mybir.dt.uint32
ALU = mybir.AluOpType
ACT = mybir.ActivationFunctionType
AX_X = mybir.AxisListType.X

P = 128
NB, S, E = 4, 512, 512
NT, KC = S // P, E // P
STATE = 16
CTX = 128
FF = 1024
NF = FF // P
HEADS, HD = 16, 32
HG = P // HD
RING = 4
EXPERTS, TOP = 32, 4
INNER = 192
HALF_IN = INNER // 2
TOK = NB * S
TT = TOK // P
TILES = TOK * TOP // P + EXPERTS
SLOTS = TILES * P
WRING = 4
LN_EPS = 1e-5
SIM_EPS = 1e-6


class Held:
    pass


def run_pass(nc, body):
    with nc.Block() as block:
        body(block)


def residual_norm(nc, st, sem, eng, norm_eps=LN_EPS):
    for j in range(NT):
        eng.wait_ge(sem["row_ready"], j + 1)
        nc.vector.bn_stats(st.stats[:, j, :], st.r[:, j, :]).then_inc(sem["stats_ready"], 1)
    for j in range(NT):
        eng.wait_ge(sem["stats_ready"], j + 1)
        nc.vector.bn_aggr(st.meanvar[:, j, :], st.stats[:, j, :]).then_inc(sem["var_ready"], 1)
    eng.wait_ge(sem["rstd_ready"], 2)
    for j in range(NT):
        nc.vector.tensor_scalar(st.x[:, j, :], st.r[:, j, :], st.meanvar[:, j, 0:1], st.rstd[:, j:j + 1],
                                ALU.subtract, ALU.mult).then_inc(sem["x_ready"], 1)


def norm_scale(nc, st, sem, eng):
    eng.wait_ge(sem["var_ready"], NT)
    nc.scalar.activation(st.lnvar[:, :], st.meanvar[:, :, 1], ACT.Ln, bias=st.eps[:, 0:1]).then_inc(sem["rstd_ready"], 1)
    eng.wait_ge(sem["rstd_ready"], 1)
    nc.scalar.activation(st.rstd[:, :], st.lnvar[:, :], ACT.Exp, scale=-0.5).then_inc(sem["rstd_ready"], 1)
    for j in range(NT):
        eng.wait_ge(sem["xt_psum"], j + 1)
        nc.scalar.activation(st.xT[:, :, j * P:(j + 1) * P],
                             st.ps[:, 4 + j, :].rearrange("p (k t) -> p k t", k=KC), ACT.Copy).then_inc(sem["xt_ready"], 1)


def transpose_rows(nc, st, sem, eng):
    for j in range(NT):
        eng.wait_ge(sem["x_ready"], j + 1)
        for k in range(KC):
            last = nc.tensor.transpose(st.ps[:, 4 + j, k * P:(k + 1) * P], st.x[:, j, k * P:(k + 1) * P],
                                       st.ident[:, :])
        last.then_inc(sem["xt_psum"], 1)


def project_rows(nc, st, eng, out, lhs, j, weights, chunks, bias=None):
    for k in range(chunks):
        last = nc.tensor.matmul(out, lhs[:, k, j * P:(j + 1) * P], weights[:, k, :],
                                start=(k == 0), stop=(k == chunks - 1 and bias is None))
    if bias is not None:
        part = slice(bias, bias + 1)
        last = nc.tensor.matmul(out, st.ones[part, 0:P], st.bias_rows[part, :], start=False, stop=True)
    return last


def recurrence_pass(nc, st, sem, T, b):
    with ExitStack() as ctx:
        sb = lambda name, shape, dt=F32: ctx.enter_context(nc.sbuf_tensor(name, shape, dt))
        xpT = sb("xpT", [P, KC, S])
        delta = sb("delta", [STATE, S])
        pick = sb("pick", [STATE, STATE * P])
        dbc = sb("dbc", [P, 2, S])
        u = sb("u", [P, RING, S])
        h = sb("h", [P, RING, S])
        sums = sb("sums", [P, S])
        yT = h
        absz, expz, logz = (u[0:STATE, n, :] for n in range(3))

        def body(block):
            @block.sync
            def _(sp):
                sp.dma_start(st.xT[:, :, :], T["xT"][bass.ds(b, 1), :, :].rearrange("a (k p) t -> p (a k) t", p=P)
                             ).then_inc(sem["xT_loaded"], 16)
                sp.dma_start(st.x[:, :, :], T["x"][bass.ds(b, 1), :, :].rearrange("a (j p) d -> p (a j) d", p=P)
                             ).then_inc(sem["x_loaded"], 16)
                sp.dma_start(pick[:, :], T["pick"]).then_inc(sem["pick_loaded"], 16)
                sp.dma_start(st.ctxT[:, :], T["ctxT"][bass.ds(b, 1), :, :].rearrange("a c t -> c (a t)")
                             ).then_inc(sem["ctx_loaded"], 16)
                sp.dma_start(st.ctx[:, :, :], T["ctx"][bass.ds(b, 1), :, :].rearrange("a (j p) c -> p (a j) c", p=P)
                             ).then_inc(sem["ctx_loaded"], 16)
                part = T["expert_rows"][bass.ds(b * (SLOTS // NB), SLOTS // NB), :].rearrange("(q p) d -> p q d", p=P)
                sp.dma_start(part, st.zeros[:, :].unsqueeze(1).to_broadcast([P, TILES // NB, E])
                             ).then_inc(sem["stored"], 16)
                sp.wait_ge(sem["ctx_loaded"], 32)
                sp.wait_ge(sem["stored"], 16)

            @block.tensor
            def _(pe):
                pe.wait_ge(sem["xT_loaded"], 16)
                for c in range(KC):
                    for k in range(KC):
                        last = nc.tensor.matmul(st.ps[:, c, :], st.w_in[:, k, c * P:(c + 1) * P], st.xT[:, k, :],
                                                start=(k == 0), stop=(k == KC - 1))
                    last.then_inc(sem["xp_psum"], 1)
                for k in range(KC):
                    pe.wait_ge(sem["xp_ready"], k + 1)
                    last = nc.tensor.matmul(st.ps[0:STATE, 7, :], st.w_b[:, k, :], xpT[:, k, :],
                                            start=(k == 0), stop=(k == KC - 1))
                last.then_inc(sem["z_psum"], 1)
                pe.wait_ge(sem["delta_ready"], 1)

                def spread(s):
                    if s >= 2:
                        pe.wait_ge(sem["spread_copied"], s - 1)
                    nc.tensor.matmul(st.ps[:, 5 + s % 2, :], pick[:, s * P:(s + 1) * P], delta[:, :],
                                     start=True, stop=True).then_inc(sem["spread_psum"], 1)

                pe.wait_ge(sem["pick_loaded"], 16)
                spread(0)
                spread(1)
                for s in range(STATE):
                    for c in range(KC):
                        i = s * KC + c
                        pe.wait_ge(sem["scanned"], i + 1)
                        nc.tensor.matmul(st.ps[c * 32:(c + 1) * 32, 4, :], st.ones_at[:, 32 - s:64 - s],
                                         h[:, i % RING, :], start=(s == 0), stop=(s == STATE - 1),
                                         tile_position=(0, c * 32)).then_inc(sem["summed"], 1)
                    if s + 2 < STATE:
                        spread(s + 2)
                pe.wait_ge(sem["sums_ready"], 1)
                for c in range(KC):
                    nc.tensor.matmul(st.ps[:, c, :], st.w_c[:, c * P:(c + 1) * P], sums[:, :],
                                     start=True, stop=True).then_inc(sem["y_psum"], 1)
                pe.wait_ge(sem["y_ready"], KC)
                for j in range(NT):
                    project_rows(nc, st, pe, st.ps[:, j, :], yT, j, st.w_o, KC, bias=0).then_inc(sem["out_psum"], 1)
                transpose_rows(nc, st, sem, pe)

            @block.scalar
            def _(act):
                for c in range(KC):
                    act.wait_ge(sem["xp_psum"], c + 1)
                    nc.scalar.activation(xpT[:, c, :], st.ps[:, c, :], ACT.Identity,
                                         bias=st.b_in[:, c:c + 1]).then_inc(sem["xp_ready"], 1)
                act.wait_ge(sem["z_psum"], 1)
                nc.scalar.activation(absz, st.ps[0:STATE, 7, :], ACT.Abs).then_inc(sem["soft"], 1)
                act.wait_ge(sem["soft"], 1)
                nc.scalar.activation(expz, absz, ACT.Exp, scale=-1.0).then_inc(sem["soft"], 1)
                act.wait_ge(sem["soft"], 2)
                nc.scalar.activation(logz, expz, ACT.Ln, bias=st.one[0:STATE, 0:1]).then_inc(sem["soft"], 1)
                for s in range(STATE):
                    act.wait_ge(sem["spread_psum"], s + 1)
                    if s >= 2:
                        act.wait_ge(sem["product"], KC * (s - 1))
                    nc.scalar.activation(dbc[:, s % 2, :], st.ps[:, 5 + s % 2, :], ACT.Copy
                                         ).then_inc(sem["spread_copied"], 1)
                norm_scale(nc, st, sem, act)

            @block.gpsimd
            def _(pool):
                for s in range(STATE):
                    pool.wait_ge(sem["spread_copied"], s + 1)
                    for c in range(KC):
                        i = s * KC + c
                        if i >= RING:
                            pool.wait_ge(sem["scanned"], i - RING + 1)
                        nc.gpsimd.tensor_tensor(u[:, i % RING, :], xpT[:, c, :], dbc[:, s % 2, :], ALU.mult
                                                ).then_inc(sem["product"], 1)

            @block.vector
            def _(dve):
                dve.wait_ge(sem["soft"], 3)
                nc.vector.scalar_tensor_tensor(delta[:, :], st.ps[0:STATE, 7, :], 0.0, logz,
                                               ALU.max, ALU.add).then_inc(sem["delta_ready"], 1)
                for s in range(STATE):
                    for c in range(KC):
                        i = s * KC + c
                        dve.wait_ge(sem["product"], i + 1)
                        if i >= RING:
                            dve.wait_ge(sem["summed"], i - RING + 1)
                        nc.vector.tensor_tensor_scan(
                            h[:, i % RING, :], st.decay[:, c, s:s + 1].to_broadcast([P, S]),
                            u[:, i % RING, :], 0.0, ALU.mult, ALU.add).then_inc(sem["scanned"], 1)
                dve.wait_ge(sem["summed"], STATE * KC)
                nc.vector.tensor_copy(sums[:, :], st.ps[:, 4, :]).then_inc(sem["sums_ready"], 1)
                for c in range(KC):
                    dve.wait_ge(sem["y_psum"], c + 1)
                    nc.vector.scalar_tensor_tensor(yT[:, c, :], xpT[:, c, :], st.d_param[:, c:c + 1],
                                                   st.ps[:, c, :], ALU.mult, ALU.add).then_inc(sem["y_ready"], 1)
                dve.wait_ge(sem["x_loaded"], 16)
                for j in range(NT):
                    dve.wait_ge(sem["out_psum"], j + 1)
                    nc.vector.scalar_tensor_tensor(st.r[:, j, :], st.x[:, j, :], 2.0, st.ps[:, j, :],
                                                   ALU.mult, ALU.add).then_inc(sem["row_ready"], 1)
                residual_norm(nc, st, sem, dve)
        run_pass(nc, body)


def similarity_pass(nc, st, sem):
    with ExitStack() as ctx:
        sb = lambda name, shape, dt=F32: ctx.enter_context(nc.sbuf_tensor(name, shape, dt))
        kv = sb("kv", [P, NT, CTX])
        kvT = sb("kvT", [P, S])
        mixT = sb("mixT", [P, S])
        simil = sb("simil", [P, NT, S])
        simil_n = sb("simil_n", [P, NT, S])
        simil_g = sb("simil_g", [P, NT, S])
        nmax = sb("nmax", [P, NT])
        esum = sb("esum", [P, NT])
        rsum = sb("rsum", [P, NT])
        s_stats = sb("s_stats", [P, NT, 6])
        s_mv = sb("s_mv", [P, NT, 2])
        s_ln = sb("s_ln", [P, NT])
        s_rstd = sb("s_rstd", [P, NT])
        SCALE = float(E) ** -0.5

        def body(block):
            @block.tensor
            def _(pe):
                nc.tensor.matmul(st.ps[:, 1, :], st.w_k[:, :], st.ctxT[:, :], start=True, stop=True
                                 ).then_inc(sem["kvT_psum"], 1)
                for j in range(NT):
                    out = st.ps[:, 0, j * P:(j + 1) * P]
                    nc.tensor.matmul(out, st.ctxT[:, j * P:(j + 1) * P], st.w_k[:, :], start=True, stop=False)
                    last = nc.tensor.matmul(out, st.ones[96:97, 0:P], st.bias_rows[96:97, 0:CTX],
                                            start=False, stop=True, tile_position=(96, 0))
                last.then_inc(sem["kv_psum"], 1)
                pe.wait_ge(sem["kv_ready"], 1)
                for j in range(NT):
                    last = nc.tensor.matmul(st.ps[:, 2, :], kv[:, j, :], st.xT[:, j, :],
                                            start=(j == 0), stop=(j == NT - 1))
                last.then_inc(sem["mix_psum"], 1)
                pe.wait_ge(sem["kvT_ready"], 1)
                pe.wait_ge(sem["mix_ready"], 1)
                for j in range(NT):
                    nc.tensor.matmul(st.ps[:, 4 + j, :], mixT[:, j * P:(j + 1) * P], kvT[:, :],
                                     start=True, stop=True).then_inc(sem["sim_psum"], 1)
                transpose_rows(nc, st, sem, pe)

            @block.scalar
            def _(act):
                act.wait_ge(sem["kvT_psum"], 1)
                nc.scalar.activation(kvT[:, :], st.ps[:, 1, :], ACT.Identity, bias=st.b_k[:, 0:1]
                                     ).then_inc(sem["kvT_ready"], 1)
                act.wait_ge(sem["kv_psum"], 1)
                nc.scalar.activation(kv[:, :, :], st.ps[:, 0, :].rearrange("p (j c) -> p j c", j=NT), ACT.Copy
                                     ).then_inc(sem["kv_ready"], 1)
                for j in range(NT):
                    act.wait_ge(sem["sim_psum"], j + 1)
                    nc.scalar.activation(simil[:, j, :], st.ps[:, 4 + j, :], ACT.Copy, scale=SCALE
                                         ).then_inc(sem["sim_ready"], 1)
                act.wait_ge(sem["sim_var"], NT)
                nc.scalar.activation(s_ln[:, :], s_mv[:, :, 1], ACT.Ln, bias=st.eps[:, 1:2]).then_inc(sem["sim_rstd"], 1)
                act.wait_ge(sem["sim_rstd"], 1)
                nc.scalar.activation(s_rstd[:, :], s_ln[:, :], ACT.Exp, scale=-0.5).then_inc(sem["sim_rstd"], 1)
                for j in range(NT):
                    act.wait_ge(sem["sim_max"], j + 1)
                    nc.scalar.activation(simil[:, j, :], simil_g[:, j, :], ACT.Exp, bias=nmax[:, j:j + 1],
                                         accum_out=esum[:, j:j + 1]).then_inc(sem["sim_exp"], 1)
                norm_scale(nc, st, sem, act)

            @block.gpsimd
            def _(pool):
                for j in range(NT):
                    pool.wait_ge(sem["sim_normed"], j + 1)
                    nc.gpsimd.tensor_tensor(simil_n[:, j, :], simil_n[:, j, :], st.gamma[:, :], ALU.mult
                                            ).then_inc(sem["sim_gamma"], 1)
                    pool.wait_ge(sem["sim_gamma"], j + 1)
                    nc.gpsimd.tensor_tensor(simil_g[:, j, :], simil_n[:, j, :], st.beta[:, :], ALU.add
                                            ).then_inc(sem["sim_affine"], 1)

            @block.vector
            def _(dve):
                dve.wait_ge(sem["mix_psum"], 1)
                nc.vector.tensor_copy(mixT[:, :], st.ps[:, 2, :]).then_inc(sem["mix_ready"], 1)
                for j in range(NT):
                    dve.wait_ge(sem["sim_ready"], j + 1)
                    nc.vector.bn_stats(s_stats[:, j, :], simil[:, j, :]).then_inc(sem["sim_stats"], 1)
                for j in range(NT):
                    dve.wait_ge(sem["sim_stats"], j + 1)
                    nc.vector.bn_aggr(s_mv[:, j, :], s_stats[:, j, :]).then_inc(sem["sim_var"], 1)
                dve.wait_ge(sem["sim_rstd"], 2)
                for j in range(NT):
                    nc.vector.tensor_scalar(simil_n[:, j, :], simil[:, j, :], s_mv[:, j, 0:1], s_rstd[:, j:j + 1],
                                            ALU.subtract, ALU.mult).then_inc(sem["sim_normed"], 1)
                for j in range(NT):
                    dve.wait_ge(sem["sim_affine"], j + 1)
                    nc.vector.tensor_reduce(nmax[:, j:j + 1], simil_g[:, j, :], AX_X, ALU.max, negate=True
                                            ).then_inc(sem["sim_max"], 1)
                for j in range(NT):
                    dve.wait_ge(sem["sim_exp"], j + 1)
                    nc.vector.reciprocal(rsum[:, j:j + 1], esum[:, j:j + 1]).then_inc(sem["sim_recip"], 1)
                    dve.wait_ge(sem["sim_recip"], j + 1)
                    nc.vector.scalar_tensor_tensor(st.r[:, j, :], simil[:, j, :], rsum[:, j:j + 1], st.x[:, j, :],
                                                   ALU.mult, ALU.add).then_inc(sem["row_ready"], 1)
                residual_norm(nc, st, sem, dve)
        run_pass(nc, body)


def two_expert_pass(nc, st, sem):
    with ExitStack() as ctx:
        sb = lambda name, shape, dt=F32: ctx.enter_context(nc.sbuf_tensor(name, shape, dt))
        h0T = sb("h0T", [P, NF, S])
        h1T = sb("h1T", [P, NF, S])
        scores = sb("scores", [P, 2 * NT])
        first = sb("first", [P, NT])
        second = sb("second", [P, NT])

        def body(block):
            @block.tensor
            def _(pe):
                for j in range(NT):
                    for k in range(KC):
                        last = nc.tensor.matmul(st.ps[:, 7, 2 * j:2 * j + 2], st.xT[:, k, j * P:(j + 1) * P],
                                                st.w_g[:, k, :], start=(k == 0), stop=(k == KC - 1))
                last.then_inc(sem["score_psum"], 1)
                for f in range(NF):
                    for n, (w, used) in enumerate(((st.w_0a, sem["h0_ready"]), (st.w_1a, sem["h1_ready"]))):
                        bank = 2 * (f % 2) + n
                        if f >= 2:
                            pe.wait_ge(used, f - 1)
                        for k in range(KC):
                            last = nc.tensor.matmul(st.ps[:, bank, :], w[:, k, f * P:(f + 1) * P], st.xT[:, k, :],
                                                    start=(k == 0), stop=(k == KC - 1))
                        last.then_inc((sem["h0_psum"], sem["h1_psum"])[n], 1)
                pe.wait_ge(sem["h0_ready"], NF)
                pe.wait_ge(sem["score_ready"], 1)
                for j in range(NT):
                    if j >= 2:
                        pe.wait_ge(sem["row_ready"], j - 1)
                    project_rows(nc, st, pe, st.ps[:, 4 + j % 2, :], h0T, j, st.w_0b, NF, bias=32
                                 ).then_inc(sem["out_psum"], 1)
                    pe.wait_ge(sem["h1_ready"], NF)
                    project_rows(nc, st, pe, st.ps[:, 6 + j % 2, :], h1T, j, st.w_1b, NF, bias=64
                                 ).then_inc(sem["out_psum"], 1)
                transpose_rows(nc, st, sem, pe)

            @block.scalar
            def _(act):
                for f in range(NF):
                    act.wait_ge(sem["h0_psum"], f + 1)
                    nc.scalar.activation(h0T[:, f, :], st.ps[:, 2 * (f % 2), :], ACT.Gelu,
                                         bias=st.b_0a[:, f:f + 1]).then_inc(sem["h0_ready"], 1)
                norm_scale(nc, st, sem, act)

            @block.vector
            def _(dve):
                dve.wait_ge(sem["score_psum"], 1)
                nc.vector.tensor_copy(scores[:, :], st.ps[:, 7, 0:2 * NT]).then_inc(sem["score_ready"], 1)
                dve.wait_ge(sem["score_ready"], 1)
                pair = scores[:, :].rearrange("p (j e) -> p j e", e=2)
                nc.vector.tensor_tensor(first[:, :], pair[:, :, 0], pair[:, :, 1], ALU.is_ge).then_inc(sem["choice"], 1)
                dve.wait_ge(sem["choice"], 1)
                nc.vector.tensor_scalar(second[:, :], first[:, :], -1.0, 1.0, ALU.mult, ALU.add
                                        ).then_inc(sem["choice"], 1)
                for f in range(NF):
                    dve.wait_ge(sem["h1_psum"], f + 1)
                    nc.vector.tensor_scalar(h1T[:, f, :], st.ps[:, 2 * (f % 2) + 1, :], st.b_1a[:, f:f + 1], 0.0,
                                            ALU.add, ALU.max).then_inc(sem["h1_ready"], 1)
                dve.wait_ge(sem["choice"], 2)
                for j in range(NT):
                    dve.wait_ge(sem["out_psum"], 2 * j + 1)
                    nc.vector.scalar_tensor_tensor(st.r[:, j, :], st.ps[:, 4 + j % 2, :], first[:, j:j + 1],
                                                   st.x[:, j, :], ALU.mult, ALU.add).then_inc(sem["half_row"], 1)
                    dve.wait_ge(sem["half_row"], j + 1)
                    dve.wait_ge(sem["out_psum"], 2 * j + 2)
                    nc.vector.scalar_tensor_tensor(st.r[:, j, :], st.ps[:, 6 + j % 2, :], second[:, j:j + 1],
                                                   st.r[:, j, :], ALU.mult, ALU.add).then_inc(sem["row_ready"], 1)
                residual_norm(nc, st, sem, dve)
        run_pass(nc, body)


def by_head(ap, heads):
    return ap.rearrange("p (h d) -> p h d", h=heads)


def polynomial_pass(nc, st, sem):
    QK = 2 * E
    NH2 = 2 * HEADS
    HALF = HD // 2
    with ExitStack() as ctx:
        sb = lambda name, shape, dt=F32: ctx.enter_context(nc.sbuf_tensor(name, shape, dt))
        v = sb("v", [P, NT, E])
        qT = sb("qT", [P, KC, S])
        kT = sb("kT", [P, KC, S])
        other = sb("other", [P, QK])
        hsum = sb("hsum", [P, NH2])
        hmean = sb("hmean", [P, NH2])
        hvar = sb("hvar", [P, NH2])
        hln = sb("hln", [P, NH2])
        hrstd = sb("hrstd", [P, NH2])
        sq = sb("sq", [P, 2, 2 * S])
        rot, turned = sq[:, 0, :], sq[:, 1, :]
        rden = sb("rden", [P, S])
        oT = qT

        def body(block):
            @block.tensor
            def _(pe):
                for j in range(NT):
                    if j >= 1:
                        pe.wait_ge(sem["qk_rotated"], 3 * j)
                        pe.wait_ge(sem["v_ready"], j)
                    for n in range(3):
                        for k in range(KC):
                            last = nc.tensor.matmul(st.ps[:, n, :], st.xT[:, k, j * P:(j + 1) * P],
                                                    st.w_qkv[:, k, n * E:(n + 1) * E],
                                                    start=(k == 0), stop=(k == KC - 1))
                    last.then_inc(sem["qkv_psum"], 1)
                    pe.wait_ge(sem["qk_normed"], j + 1)
                    if j >= 1:
                        pe.wait_ge(sem["qkT_ready"], 2 * j)
                    for n in range(2):
                        for k in range(KC):
                            at = n * E + k * P
                            last = nc.tensor.transpose(st.ps[:, 6 + n, k * P:(k + 1) * P], other[:, at:at + P],
                                                       st.ident[:, :])
                        last.then_inc(sem["qkT_psum"], 1)
                pe.wait_ge(sem["qkT_ready"], 2 * NT)
                pe.wait_ge(sem["v_ready"], NT)

                def weigh(n):
                    g, pair, i = n // 8, n // 4 % 2, n % 4
                    w = S - i * P
                    pe.wait_ge(sem["weighed"], n + 1)
                    for q in range(2):
                        hh = 2 * pair + q
                        part = slice(hh * HD, (hh + 1) * HD)
                        a = sq[:, n % 2, q * S:q * S + w]
                        head = g * HG + hh
                        nc.tensor.matmul(st.ps[part, 4 + 2 * (g % 2), i * P:S], v[:, i, head * HD:(head + 1) * HD], a,
                                         start=(i == 0), stop=(i == NT - 1), tile_position=(0, hh * HD))
                        last = nc.tensor.matmul(st.ps[part, 5 + 2 * (g % 2), i * P:S], st.ones[:, 0:HD], a,
                                                start=(i == 0), stop=(i == NT - 1), tile_position=(0, hh * HD))
                    last.then_inc(sem["pv_done"], 1)

                for n in range(8 * KC):
                    g, pair, i = n // 8, n // 4 % 2, n % 4
                    if n >= 2:
                        pe.wait_ge(sem["squared"], n - 1)
                    for q in range(2):
                        part = slice((2 * pair + q) * HD, (2 * pair + q + 1) * HD)
                        last = nc.tensor.matmul(st.ps[:, 2 * (n % 2) + q, 0:S - i * P], kT[part, g, i * P:(i + 1) * P],
                                                qT[part, g, i * P:S], start=True, stop=True,
                                                tile_position=((2 * pair + q) * HD, 0))
                    last.then_inc(sem["qk_psum"], 1)
                    if n >= 1:
                        if n - 1 >= 16 and (n - 1) % 8 == 0:
                            pe.wait_ge(sem["o_ready"], (n - 1) // 8 - 1)
                        weigh(n - 1)
                weigh(8 * KC - 1)
                pe.wait_ge(sem["o_ready"], KC)
                for j in range(NT):
                    project_rows(nc, st, pe, st.ps[:, j, :], oT, j, st.w_oatt, KC).then_inc(sem["out_psum"], 1)
                transpose_rows(nc, st, sem, pe)

            @block.scalar
            def _(act):
                for j in range(NT):
                    act.wait_ge(sem["qkv_psum"], j + 1)
                    nc.scalar.activation(v[:, j, :], st.ps[:, 2, :], ACT.Copy).then_inc(sem["v_ready"], 1)
                    act.wait_ge(sem["qk_centred"], j + 1)
                    nc.scalar.activation(turned[:, :], other[:, :], ACT.Square).then_inc(sem["qk_square"], 1)
                    act.wait_ge(sem["qk_var"], j + 1)
                    nc.scalar.activation(hln[:, :], hvar[:, :], ACT.Ln, scale=1.0 / HD, bias=st.eps[:, 0:1]
                                         ).then_inc(sem["qk_rstd"], 1)
                    act.wait_ge(sem["qk_rstd"], 2 * j + 1)
                    nc.scalar.activation(hrstd[:, :], hln[:, :], ACT.Exp, scale=-0.5).then_inc(sem["qk_rstd"], 1)
                    for n, dst in enumerate((qT, kT)):
                        act.wait_ge(sem["qkT_psum"], 2 * j + n + 1)
                        nc.scalar.activation(dst[:, :, j * P:(j + 1) * P],
                                             st.ps[:, 6 + n, :].rearrange("p (k t) -> p k t", k=KC), ACT.Identity,
                                             bias=st.head_ln[:, 1:2], scale=st.head_ln[:, 0:1]
                                             ).then_inc(sem["qkT_ready"], 1)
                for n in range(8 * KC):
                    w = S - n % 4 * P
                    act.wait_ge(sem["qk_psum"], n + 1)
                    if n >= 2:
                        act.wait_ge(sem["pv_done"], n - 1)
                    dst = sq[:, n % 2, :].rearrange("p (q t) -> p q t", q=2)
                    b0 = 2 * (n % 2)
                    nc.scalar.activation(dst[:, :, 0:w], st.ps[:, b0:b0 + 2, 0:w], ACT.Square).then_inc(sem["squared"], 1)
                norm_scale(nc, st, sem, act)

            @block.gpsimd
            def _(pool):
                for j in range(NT):
                    pool.wait_ge(sem["qk_rotated"], 3 * j + 3)
                    nc.gpsimd.tensor_tensor(rot[:, :], turned[:, :], other[:, :], ALU.add).then_inc(sem["qk_rope"], 1)
                    pool.wait_ge(sem["qk_mean"], j + 1)
                    nc.gpsimd.tensor_tensor(by_head(other[:, :], NH2), by_head(rot[:, :], NH2),
                                            hmean[:, :].unsqueeze(2).to_broadcast([P, NH2, HD]), ALU.add
                                            ).then_inc(sem["qk_centred"], 1)
                for n in range(8 * KC):
                    pool.wait_ge(sem["squared"], n + 1)
                    diag = sq[:, n % 2, :].rearrange("p (q t) -> p q t", q=2)[:, :, 0:P]
                    nc.gpsimd.affine_select(out=diag, in_=diag, compare_op=ALU.is_ge, fill=0.0, base=0,
                                            pattern=[[0, 2], [1, P]], channel_multiplier=-1).then_inc(sem["masked"], 1)

            def attended(dve, g):
                dve.wait_ge(sem["pv_done"], 8 * g + 8)
                nc.vector.reciprocal(rden[:, :], st.ps[:, 5 + 2 * (g % 2), :]).then_inc(sem["den_ready"], 1)
                dve.wait_ge(sem["den_ready"], g + 1)
                nc.vector.tensor_tensor(oT[:, g, :], st.ps[:, 4 + 2 * (g % 2), :], rden[:, :], ALU.mult
                                        ).then_inc(sem["o_ready"], 1)

            @block.vector
            def _(dve):
                for j in range(NT):
                    dve.wait_ge(sem["qkv_psum"], j + 1)
                    if j >= 1:
                        dve.wait_ge(sem["qkT_psum"], 2 * j)
                        dve.wait_ge(sem["qk_var"], j)
                    qk = st.ps[:, 0:2, :].rearrange("p n (h d) -> p (n h) d", h=HEADS)
                    cos = st.cos[:, j, :].unsqueeze(1).to_broadcast([P, NH2, HD])
                    sin = st.sin[:, j, :].unsqueeze(1).to_broadcast([P, NH2, HALF])
                    msin = st.msin[:, j, :].unsqueeze(1).to_broadcast([P, NH2, HALF])
                    nc.vector.tensor_tensor(by_head(turned[:, :], NH2), qk, cos, ALU.mult).then_inc(sem["qk_rotated"], 1)
                    nc.vector.tensor_tensor(by_head(other[:, :], NH2)[:, :, 0:HALF], qk[:, :, HALF:HD], msin, ALU.mult
                                            ).then_inc(sem["qk_rotated"], 1)
                    nc.vector.tensor_tensor(by_head(other[:, :], NH2)[:, :, HALF:HD], qk[:, :, 0:HALF], sin, ALU.mult
                                            ).then_inc(sem["qk_rotated"], 1)
                    dve.wait_ge(sem["qk_rope"], j + 1)
                    nc.vector.tensor_reduce(hsum[:, :], by_head(rot[:, :], NH2), AX_X, ALU.add
                                            ).then_inc(sem["qk_sum"], 1)
                    dve.wait_ge(sem["qk_sum"], j + 1)
                    nc.vector.tensor_scalar(hmean[:, :], hsum[:, :], -1.0 / HD, None, ALU.mult).then_inc(sem["qk_mean"], 1)
                    dve.wait_ge(sem["qk_square"], j + 1)
                    nc.vector.tensor_reduce(hvar[:, :], by_head(turned[:, :], NH2), AX_X, ALU.add
                                            ).then_inc(sem["qk_var"], 1)
                    dve.wait_ge(sem["qk_rstd"], 2 * j + 2)
                    nc.vector.tensor_tensor(by_head(other[:, :], NH2), by_head(other[:, :], NH2),
                                            hrstd[:, :].unsqueeze(2).to_broadcast([P, NH2, HD]), ALU.mult
                                            ).then_inc(sem["qk_normed"], 1)
                for n in range(8 * KC):
                    w = S - n % 4 * P
                    dve.wait_ge(sem["masked"], n + 1)
                    part = sq[:, n % 2, :].rearrange("p (q t) -> p q t", q=2)[:, :, 0:w]
                    nc.vector.tensor_tensor(part, part, part, ALU.mult).then_inc(sem["weighed"], 1)
                    if n % 8 == 0 and n >= 8:
                        attended(dve, n // 8 - 1)
                attended(dve, KC - 1)
                for j in range(NT):
                    dve.wait_ge(sem["out_psum"], j + 1)
                    nc.vector.tensor_tensor(st.r[:, j, :], st.x[:, j, :], st.ps[:, j, :], ALU.add
                                            ).then_inc(sem["row_ready"], 1)
                residual_norm(nc, st, sem, dve)
        run_pass(nc, body)


def softmax_pass(nc, st, sem, T, b):
    HALF = HD // 2
    KVH = CTX // HD
    SCALE = float(HD) ** -0.5
    with ExitStack() as ctx:
        sb = lambda name, shape, dt=F32: ctx.enter_context(nc.sbuf_tensor(name, shape, dt))
        kT = sb("kT2", [P, KVH, S])
        qT = sb("qT2", [P, KC, S])
        ssum = sb("ssum", [P, 2 * NT])
        sln = sb("sln", [P, 2 * NT])
        srstd = sb("srstd", [P, 2 * NT])
        pr = sb("pr", [P, 3, S])
        pT = sb("pT", [P, 2, NT, S])
        kn, kt1, kt2 = (pT[:, 0, 0, n * CTX:(n + 1) * CTX] for n in range(3))
        krep = pT[:, 0, 1, :].rearrange("p (g r d) -> p g r d", g=KVH, r=HG)
        qn, t1, t2, qr = (pT[:, 1, n, :] for n in range(4))
        nmx = sb("nmx", [P, 4])
        nbias = sb("nbias", [P, 4])
        rden = sb("rden2", [P, S])
        oT = qT
        NSTEP = HEADS * NT

        def body(block):
            @block.tensor
            def _(pe):
                for j in range(NT):
                    pe.wait_ge(sem["krep_ready"], j + 1)
                    if j >= 1:
                        pe.wait_ge(sem["qkT_ready"], 2 * j)
                    for g in range(KVH):
                        last = nc.tensor.transpose(st.ps[:, 6, g * P:(g + 1) * P],
                                                   krep[:, g, :, :].rearrange("p r d -> p (r d)"), st.ident[:, :])
                    last.then_inc(sem["qkT_psum"], 1)
                    pe.wait_ge(sem["q_rope"], j + 1)
                    for k in range(KC):
                        last = nc.tensor.transpose(st.ps[:, 7, k * P:(k + 1) * P], qr[:, k * P:(k + 1) * P],
                                                   st.ident[:, :])
                    last.then_inc(sem["qkT_psum"], 1)
                pe.wait_ge(sem["qkT_ready"], 2 * NT)

                def score(n):
                    head, j = n // NT, n % NT
                    g, hh = head // HG, head % HG
                    part = slice(hh * HD, (hh + 1) * HD)
                    w = (j + 1) * P
                    if n >= 2:
                        pe.wait_ge(sem["exped"], n - 1)
                    nc.tensor.matmul(st.ps[:, n % 2, 0:w], qT[part, g, j * P:(j + 1) * P], kT[part, g, 0:w],
                                     start=True, stop=False, tile_position=(hh * HD, 0))
                    nc.tensor.matmul(st.ps[:, n % 2, j * P:w], st.ident_b[:, :], st.causal_b[:, :],
                                     start=False, stop=True).then_inc(sem["qk_psum"], 1)

                def turn(n):
                    j = n % NT
                    pe.wait_ge(sem["exped"], n + 1)
                    if n >= 2:
                        pe.wait_ge(sem["pT_ready"], n - 1)
                    for i in range(j + 1):
                        last = nc.tensor.transpose(st.ps[:, 2 + n % 2, i * P:(i + 1) * P],
                                                   pr[:, n % 3, i * P:(i + 1) * P], st.ident[:, :])
                    last.then_inc(sem["pT_psum"], 1)

                def weigh(head):
                    g, hh = head // HG, head % HG
                    part = slice(hh * HD, (hh + 1) * HD)
                    pe.wait_ge(sem["pT_ready"], NT * (head + 1))
                    if hh == 0 and g >= 2:
                        pe.wait_ge(sem["o_ready"], g - 1)
                    for i in range(NT):
                        a = pT[:, head % 2, i, i * P:S]
                        nc.tensor.matmul(st.ps[part, 4 + 2 * (g % 2), i * P:S], st.ctx[:, i, g * HD:(g + 1) * HD], a,
                                         start=(i == 0), stop=(i == NT - 1), tile_position=(0, hh * HD))
                        last = nc.tensor.matmul(st.ps[part, 5 + 2 * (g % 2), i * P:S], st.ones[:, 0:HD], a,
                                                start=(i == 0), stop=(i == NT - 1), tile_position=(0, hh * HD))
                    last.then_inc(sem["pv_done"], 1)

                score(0)
                for n in range(NSTEP):
                    if n + 1 < NSTEP:
                        score(n + 1)
                    turn(n)
                    if n % NT == 1 and n > NT:
                        weigh(n // NT - 1)
                weigh(HEADS - 1)
                pe.wait_ge(sem["o_ready"], KC)
                for j in range(NT):
                    project_rows(nc, st, pe, st.ps[:, j, :], oT, j, st.w_oxatt, KC).then_inc(sem["out_psum"], 1)
                transpose_rows(nc, st, sem, pe)

            @block.scalar
            def _(act):
                for j in range(NT):
                    nc.scalar.activation(pr[:, 0, 0:CTX], st.ctx[:, j, :], ACT.Square, scale=float(CTX) ** -0.5,
                                         accum_out=ssum[:, 2 * j:2 * j + 1]).then_inc(sem["rms_sum"], 1)
                    act.wait_ge(sem["rms_sum"], 2 * j + 1)
                    nc.scalar.activation(pr[:, 1, :], st.x[:, j, :], ACT.Square, scale=float(E) ** -0.5,
                                         accum_out=ssum[:, 2 * j + 1:2 * j + 2]).then_inc(sem["rms_sum"], 1)
                    act.wait_ge(sem["rms_sum"], 2 * j + 2)
                nc.scalar.activation(sln[:, :], ssum[:, :], ACT.Ln, bias=st.eps[:, 0:1]).then_inc(sem["rms_rstd"], 1)
                act.wait_ge(sem["rms_rstd"], 1)
                nc.scalar.activation(srstd[:, :], sln[:, :], ACT.Exp, scale=-0.5).then_inc(sem["rms_rstd"], 1)
                for j in range(NT):
                    for n, dst in enumerate((kT, qT)):
                        act.wait_ge(sem["qkT_psum"], 2 * j + n + 1)
                        nc.scalar.activation(dst[:, :, j * P:(j + 1) * P],
                                             st.ps[:, 6 + n, :].rearrange("p (k t) -> p k t", k=KC), ACT.Copy
                                             ).then_inc(sem["qkT_ready"], 1)
                for n in range(NSTEP):
                    w = (n % NT + 1) * P
                    act.wait_ge(sem["bias_ready"], n + 1)
                    if n >= 3:
                        act.wait_ge(sem["pT_psum"], n - 2)
                    nc.scalar.activation(pr[:, n % 3, 0:w], st.ps[:, n % 2, 0:w], ACT.Exp, scale=SCALE,
                                         bias=nbias[:, n % 4:n % 4 + 1]).then_inc(sem["exped"], 1)
                norm_scale(nc, st, sem, act)

            @block.gpsimd
            def _(pool):
                for j in range(NT):
                    pool.wait_ge(sem["k_turned"], 3 * j + 3)
                    nc.gpsimd.tensor_tensor(kn[:, :], kt1[:, :], kt2[:, :], ALU.add).then_inc(sem["k_rope"], 1)
                    pool.wait_ge(sem["k_rope"], j + 1)
                    if j >= 1:
                        pool.wait_ge(sem["qkT_psum"], 2 * j - 1)
                    nc.gpsimd.tensor_copy(krep[:, :, :, :],
                                          by_head(kn[:, :], KVH).unsqueeze(2).to_broadcast([P, KVH, HG, HD])
                                          ).then_inc(sem["krep_ready"], 1)
                    pool.wait_ge(sem["q_turned"], 3 * j + 3)
                    if j >= 1:
                        pool.wait_ge(sem["qkT_psum"], 2 * j)
                    nc.gpsimd.tensor_tensor(qr[:, :], t1[:, :], t2[:, :], ALU.add).then_inc(sem["q_rope"], 1)

            @block.vector
            def _(dve):
                dve.wait_ge(sem["rms_rstd"], 2)

                def rope(src, a, c, heads, sems, j):
                    cos = st.cos[:, j, :].unsqueeze(1).to_broadcast([P, heads, HD])
                    sin = st.sin[:, j, :].unsqueeze(1).to_broadcast([P, heads, HALF])
                    msin = st.msin[:, j, :].unsqueeze(1).to_broadcast([P, heads, HALF])
                    x, y, z = by_head(src[:, :], heads), by_head(a[:, :], heads), by_head(c[:, :], heads)
                    nc.vector.tensor_tensor(y, x, cos, ALU.mult).then_inc(sems, 1)
                    nc.vector.tensor_tensor(z[:, :, 0:HALF], x[:, :, HALF:HD], msin, ALU.mult).then_inc(sems, 1)
                    nc.vector.tensor_tensor(z[:, :, HALF:HD], x[:, :, 0:HALF], sin, ALU.mult).then_inc(sems, 1)

                for j in range(NT):
                    if j >= 1:
                        dve.wait_ge(sem["krep_ready"], j)
                        dve.wait_ge(sem["q_rope"], j)
                    nc.vector.scalar_tensor_tensor(kn[:, :], st.ctx[:, j, :], srstd[:, 2 * j:2 * j + 1], st.k_norm[:, :],
                                                   ALU.mult, ALU.mult).then_inc(sem["rms_done"], 1)
                    dve.wait_ge(sem["rms_done"], 2 * j + 1)
                    rope(kn, kt1, kt2, KVH, sem["k_turned"], j)
                    nc.vector.scalar_tensor_tensor(qn[:, :], st.x[:, j, :], srstd[:, 2 * j + 1:2 * j + 2],
                                                   st.q_norm[:, :], ALU.mult, ALU.mult).then_inc(sem["rms_done"], 1)
                    dve.wait_ge(sem["rms_done"], 2 * j + 2)
                    rope(qn, t1, t2, HEADS, sem["q_turned"], j)

                def row_max(n):
                    w = (n % NT + 1) * P
                    dve.wait_ge(sem["qk_psum"], n + 1)
                    if n >= 4:
                        dve.wait_ge(sem["exped"], n - 3)
                    nc.vector.tensor_reduce(nmx[:, n % 4:n % 4 + 1], st.ps[:, n % 2, 0:w], AX_X, ALU.max, negate=True
                                            ).then_inc(sem["max_ready"], 1)
                    dve.wait_ge(sem["max_ready"], n + 1)
                    nc.vector.tensor_scalar(nbias[:, n % 4:n % 4 + 1], nmx[:, n % 4:n % 4 + 1], SCALE, None, ALU.mult
                                            ).then_inc(sem["bias_ready"], 1)

                def keep(n):
                    head, j = n // NT, n % NT
                    dve.wait_ge(sem["pT_psum"], n + 1)
                    if head >= 2 and j == 0:
                        dve.wait_ge(sem["pv_done"], head - 1)
                    nc.vector.tensor_copy(pT[:, head % 2, 0:j + 1, j * P:(j + 1) * P],
                                          st.ps[:, 2 + n % 2, 0:(j + 1) * P].rearrange("p (i t) -> p i t", t=P)
                                          ).then_inc(sem["pT_ready"], 1)

                def attended(g):
                    dve.wait_ge(sem["pv_done"], HG * (g + 1))
                    nc.vector.reciprocal(rden[:, :], st.ps[:, 5 + 2 * (g % 2), :]).then_inc(sem["den_ready"], 1)
                    dve.wait_ge(sem["den_ready"], g + 1)
                    dve.wait_ge(sem["exped"], NT * HG * (g + 1))
                    nc.vector.tensor_tensor(oT[:, g, :], st.ps[:, 4 + 2 * (g % 2), :], rden[:, :], ALU.mult
                                            ).then_inc(sem["o_ready"], 1)

                row_max(0)
                for n in range(NSTEP):
                    if n + 1 < NSTEP:
                        row_max(n + 1)
                    keep(n)
                    if n % (NT * HG) == 3 and n > NT * HG:
                        attended(n // (NT * HG) - 1)
                attended(KC - 1)
                for j in range(NT):
                    dve.wait_ge(sem["out_psum"], j + 1)
                    nc.vector.tensor_tensor(st.r[:, j, :], st.x[:, j, :], st.ps[:, j, :], ALU.add
                                            ).then_inc(sem["row_ready"], 1)
                residual_norm(nc, st, sem, dve)

            @block.sync
            def _(sp):
                sp.wait_ge(sem["x_ready"], NT)
                sp.dma_start(T["x5"][bass.ds(b, 1), :, :].rearrange("a (j p) d -> p (a j) d", p=P), st.x[:, :, :]
                             ).then_inc(sem["stored"], 16)
                sp.wait_ge(sem["xt_ready"], NT)
                sp.dma_start(T["x5T"][bass.ds(b, 1), :, :].rearrange("a (k p) t -> p (a k) t", p=P), st.xT[:, :, :]
                             ).then_inc(sem["stored"], 16)
                sp.wait_ge(sem["stored"], 32)
        run_pass(nc, body)


def signals(nc, ctx, names):
    sem = {n: ctx.enter_context(nc.semaphore(n)) for n in names}
    nums = [h.num for h in sem.values()]
    assert nums == list(range(nums[0], nums[0] + len(nums)))
    sem["all"] = range(nums[0], nums[-1] + 1)
    return sem


LAYER_SIGNALS = """xT_loaded pick_loaded x_loaded ctx_loaded row_ready stats_ready var_ready rstd_ready x_ready xt_psum xt_ready
xp_psum xp_ready z_psum soft delta_ready spread_psum spread_copied product scanned summed sums_ready y_psum y_ready
out_psum kvT_psum kvT_ready kv_psum kv_ready mix_psum mix_ready sim_psum sim_ready sim_stats sim_var sim_rstd
sim_normed sim_gamma sim_affine sim_max sim_exp sim_recip score_psum score_ready choice h0_psum h0_ready h1_psum
h1_ready half_row qkv_psum v_ready qk_rotated qk_rope qk_sum qk_mean qk_centred qk_square qk_var qk_rstd qk_normed
qkT_psum qkT_ready qk_psum squared masked weighed pv_done den_ready o_ready rms_sum rms_rstd rms_done k_turned
k_rope krep_ready q_turned q_rope max_ready bias_ready exped pT_psum pT_ready stored""".split()


def clear(nc, sem, block):
    @block.sync
    def _(sp):
        sp.sem_clear(sem["all"])


def layers(nc, T, upto=5):
    with ExitStack() as ctx:
        sb = lambda name, shape, dt=F32: ctx.enter_context(nc.sbuf_tensor(name, shape, dt))
        st = Held()
        sem = signals(nc, ctx, LAYER_SIGNALS + ["weights_loaded", "made"])
        sem["all"] = range(sem["all"][0], sem["all"][-1] - 1)
        st.ps = ctx.enter_context(nc.psum_tensor("ps", [P, 8, 512], F32))
        loads = []

        def held(name, shape, src):
            t = sb(name, shape)
            loads.append((t[(slice(None),) * len(shape)], src))
            return t

        weights = lambda a: a.rearrange("(k p) n -> p k n", p=P)
        st.w_in = held("w_in", [P, KC, E], weights(T["w_in"]))
        st.w_b = held("w_b", [P, KC, STATE], weights(T["w_b"]))
        st.w_c = held("w_c", [P, E], T["w_c"])
        st.w_o = held("w_o", [P, KC, E], weights(T["w_o"]))
        st.w_k = held("w_k", [P, CTX], T["w_k"])
        st.w_g = held("w_g", [P, KC, 2], weights(T["w_g"]))
        st.w_0a = held("w_0a", [P, KC, FF], weights(T["w_0a"]))
        st.w_1a = held("w_1a", [P, KC, FF], weights(T["w_1a"]))
        st.w_0b = held("w_0b", [P, NF, E], weights(T["w_0b"]))
        st.w_1b = held("w_1b", [P, NF, E], weights(T["w_1b"]))
        st.w_qkv = held("w_qkv", [P, KC, 3 * E], weights(T["w_qkv"]))
        st.w_oatt = held("w_oatt", [P, KC, E], weights(T["w_oatt"]))
        st.w_oxatt = held("w_oxatt", [P, KC, E], weights(T["w_oxatt"]))
        st.bias_rows = held("bias_rows", [P, E], T["bias_rows"])
        st.b_in = held("b_in", [P, KC], T["b_in"])
        st.d_param = held("d_param", [P, KC], T["d_param"])
        st.b_0a = held("b_0a", [P, NF], T["b_0a"])
        st.b_1a = held("b_1a", [P, NF], T["b_1a"])
        st.b_k = held("b_k", [P, 1], T["b_k"])
        st.head_ln = held("head_ln", [P, 2], T["head_ln"])
        a_in = held("a_in", [P, KC, STATE], T["a_in"])
        st.gamma = held("gamma", [P, S], T["gamma"].partition_broadcast(P))
        st.beta = held("beta", [P, S], T["beta"].partition_broadcast(P))
        st.q_norm = held("q_norm", [P, E], T["q_norm"].partition_broadcast(P))
        st.k_norm = held("k_norm", [P, CTX], T["k_norm"].partition_broadcast(P))
        st.ident = held("ident", [P, P], T["ident"])
        causal = held("causal", [P, P], T["causal"])
        st.ones_at = held("ones_at", [P, 64], T["ones_at"])
        st.cos = held("cos", [P, NT, HD], T["cos"])
        st.sin = held("sin", [P, NT, HD // 2], T["sin"])
        st.msin = held("msin", [P, NT, HD // 2], T["msin"])
        st.ones = sb("ones", [P, P])
        st.one = sb("one", [P, 1])
        st.zeros = sb("zeros", [P, E])
        st.eps = sb("eps", [P, 2])
        st.ident_b = sb("ident_b", [P, P], BF16)
        st.causal_b = sb("causal_b", [P, P], BF16)
        st.decay = sb("decay", [P, KC, STATE])
        a_exp = sb("a_exp", [P, KC, STATE])
        st.x = sb("x_rows", [P, NT, E])
        st.xT = sb("x_rowsT", [P, KC, S])
        st.r = sb("r_rows", [P, NT, E])
        st.ctx = sb("ctx_rows", [P, NT, CTX])
        st.ctxT = sb("ctx_T", [P, S])
        st.stats = sb("stats", [P, NT, 6])
        st.meanvar = sb("meanvar", [P, NT, 2])
        st.lnvar = sb("lnvar", [P, NT])
        st.rstd = sb("rstd", [P, NT])

        with nc.Block() as block:
            @block.sync
            def _(sp):
                for t, src in loads:
                    sp.dma_start(t, src).then_inc(sem["weights_loaded"], 16)
                sp.wait_ge(sem["weights_loaded"], 16 * len(loads))

            @block.scalar
            def _(act):
                act.wait_ge(sem["weights_loaded"], 16 * len(loads))
                nc.scalar.activation(a_exp[:, :, :], a_in[:, :, :], ACT.Exp, scale=-1.0).then_inc(sem["made"], 1)
                nc.scalar.activation(st.ident_b[:, :], st.ident[:, :], ACT.Copy)
                nc.scalar.activation(st.causal_b[:, :], causal[:, :], ACT.Copy)

            @block.vector
            def _(dve):
                nc.vector.memset(st.ones[:, :], 1.0)
                nc.vector.memset(st.one[:, :], 1.0)
                nc.vector.memset(st.zeros[:, :], 0.0)
                nc.vector.memset(st.eps[:, 0:1], LN_EPS)
                nc.vector.memset(st.eps[:, 1:2], SIM_EPS)
                dve.wait_ge(sem["made"], 1)
                nc.vector.tensor_scalar(a_exp[:, :, :], a_exp[:, :, :], 1.0, None, ALU.add).then_inc(sem["made"], 1)
                dve.wait_ge(sem["made"], 2)
                nc.vector.reciprocal(st.decay[:, :, :], a_exp[:, :, :])

        with nc.Fori(0, NB) as b:
            def again():
                with nc.Block() as block:
                    clear(nc, sem, block)
            recurrence_pass(nc, st, sem, T, b)
            again()
            if upto >= 2:
                similarity_pass(nc, st, sem)
                again()
            if upto >= 3:
                two_expert_pass(nc, st, sem)
                again()
            if upto >= 4:
                polynomial_pass(nc, st, sem)
                again()
            if upto >= 5:
                softmax_pass(nc, st, sem, T, b)
                again()
            else:
                with nc.Block() as block:
                    @block.sync
                    def _(sp):
                        sp.dma_start(T["x5"][bass.ds(b, 1), :, :].rearrange("a (j p) d -> p (a j) d", p=P), st.x[:, :, :]
                                     ).then_inc(sem["stored"], 16)
                        sp.wait_ge(sem["stored"], 16)
                again()


DISPATCH_SIGNALS = """x5T_loaded x5_loaded const_loaded shared_loaded logits_psum logits_ready top_ready index_ready
less_max exp_top top_sum top_recip weight_ready index_real onehot chosen prefix_psum count_ready step_ready
tiles_real tiles_int tiles_shift tiles_ready ends_ready starts_ready base_ready pos_part pos_ready picked slot_real
slot_ready passed passed_sum table_part table_ready table_psum table_real expert_ready scattered gate_psum up_psum
silu_ready hidden_ready down_psum shared_ready ones_made""".split()


def dispatch_pass(nc, T, M):
    with ExitStack() as ctx:
        sb = lambda name, shape, dt=F32: ctx.enter_context(nc.sbuf_tensor(name, shape, dt))
        sem = signals(nc, ctx, DISPATCH_SIGNALS)
        ps = ctx.enter_context(nc.psum_tensor("ps_dispatch", [P, 8, 512], F32))
        xT = sb("x5T_all", [P, KC, TOK])
        x = sb("x5_all", [P, TT, E])
        router = sb("router", [P, KC, EXPERTS])
        before = sb("before", [P, P])
        iota = sb("iota", [P, EXPERTS])
        tile_no = sb("tile_no", [P, 3])
        ident = sb("ident_d", [P, P])
        ones = sb("ones_d", [P, P])
        ws_gate = sb("ws_gate", [P, KC, FF])
        ws_up = sb("ws_up", [P, KC, FF])
        ws_down = sb("ws_down", [P, NF, E])
        logits = sb("logits", [P, TT, EXPERTS])
        top = sb("top", [P, TT, 8])
        index = sb("index", [P, TT, 8], U32)
        index_f = sb("index_f", [P, TT, 8])
        e_top = sb("e_top", [P, TT, TOP])
        e_sum = sb("e_sum", [P, TT])
        onehot = sb("onehot", [P, TOP, TT, EXPERTS])
        chosen = sb("chosen", [P, 3, TT * EXPERTS])
        count = sb("count", [P, 2, TT, EXPERTS])
        pos = sb("pos", [P, TT, EXPERTS])
        picked = sb("picked", [P, 2, TT, EXPERTS])
        slot_f = sb("slot_f", [P, TT, TOP])
        need_f = sb("need_f", [P, EXPERTS])
        need_i = sb("need_i", [P, 2, EXPERTS], I32)
        need = sb("need", [P, EXPERTS])
        used = sb("used", [P, EXPERTS])
        ends = sb("ends", [P, EXPERTS])
        starts = sb("starts", [P, EXPERTS])
        base = sb("base", [P, EXPERTS])
        passed = sb("passed", [P, 4, EXPERTS])
        sums = sb("passed_sums", [P, 4])
        table = sb("table", [P, 4])
        gate = sb("gate", [P, 2, S])
        hidden = sb("hidden", [P, NF, S])
        x5T = T["x5T"].rearrange("b (k p) t -> b p k t", p=P)
        x5 = T["x5"].rearrange("b (j p) d -> b p j d", p=P)

        with nc.Block() as block:
            @block.sync
            def _(sp):
                for b in range(NB):
                    sp.dma_start(xT[:, :, b * S:(b + 1) * S], x5T[b]).then_inc(sem["x5T_loaded"], 16)
                consts = ((router[:, :, :], T["router"].rearrange("(k p) n -> p k n", p=P)), (before[:, :], T["before"]),
                          (iota[:, :], T["iota"]), (tile_no[:, :], T["tile_no"]), (ident[:, :], T["ident"]))
                for t, src in consts:
                    sp.dma_start(t, src).then_inc(sem["const_loaded"], 16)
                for b in range(NB):
                    sp.dma_start(x[:, b * NT:(b + 1) * NT, :], x5[b]).then_inc(sem["x5_loaded"], 16)
                for t, src in ((ws_gate, T["ws_gate"]), (ws_up, T["ws_up"]), (ws_down, T["ws_down"])):
                    sp.dma_start(t[:, :, :], src.rearrange("(k p) n -> p k n", p=P)).then_inc(sem["shared_loaded"], 16)
                sp.wait_ge(sem["shared_loaded"], 48)

            @block.tensor
            def _(pe):
                pe.wait_ge(sem["x5T_loaded"], 16 * NB)
                pe.wait_ge(sem["const_loaded"], 16 * 5)
                for i in range(TT):
                    for k in range(KC):
                        last = nc.tensor.matmul(ps[:, 0, i * EXPERTS:(i + 1) * EXPERTS], xT[:, k, i * P:(i + 1) * P],
                                                router[:, k, :], start=(k == 0), stop=(k == KC - 1))
                last.then_inc(sem["logits_psum"], 1)
                pe.wait_ge(sem["ones_made"], 1)
                pe.wait_ge(sem["chosen"], 3)
                nc.tensor.matmul(ps[:, 1, :], before[:, :], chosen[:, 2, :], start=True, stop=True)
                nc.tensor.matmul(ps[:, 2, :], ones[:, :], chosen[:, 2, :], start=True, stop=True
                                 ).then_inc(sem["prefix_psum"], 1)
                pe.wait_ge(sem["table_part"], 3)
                pe.wait_ge(sem["passed_sum"], 4)
                nc.tensor.transpose(ps[0:4, 3, 0:P], table[:, :], ident[:, :]).then_inc(sem["table_psum"], 1)
                pe.wait_ge(sem["shared_loaded"], 48)
                with pe.Fori(0, NB) as n:
                    block_T = xT[:, :, bass.ds(n * S, S)]
                    for f in range(NF):
                        pe.wait_ge(sem["hidden_ready"], n * NF + f + 1)
                        for w, bank, s in ((ws_gate, 4, sem["gate_psum"]), (ws_up, 6, sem["up_psum"])):
                            for k in range(KC):
                                last = nc.tensor.matmul(ps[:, bank + f % 2, :], w[:, k, f * P:(f + 1) * P],
                                                        block_T[:, k, :], start=(k == 0), stop=(k == KC - 1))
                            last.then_inc(s, 1)
                    pe.wait_ge(sem["hidden_ready"], n * NF + NF + 2)
                    for j in range(NT):
                        pe.wait_ge(sem["shared_ready"], n * NT + j + 1)
                        for f in range(NF):
                            last = nc.tensor.matmul(ps[:, j % 2, :], hidden[:, f, j * P:(j + 1) * P], ws_down[:, f, :],
                                                    start=(f == 0), stop=(f == NF - 1))
                        last.then_inc(sem["down_psum"], 1)

            @block.scalar
            def _(act):
                act.wait_ge(sem["less_max"], 1)
                nc.scalar.activation(e_top[:, :, :], e_top[:, :, :], ACT.Exp).then_inc(sem["exp_top"], 1)
                with act.Fori(0, NB) as n:
                    for f in range(NF):
                        act.wait_ge(sem["gate_psum"], n * NF + f + 1)
                        act.wait_ge(sem["hidden_ready"], n * NF + f + 1)
                        nc.scalar.activation(gate[:, f % 2, :], ps[:, 4 + f % 2, :], ACT.Silu
                                             ).then_inc(sem["silu_ready"], 1)

            @block.gpsimd
            def _(pool):
                nc.gpsimd.memset(ones[:, :], 1.0).then_inc(sem["ones_made"], 1)
                pool.wait_ge(sem["slot_ready"], 1)
                pool.wait_ge(sem["x5_loaded"], 16 * NB)
                for i in range(TT):
                    for k in range(TOP):
                        nc.gpsimd.indirect_dma_start(
                            T["expert_rows"], bass.IndirectOffsetOnAxis(ap=M.slots[:, i, k:k + 1], axis=0),
                            x[:, i, :], None).then_inc(sem["scattered"], 16)
                pool.wait_ge(sem["scattered"], 16 * TT * TOP)

            @block.vector
            def _(dve):
                flat3 = lambda t: t.rearrange("p i e -> p (i e)")
                dve.wait_ge(sem["logits_psum"], 1)
                nc.vector.tensor_copy(flat3(logits[:, :, :]), ps[:, 0, :]).then_inc(sem["logits_ready"], 1)
                dve.wait_ge(sem["logits_ready"], 1)
                for i in range(TT):
                    nc.vector.max(top[:, i, :], logits[:, i, :]).then_inc(sem["top_ready"], 1)
                dve.wait_ge(sem["top_ready"], TT)
                nc.vector.tensor_tensor(e_top[:, :, :], top[:, :, 0:TOP], top[:, :, 0:1].to_broadcast([P, TT, TOP]),
                                        ALU.subtract).then_inc(sem["less_max"], 1)
                for i in range(TT):
                    nc.vector.max_index(index[:, i, :], top[:, i, :], logits[:, i, :]).then_inc(sem["index_ready"], 1)
                dve.wait_ge(sem["index_ready"], TT)
                nc.vector.tensor_copy(index_f[:, :, :], index[:, :, :]).then_inc(sem["index_real"], 1)
                dve.wait_ge(sem["index_real"], 1)
                experts = iota[:, :].unsqueeze(1).to_broadcast([P, TT, EXPERTS])
                dve.wait_ge(sem["const_loaded"], 16 * 5)
                for k in range(TOP):
                    nc.vector.tensor_tensor(onehot[:, k, :, :], experts,
                                            index_f[:, :, k:k + 1].to_broadcast([P, TT, EXPERTS]), ALU.is_equal
                                            ).then_inc(sem["onehot"], 1)
                dve.wait_ge(sem["onehot"], TOP)
                for n in range(3):
                    before_n = onehot[:, 0, :, :] if n == 0 else chosen[:, n - 1, :].rearrange(
                        "p (i e) -> p i e", e=EXPERTS)
                    if n:
                        dve.wait_ge(sem["chosen"], n)
                    nc.vector.tensor_tensor(chosen[:, n, :].rearrange("p (i e) -> p i e", e=EXPERTS), before_n,
                                            onehot[:, n + 1, :, :], ALU.add).then_inc(sem["chosen"], 1)
                dve.wait_ge(sem["exp_top"], 1)
                nc.vector.tensor_reduce(e_sum[:, :], e_top[:, :, :], AX_X, ALU.add).then_inc(sem["top_sum"], 1)
                dve.wait_ge(sem["top_sum"], 1)
                nc.vector.reciprocal(e_sum[:, :], e_sum[:, :]).then_inc(sem["top_recip"], 1)
                dve.wait_ge(sem["top_recip"], 1)
                nc.vector.tensor_tensor(M.weights[:, :, :], e_top[:, :, :],
                                        e_sum[:, :].unsqueeze(2).to_broadcast([P, TT, TOP]), ALU.mult
                                        ).then_inc(sem["weight_ready"], 1)
                dve.wait_ge(sem["prefix_psum"], 1)
                nc.vector.tensor_copy(flat3(count[:, 0, :, :]), ps[:, 2, :]).then_inc(sem["step_ready"], 1)
                for n in range(4):
                    d = 1 << n
                    src, dst = count[:, n % 2, :, :], count[:, (n + 1) % 2, :, :]
                    dve.wait_ge(sem["step_ready"], 2 * n + 1)
                    nc.vector.tensor_tensor(dst[:, d:TT, :], src[:, d:TT, :], src[:, 0:TT - d, :], ALU.add
                                            ).then_inc(sem["step_ready"], 1)
                    nc.vector.tensor_copy(dst[:, 0:d, :], src[:, 0:d, :]).then_inc(sem["step_ready"], 1)
                dve.wait_ge(sem["step_ready"], 9)
                nc.vector.tensor_scalar(need_f[:, :], count[:, 0, TT - 1, :], float(P - 1), None, ALU.add
                                        ).then_inc(sem["tiles_real"], 1)
                dve.wait_ge(sem["tiles_real"], 1)
                nc.vector.tensor_copy(need_i[:, 0, :], need_f[:, :]).then_inc(sem["tiles_int"], 1)
                dve.wait_ge(sem["tiles_int"], 1)
                nc.vector.tensor_scalar(need_i[:, 1, :], need_i[:, 0, :], 7, None, ALU.arith_shift_right
                                        ).then_inc(sem["tiles_shift"], 1)
                dve.wait_ge(sem["tiles_shift"], 1)
                nc.vector.tensor_copy(need[:, :], need_i[:, 1, :]).then_inc(sem["tiles_ready"], 1)
                dve.wait_ge(sem["tiles_ready"], 1)
                dve.wait_ge(sem["ones_made"], 1)
                nc.vector.tensor_scalar(used[:, :], need[:, :], 0.0, None, ALU.is_gt).then_inc(sem["tiles_ready"], 1)
                nc.vector.tensor_tensor_scan(ends[:, :], ones[:, 0:EXPERTS], need[:, :], 0.0, ALU.mult, ALU.add
                                             ).then_inc(sem["ends_ready"], 1)
                dve.wait_ge(sem["ends_ready"], 1)
                nc.vector.tensor_tensor(starts[:, :], ends[:, :], need[:, :], ALU.subtract).then_inc(sem["starts_ready"], 1)
                dve.wait_ge(sem["starts_ready"], 1)
                nc.vector.tensor_scalar(base[:, :], starts[:, :], float(P), None, ALU.mult).then_inc(sem["base_ready"], 1)
                within = ps[:, 1, :].rearrange("p (i e) -> p i e", e=EXPERTS)
                nc.vector.tensor_copy(pos[:, 0, :], within[:, 0, :]).then_inc(sem["pos_part"], 1)
                nc.vector.tensor_tensor(pos[:, 1:TT, :], within[:, 1:TT, :], count[:, 0, 0:TT - 1, :], ALU.add
                                        ).then_inc(sem["pos_part"], 1)
                dve.wait_ge(sem["base_ready"], 1)
                dve.wait_ge(sem["pos_part"], 2)
                nc.vector.tensor_tensor(pos[:, :, :], pos[:, :, :],
                                        base[:, :].unsqueeze(1).to_broadcast([P, TT, EXPERTS]), ALU.add
                                        ).then_inc(sem["pos_ready"], 1)
                dve.wait_ge(sem["pos_ready"], 1)
                for k in range(TOP):
                    if k >= 2:
                        dve.wait_ge(sem["slot_real"], k - 1)
                    nc.vector.tensor_tensor(picked[:, k % 2, :, :], onehot[:, k, :, :], pos[:, :, :], ALU.mult
                                            ).then_inc(sem["picked"], 1)
                    dve.wait_ge(sem["picked"], k + 1)
                    nc.vector.tensor_reduce(slot_f[:, :, k], picked[:, k % 2, :, :], AX_X, ALU.add
                                            ).then_inc(sem["slot_real"], 1)
                dve.wait_ge(sem["slot_real"], TOP)
                nc.vector.tensor_copy(M.slots[:, :, :], slot_f[:, :, :]).then_inc(sem["slot_ready"], 1)
                dve.wait_ge(sem["tiles_ready"], 2)
                for n in range(2):
                    nc.vector.tensor_scalar(passed[:, n, :], ends[:, :], tile_no[:, n:n + 1], None, ALU.is_le
                                            ).then_inc(sem["passed"], 1)
                dve.wait_ge(sem["passed"], 2)
                for n in range(2):
                    nc.vector.tensor_tensor(passed[:, 2 + n, :], passed[:, n, :], used[:, :], ALU.mult
                                            ).then_inc(sem["passed"], 1)
                dve.wait_ge(sem["passed"], 4)
                nc.vector.tensor_reduce(sums[:, :], passed[:, :, :], AX_X, ALU.add).then_inc(sem["passed"], 1)
                dve.wait_ge(sem["passed"], 5)
                nc.vector.tensor_scalar(table[:, 0:1], sums[:, 0:1], float(EXPERTS - 1), None, ALU.min
                                        ).then_inc(sem["passed_sum"], 1)
                nc.vector.tensor_copy(table[:, 1:2], sums[:, 2:3]).then_inc(sem["passed_sum"], 1)
                nc.vector.tensor_tensor(table[:, 3:4], sums[:, 2:3], sums[:, 3:4], ALU.not_equal
                                        ).then_inc(sem["passed_sum"], 1)
                dve.wait_ge(sem["passed_sum"], 3)
                nc.vector.tensor_tensor(table[:, 2:3], table[:, 3:4], tile_no[:, 2:3], ALU.max
                                        ).then_inc(sem["passed_sum"], 1)
                nc.vector.tensor_copy(sums[:, 0:1], table[:, 3:4]).then_inc(sem["table_part"], 3)
                dve.wait_ge(sem["table_psum"], 1)
                nc.vector.tensor_copy(M.tile_info[:, :], ps[0:4, 3, 0:P]).then_inc(sem["expert_ready"], 1)
                dve.wait_ge(sem["expert_ready"], 1)
                nc.vector.tensor_scalar(M.ring_at[:, :], M.tile_info[:, :], WRING - 1, None, ALU.bitwise_and
                                        ).then_inc(sem["expert_ready"], 1)
                dve.sem_inc(sem["hidden_ready"], 2)
                dve.sem_inc(sem["shared_ready"], 2)
                dve.wait_ge(sem["x5_loaded"], 16 * NB)
                with dve.Fori(0, NB) as n:
                    for f in range(NF):
                        if f == 0:
                            dve.wait_ge(sem["shared_ready"], n * NT + 2)
                        dve.wait_ge(sem["silu_ready"], n * NF + f + 1)
                        dve.wait_ge(sem["up_psum"], n * NF + f + 1)
                        nc.vector.tensor_tensor(hidden[:, f, :], gate[:, f % 2, :], ps[:, 6 + f % 2, :], ALU.mult
                                                ).then_inc(sem["hidden_ready"], 1)
                    for j in range(NT):
                        dve.wait_ge(sem["down_psum"], n * NT + j + 1)
                        nc.vector.tensor_tensor(M.acc[:, bass.ds(n * NT + j, 1), :].rearrange("p a d -> p (a d)"),
                                                x[:, bass.ds(n * NT + j, 1), :].rearrange("p a d -> p (a d)"),
                                                ps[:, j % 2, :], ALU.add).then_inc(sem["shared_ready"], 1)


EXPERT_SIGNALS = """w_loaded row_loaded0 row_loaded1 row_turned rowT_ready gu_psum silu_done h_rows h_turned hT_ready
y_psum y_ready y_stored0 y_stored1 ident_loaded""".split()
PEEL = 4


def expert_pass(nc, T, M):
    with ExitStack() as ctx:
        sb = lambda name, shape, dt=F32: ctx.enter_context(nc.sbuf_tensor(name, shape, dt))
        sem = signals(nc, ctx, EXPERT_SIGNALS)
        ps = ctx.enter_context(nc.psum_tensor("ps_expert", [P, 8, 512], F32))
        ident = sb("ident_e", [P, P])
        w_gu = sb("w_gu", [P, WRING, KC, 2 * INNER])
        w_dn = sb("w_dn", [P, WRING, 2, E])
        rows = sb("rows", [P, 2, E])
        rowsT = sb("rowsT", [P, 2, KC, P])
        silu = sb("silu", [P, 2, INNER])
        h = sb("h_exp", [P, 2, INNER])
        hT = sb("hT_exp", [HALF_IN, 2, 2, P])
        y = sb("y_exp", [P, 2, E])
        row_loaded = (sem["row_loaded0"], sem["row_loaded1"])
        y_stored = (sem["y_stored0"], sem["y_stored1"])
        w_gate = T["w_gate"].rearrange("e (k p) n -> e p k n", p=P)
        w_up = T["w_up"].rearrange("e (k p) n -> e p k n", p=P)
        w_down = T["w_down"].rearrange("e (k p) n -> e p k n", p=HALF_IN)

        def steps(eng, step):
            for q in range(PEEL):
                step(q // 2, q % 2)
            with eng.Fori(PEEL // 2, (TILES - PEEL) // 2) as i:
                for p in range(2):
                    step(i, p)
            for q in range(TILES - PEEL, TILES):
                step(q // 2, q % 2)

        def after(i, p, d):
            at, parity = (p + d) // 2, (p + d) % 2
            if isinstance(i, int):
                q = 2 * i + p + d
                return (i + at, parity) if 0 <= q < TILES else None
            return i + at, parity

        def later(i, n):
            return not isinstance(i, int) or i >= n

        number = lambda i, p: 2 * i + p

        with nc.Block() as block:
            @block.sync
            def _(sp):
                sp.dma_start(ident[:, :], T["ident"]).then_inc(sem["ident_loaded"], 16)
                sp.wait_ge(sem["ident_loaded"], 16)

                def weights(i, p):
                    q = number(i, p)
                    expert = sp.value_load(M.tile_info[0:1, bass.ds(q, 1)], min_val=0, max_val=EXPERTS - 1)
                    at = sp.value_load(M.ring_at[1:2, bass.ds(q, 1)], min_val=0, max_val=WRING - 1)
                    fresh = sp.value_load(M.tile_info[2:3, bass.ds(q, 1)], min_val=0, max_val=1)
                    if later(i, WRING // 2):
                        sp.wait_ge(sem["y_psum"], q - WRING + 1)
                    if later(i, 1) or p:
                        sp.wait_ge(sem["w_loaded"], 48 * (q - 1) + 48)
                    new = fresh > 0
                    for src, lo in ((w_gate, 0), (w_up, INNER)):
                        sp.dma_start(w_gu[:, bass.ds(at, 1), :, lo:lo + INNER].rearrange("p a k n -> p (a k) n"),
                                     src[bass.ds(expert, 1), :, :, :].rearrange("a p k n -> p (a k) n"), cond=new
                                     ).then_inc(sem["w_loaded"], 16)
                    sp.dma_start(w_dn[0:HALF_IN, bass.ds(at, 1), :, :].rearrange("p a k n -> p (a k) n"),
                                 w_down[bass.ds(expert, 1), :, :, :].rearrange("a p k n -> p (a k) n"), cond=new
                                 ).then_inc(sem["w_loaded"], 16)
                steps(sp, weights)

            @block.tensor
            def _(pe):
                def ring(i, p):
                    return pe.value_load(M.ring_at[1:2, bass.ds(number(i, p), 1)], min_val=0, max_val=WRING - 1)

                def turn_rows(i, p):
                    pe.wait_ge(row_loaded[p], 16 * (i + 1))
                    if later(i, 1):
                        pe.wait_ge(sem["rowT_ready"], number(i, p) - 1)
                    for k in range(KC):
                        last = nc.tensor.transpose(ps[:, p, k * P:(k + 1) * P], rows[:, p, k * P:(k + 1) * P],
                                                   ident[:, :])
                    last.then_inc(sem["row_turned"], 1)

                def gate_up(i, p):
                    at = ring(i, p)
                    pe.wait_ge(sem["w_loaded"], 48 * (number(i, p) + 1))
                    pe.wait_ge(sem["rowT_ready"], number(i, p) + 1)
                    if later(i, 1):
                        pe.wait_ge(sem["h_rows"], number(i, p) - 1)
                    for k in range(KC):
                        last = nc.tensor.matmul(ps[:, 2 + p, 0:2 * INNER], rowsT[:, p, k, :],
                                                w_gu[:, bass.ds(at, 1), k, :].rearrange("p a n -> p (a n)"),
                                                start=(k == 0), stop=(k == KC - 1))
                    last.then_inc(sem["gu_psum"], 1)

                def turn_h(i, p):
                    pe.wait_ge(sem["h_rows"], number(i, p) + 1)
                    if later(i, 1):
                        pe.wait_ge(sem["hT_ready"], number(i, p) - 1)
                    for c in range(2):
                        last = nc.tensor.transpose(ps[0:HALF_IN, 4 + p, c * P:(c + 1) * P],
                                                   h[:, p, c * HALF_IN:(c + 1) * HALF_IN], ident[:, :])
                    last.then_inc(sem["h_turned"], 1)

                def down(i, p):
                    at = ring(i, p)
                    pe.wait_ge(sem["hT_ready"], number(i, p) + 1)
                    if later(i, 1):
                        pe.wait_ge(sem["y_ready"], number(i, p) - 1)
                    for c in range(2):
                        last = nc.tensor.matmul(ps[:, 6 + p, :], hT[:, p, c, :],
                                                w_dn[0:HALF_IN, bass.ds(at, 1), c, :].rearrange("p a n -> p (a n)"),
                                                start=(c == 0), stop=(c == 1))
                    last.then_inc(sem["y_psum"], 1)

                def step(i, p):
                    if after(i, p, -1):
                        down(*after(i, p, -1))
                    turn_h(i, p)
                    if after(i, p, 2):
                        turn_rows(*after(i, p, 2))
                    if after(i, p, 1):
                        gate_up(*after(i, p, 1))

                pe.wait_ge(sem["ident_loaded"], 16)
                turn_rows(0, 0)
                turn_rows(0, 1)
                gate_up(0, 0)
                steps(pe, step)
                down(TILES // 2 - 1, 1)

            @block.vector
            def _(dve):
                def keep_rows(i, p):
                    dve.wait_ge(sem["row_turned"], number(i, p) + 1)
                    if later(i, 1):
                        dve.wait_ge(sem["gu_psum"], number(i, p) - 1)
                    nc.vector.tensor_copy(rowsT[:, p, :, :], ps[:, p, :].rearrange("p (k t) -> p k t", k=KC)
                                          ).then_inc(sem["rowT_ready"], 1)

                def step(i, p):
                    dve.wait_ge(sem["silu_done"], number(i, p) + 1)
                    if later(i, 1):
                        dve.wait_ge(sem["h_turned"], number(i, p) - 1)
                    nc.vector.tensor_tensor(h[:, p, :], silu[:, p, :], ps[:, 2 + p, INNER:2 * INNER], ALU.mult
                                            ).then_inc(sem["h_rows"], 1)
                    dve.wait_ge(sem["h_turned"], number(i, p) + 1)
                    if later(i, 1):
                        dve.wait_ge(sem["y_psum"], number(i, p) - 1)
                    nc.vector.tensor_copy(hT[:, p, :, :], ps[0:HALF_IN, 4 + p, 0:2 * P].rearrange(
                        "p (c t) -> p c t", c=2)).then_inc(sem["hT_ready"], 1)
                    if after(i, p, 2):
                        keep_rows(*after(i, p, 2))

                keep_rows(0, 0)
                keep_rows(0, 1)
                steps(dve, step)

            @block.scalar
            def _(act):
                def out_rows(i, p):
                    act.wait_ge(sem["y_psum"], number(i, p) + 1)
                    if later(i, 1):
                        act.wait_ge(y_stored[p], 16 * i)
                    nc.scalar.activation(y[:, p, :], ps[:, 6 + p, :], ACT.Copy).then_inc(sem["y_ready"], 1)

                def step(i, p):
                    act.wait_ge(sem["gu_psum"], number(i, p) + 1)
                    if later(i, 1):
                        act.wait_ge(sem["h_rows"], number(i, p) - 1)
                    nc.scalar.activation(silu[:, p, :], ps[:, 2 + p, 0:INNER], ACT.Silu).then_inc(sem["silu_done"], 1)
                    if after(i, p, -1):
                        out_rows(*after(i, p, -1))
                steps(act, step)
                out_rows(TILES // 2 - 1, 1)

            @block.gpsimd
            def _(pool):
                def load(i, p):
                    if later(i, 1):
                        pool.wait_ge(sem["row_turned"], number(i, p) - 1)
                    pool.dma_start(rows[:, p, :], T["expert_rows"][bass.ds(number(i, p) * P, P), :]
                                   ).then_inc(row_loaded[p], 16)

                def store(i, p):
                    pool.wait_ge(sem["y_ready"], number(i, p) + 1)
                    pool.dma_start(T["expert_out"][bass.ds(number(i, p) * P, P), :], y[:, p, :]
                                   ).then_inc(y_stored[p], 16)

                def step(i, p):
                    if after(i, p, 3):
                        load(*after(i, p, 3))
                    if after(i, p, -1):
                        store(*after(i, p, -1))
                load(0, 0)
                load(0, 1)
                load(1, 0)
                steps(pool, step)
                store(TILES // 2 - 1, 1)
                for s in y_stored:
                    pool.wait_ge(s, 16 * (TILES // 2))


COMBINE_SIGNALS = """slots_now part_ready row_ready stats_ready var_ready rstd_ready x_ready out_stored
weights_now gathered""".split()


def combine_pass(nc, T, M):
    with ExitStack() as ctx:
        sb = lambda name, shape, dt=F32: ctx.enter_context(nc.sbuf_tensor(name, shape, dt))
        sem = signals(nc, ctx, COMBINE_SIGNALS)
        sem["all"] = range(sem["all"][0], sem["all"][-1])
        st = Held()
        slots = sb("slots_b", [P, NT, TOP], U32)
        weights = sb("weights_b", [P, NT, TOP])
        got = sb("got", [P, NT, TOP, E])
        part = sb("part", [P, NT, TOP - 1, E])
        st.r = sb("r_out", [P, NT, E])
        st.x = sb("x_out", [P, NT, E])
        st.stats = sb("stats_o", [P, NT, 6])
        st.meanvar = sb("meanvar_o", [P, NT, 2])
        lnvar = sb("lnvar_o", [P, NT])
        st.rstd = sb("rstd_o", [P, NT])
        eps = sb("eps_o", [P, 1])
        with nc.Block() as block:
            @block.vector
            def _(dve):
                nc.vector.memset(eps[:, :], LN_EPS)
        with nc.Fori(0, NB) as b:
            with nc.Block() as block:
                @block.gpsimd
                def _(pool):
                    pool.wait_ge(sem["slots_now"], 1)
                    for j in range(NT):
                        for k in range(TOP):
                            nc.gpsimd.indirect_dma_start(
                                got[:, j, k, :], None, T["expert_out"],
                                bass.IndirectOffsetOnAxis(ap=slots[:, j, k:k + 1], axis=0)
                                ).then_inc(sem["gathered"], 16)

                @block.vector
                def _(dve):
                    nc.vector.tensor_copy(slots[:, :, :], M.slots[:, bass.ds(b * NT, NT), :]).then_inc(sem["slots_now"], 1)
                    nc.vector.tensor_copy(weights[:, :, :], M.weights[:, bass.ds(b * NT, NT), :]
                                          ).then_inc(sem["weights_now"], 1)
                    dve.wait_ge(sem["weights_now"], 1)
                    dve.wait_ge(sem["gathered"], (b + 1) * (16 * NT * TOP))
                    for j in range(NT):
                        for k in range(TOP):
                            if k:
                                dve.wait_ge(sem["part_ready"], (TOP - 1) * j + k)
                                before = part[:, j, k - 1, :]
                            else:
                                before = M.acc[:, bass.ds(b * NT + j, 1), :].rearrange("p a d -> p (a d)")
                            dst, s = (part[:, j, k, :], sem["part_ready"]) if k < TOP - 1 else (st.r[:, j, :], sem["row_ready"])
                            nc.vector.scalar_tensor_tensor(dst, got[:, j, k, :], weights[:, j, k:k + 1], before,
                                                           ALU.mult, ALU.add).then_inc(s, 1)
                    residual_norm(nc, st, sem, dve)

                @block.scalar
                def _(act):
                    act.wait_ge(sem["var_ready"], NT)
                    nc.scalar.activation(lnvar[:, :], st.meanvar[:, :, 1], ACT.Ln, bias=eps[:, 0:1]
                                         ).then_inc(sem["rstd_ready"], 1)
                    act.wait_ge(sem["rstd_ready"], 1)
                    nc.scalar.activation(st.rstd[:, :], lnvar[:, :], ACT.Exp, scale=-0.5).then_inc(sem["rstd_ready"], 1)

                @block.sync
                def _(sp):
                    sp.wait_ge(sem["x_ready"], NT)
                    sp.dma_start(T["out"][bass.ds(b, 1), :, :].rearrange("a (j p) d -> p (a j) d", p=P), st.x[:, :, :]
                                 ).then_inc(sem["out_stored"], 16)
                    sp.wait_ge(sem["out_stored"], 16)
            with nc.Block() as block:
                clear(nc, sem, block)


def mixture(nc, T):
    with ExitStack() as ctx:
        M = Held()
        M.acc = ctx.enter_context(nc.sbuf_tensor("acc", [P, TT, E], F32))
        M.slots = ctx.enter_context(nc.sbuf_tensor("slots", [P, TT, TOP], U32))
        M.weights = ctx.enter_context(nc.sbuf_tensor("weights", [P, TT, TOP], F32))
        M.tile_info = ctx.enter_context(nc.sbuf_tensor("tile_info", [4, P], I32))
        M.ring_at = ctx.enter_context(nc.sbuf_tensor("ring_at", [4, P], I32))
        dispatch_pass(nc, T, M)
        expert_pass(nc, T, M)
        combine_pass(nc, T, M)


def program(nc, T):
    layers(nc, T)
    mixture(nc, T)


def layout(inputs):
    import numpy as np
    A = {k: np.asarray(v) for k, v in inputs.items()}
    flat = np.ascontiguousarray
    columns = lambda v, n: flat(v.reshape(n, P).T)
    t = np.arange(S, dtype=np.float32)
    inv_freq = (np.float32(1.0) / np.float32(10000.0) ** (np.arange(0, HD, 2, dtype=np.float32) / np.float32(HD))
                ).astype(np.float32)
    angle = (t[:, None] * inv_freq[None, :]).astype(np.float32)
    tiles = lambda a: flat(a.astype(np.float32).reshape(NT, P, -1).transpose(1, 0, 2))
    w_c = np.zeros((P, E), np.float32)
    for c in range(KC):
        w_c[32 * c:32 * c + STATE] = A["L0_attn_C_w"].T
    bias_rows = np.zeros((P, E), np.float32)
    for at, name in ((0, "L0_attn_proj_out_b"), (32, "L0_ffn_b0b"), (64, "L0_ffn_b1b"), (96, "L0_xattn_b_k")):
        bias_rows[at, :A[name].shape[0]] = A[name]
    pick = np.zeros((STATE, STATE * P), np.float32)
    ones_at = np.zeros((P, 64), np.float32)
    ones_at[:, 32] = 1.0
    for s in range(STATE):
        pick[s, s * P:(s + 1) * P] = 1.0
    rows = np.arange(P)
    return {
        "x": flat(A["x"]), "xT": flat(A["x"].transpose(0, 2, 1)),
        "ctx": flat(A["ctx_512"]), "ctxT": flat(A["ctx_512"].transpose(0, 2, 1)),
        "w_in": flat(A["L0_attn_proj_in_w"].T), "w_b": flat(A["L0_attn_B_w"].T), "w_c": w_c,
        "w_o": flat(A["L0_attn_proj_out_w"].T), "w_k": flat(A["L0_xattn_W_k"].T), "w_g": flat(A["L0_ffn_Wg"].T),
        "w_0a": flat(A["L0_ffn_W0a"].T), "w_1a": flat(A["L0_ffn_W1a"].T),
        "w_0b": flat(A["L0_ffn_W0b"].T), "w_1b": flat(A["L0_ffn_W1b"].T),
        "w_qkv": flat(A["L1_attn_w_qkv"]), "w_oatt": flat(A["L1_attn_w_out"]),
        "w_oxatt": flat(A["L1_xattn_w_out"].T), "bias_rows": bias_rows,
        "b_in": columns(A["L0_attn_proj_in_b"], KC), "d_param": columns(A["L0_attn_D_param"], KC),
        "b_0a": columns(A["L0_ffn_b0a"], NF), "b_1a": columns(A["L0_ffn_b1a"], NF),
        "b_k": columns(A["L0_xattn_b_k"], 1),
        "head_ln": flat(np.stack([np.tile(A["L1_attn_ln_scale"], HG), np.tile(A["L1_attn_ln_bias"], HG)], 1)),
        "a_in": flat(A["L0_attn_A"].reshape(KC, P, STATE).transpose(1, 0, 2)),
        "gamma": flat(A["L0_xattn_ln_gamma"]), "beta": flat(A["L0_xattn_ln_beta"]),
        "q_norm": flat(A["L1_xattn_q_norm_w"]), "k_norm": flat(A["L1_xattn_k_norm_w"]),
        "ident": np.eye(P, dtype=np.float32),
        "causal": np.where(rows[None, :] > rows[:, None], np.float32(-1e30), np.float32(0.0)),
        "pick": pick, "ones_at": ones_at,
        "router": flat(A["L1_ffn_router_w"]), "w_gate": flat(A["L1_ffn_w_gate"]), "w_up": flat(A["L1_ffn_w_up"]),
        "w_down": flat(A["L1_ffn_w_down"]), "ws_gate": flat(A["L1_ffn_ws_gate"]), "ws_up": flat(A["L1_ffn_ws_up"]),
        "ws_down": flat(A["L1_ffn_ws_down"]),
        "before": (rows[:, None] < rows[None, :]).astype(np.float32),
        "iota": np.tile(np.arange(EXPERTS, dtype=np.float32), (P, 1)),
        "tile_no": np.stack([rows, rows - 1, rows == 0], 1).astype(np.float32),
        "cos": tiles(np.concatenate([np.cos(angle), np.cos(angle)], 1)),
        "sin": tiles(np.sin(angle)), "msin": tiles(-np.sin(angle)),
    }


def kernel(**inputs):
    import numpy as _np
    import concourse.bacc as _bacc
    from concourse import mybir as _mybir
    from concourse.bass_utils import run_bass_kernel_spmd as _run

    nc = _bacc.Bacc("TRN2", target_bir_lowering=False, num_devices=1)
    arrays, tensors = {}, {}
    for name, a in layout(inputs).items():
        arrays[f"in_{name}"] = a
        tensors[name] = nc.dram_tensor(f"in_{name}", a.shape, _mybir.dt.from_np(a.dtype), kind="ExternalInput").ap()
    tensors["out"] = nc.dram_tensor("out", (NB, S, E), F32, kind="ExternalOutput").ap()
    for name, shape in (("x5", (NB, S, E)), ("x5T", (NB, E, S)), ("expert_rows", (SLOTS, E)), ("expert_out", (SLOTS, E))):
        tensors[name] = nc.dram_tensor(name, shape, F32, kind="Internal").ap()
    program(nc, tensors)
    r = _run(nc, [arrays], core_ids=[0])
    return r.results[0]["out"]
```

```python
from contextlib import ExitStack

import concourse.bass as bass
from concourse import mybir

F32 = mybir.dt.float32
BF16 = mybir.dt.bfloat16
I32 = mybir.dt.int32
U32 = mybir.dt.uint32
ALU = mybir.AluOpType
ACT = mybir.ActivationFunctionType
AX_X = mybir.AxisListType.X

P = 128
NB, S, E = 4, 512, 512
NT, KC = S // P, E // P
STATE = 16
CTX = 128
FF = 1024
NF = FF // P
HEADS, HD = 16, 32
HG = P // HD
RING = 4
EXPERTS, TOP = 32, 4
INNER = 192
HALF_IN = INNER // 2
TOK = NB * S
TT = TOK // P
TILES = TOK * TOP // P + EXPERTS
SLOTS = TILES * P
WRING = 4
LN_EPS = 1e-5
SIM_EPS = 1e-6


class Held:
    pass


def run_pass(nc, body):
    with nc.Block() as block:
        body(block)


def load_log_exp(nc):
    nc.scalar.preload_act_table_set("natural_log_exp_and_others")


def norm_rows(nc, st, sem, eng, row, tiles=NT):
    def finish(j):
        eng.wait_ge(sem["rstd_ready"], 2 * j + 2)
        nc.vector.tensor_scalar(st.x[:, j, :], st.r[:, j, :], st.meanvar[:, j, 0:1], st.rstd[:, j:j + 1],
                                ALU.subtract, ALU.mult).then_inc(sem["x_ready"], 1)
    for j in range(tiles):
        row(j)
        eng.wait_ge(sem["row_ready"], j + 1)
        nc.vector.bn_stats(st.stats[:, j, :], st.r[:, j, :]).then_inc(sem["stats_ready"], 1)
        eng.wait_ge(sem["stats_ready"], j + 1)
        nc.vector.bn_aggr(st.meanvar[:, j, :], st.stats[:, j, :]).then_inc(sem["var_ready"], 1)
        if j:
            finish(j - 1)
    finish(tiles - 1)


def norm_scale(nc, st, sem, eng, tiles=NT):
    for j in range(tiles):
        eng.wait_ge(sem["var_ready"], j + 1)
        nc.scalar.activation(st.lnvar[:, j:j + 1], st.meanvar[:, j, 1:2], ACT.Ln, bias=st.eps[:, 0:1]
                             ).then_inc(sem["rstd_ready"], 1)
        eng.wait_ge(sem["rstd_ready"], 2 * j + 1)
        nc.scalar.activation(st.rstd[:, j:j + 1], st.lnvar[:, j:j + 1], ACT.Exp, scale=-0.5
                             ).then_inc(sem["rstd_ready"], 1)


def keep_transposed(nc, st, sem, eng, first=4):
    for j in range(NT):
        eng.wait_ge(sem["xt_psum"], j + 1)
        nc.scalar.activation(st.xT[:, :, j * P:(j + 1) * P],
                             st.ps[:, first + j, :].rearrange("p (k t) -> p k t", k=KC), ACT.Copy).then_inc(sem["xt_ready"], 1)


def transpose_rows(nc, st, sem, eng, first=4):
    for j in range(NT):
        eng.wait_ge(sem["x_ready"], j + 1)
        for k in range(KC):
            last = nc.tensor.transpose(st.ps[:, first + j, k * P:(k + 1) * P], st.x[:, j, k * P:(k + 1) * P],
                                       st.ident[:, :])
        last.then_inc(sem["xt_psum"], 1)


def project_rows(nc, out, lhs, j, weights, chunks, total):
    for k in chunks:
        last = nc.tensor.matmul(out, lhs[:, k, j * P:(j + 1) * P], weights[:, k, :],
                                start=(k == 0), stop=(k == total - 1))
    return last


def project_attended(nc, st, sem, eng, oT, weights):
    eng.wait_ge(sem["o_ready"], NT * (KC - 1))
    project = lambda j, chunks: project_rows(nc, st.ps[:, j, :], oT, j, weights, chunks, KC)
    project(0, range(KC - 1))
    for j in range(NT):
        if j + 1 < NT:
            project(j + 1, range(KC - 1))
        eng.wait_ge(sem["o_ready"], NT * (KC - 1) + j + 1)
        project(j, range(KC - 1, KC)).then_inc(sem["out_psum"], 1)


def attended(nc, st, sem, eng, oT, rden, pv_needed, g, j):
    at = slice(j * P, (j + 1) * P)
    n = NT * g + j
    eng.wait_ge(sem["pv_done"], pv_needed)
    nc.vector.reciprocal(rden[:, n % 2, :], st.ps[:, 5 + 2 * (g % 2), at]).then_inc(sem["den_ready"], 1)
    eng.wait_ge(sem["den_ready"], n + 1)
    nc.vector.tensor_tensor(oT[:, g, at], st.ps[:, 4 + 2 * (g % 2), at], rden[:, n % 2, :], ALU.mult
                            ).then_inc(sem["o_ready"], 1)


def by_vector(i):
    return i % 4 == 3 or i % 8 == 1


def shared_out(i):
    return sum(not by_vector(n) for n in range(i))


def recurrence_pass(nc, st, sem, T, b):
    with ExitStack() as ctx:
        sb = lambda name, shape, dt=F32: ctx.enter_context(nc.sbuf_tensor(name, shape, dt))
        xpT = sb("xpT", [P, KC, S])
        delta = sb("delta", [STATE, S])
        dbc = sb("dbc", [P, 2, S])
        u = sb("u", [P, RING, S])
        h = sb("h", [P, RING, S])
        sums = sb("sums", [P, S])
        Y_BANKS = (7, 5, 6, 4)
        yT = h
        absz, expz, logz = (u[0:STATE, n, :] for n in range(3))

        def body(block):
            @block.sync
            def _(sp):
                sp.wait_ge(sem["rows_stored"], b * 32 + 32)
                sp.dma_start(st.x[:, :, :], T["x"][bass.ds(b, 1), :, :].rearrange("a (j p) d -> p (a j) d", p=P)
                             ).then_inc(sem["x_loaded"], 16)
                sp.dma_start(st.ctxT[:, :], T["ctxT"][bass.ds(b, 1), :, :].rearrange("a c t -> c (a t)")
                             ).then_inc(sem["ctx_loaded"], 16)
                sp.dma_start(st.ctx[:, :, :], T["ctx"][bass.ds(b, 1), :, :].rearrange("a (j p) c -> p (a j) c", p=P)
                             ).then_inc(sem["ctx_loaded"], 16)
                part = T["expert_rows"][bass.ds(b * (SLOTS // NB), SLOTS // NB), :].rearrange("(p q) (k d) -> p (q k) d", p=P, k=KC)
                sp.dma_start(part, st.zeros[:, :].unsqueeze(1).to_broadcast([P, TILES // NB * KC, P])
                             ).then_inc(sem["stored"], 16)
                sp.wait_ge(sem["ctx_loaded"], 32)
                sp.wait_ge(sem["stored"], 16)
                sp.wait_ge(sem["later_loaded"], 16 * st.later)

            @block.tensor
            def _(pe):
                for c in range(KC):
                    for k in range(KC):
                        last = nc.tensor.matmul(st.ps[:, c, :], st.w_in[:, k, c * P:(c + 1) * P], st.xT_in[:, k, :],
                                                start=(k == 0), stop=(k == KC - 1))
                    last.then_inc(sem["xp_psum"], 1)
                for k in range(KC):
                    pe.wait_ge(sem["xp_ready"], k + 1)
                    last = nc.tensor.matmul(st.ps[0:STATE, 7, :], st.w_b[:, k, :], xpT[:, k, :],
                                            start=(k == 0), stop=(k == KC - 1))
                last.then_inc(sem["z_psum"], 1)
                pe.wait_ge(sem["delta_ready"], 1)

                def spread(s):
                    if s >= 2:
                        pe.wait_ge(sem["spread_copied"], s - 1)
                    nc.tensor.matmul(st.ps[:, 5 + s % 2, :], st.ident[0:STATE, s:s + 1].to_broadcast([STATE, P]), delta[:, :],
                                     start=True, stop=True).then_inc(sem["spread_psum"], 1)

                spread(0)
                spread(1)
                for j in range(NT):
                    nc.tensor.matmul(st.ps[:, j, :], st.ones[0:1, 0:P], st.bias_rows[0:1, :], start=True, stop=False)
                for s in range(STATE):
                    for c in range(KC):
                        i = s * KC + c
                        pe.wait_ge(sem["scanned"], i + 1)
                        nc.tensor.matmul(st.ps[c * 32:(c + 1) * 32, 4, :], st.ones_at[:, 32 - s:64 - s],
                                         h[:, i % RING, :], start=(s == 0), stop=(s == STATE - 1),
                                         tile_position=(0, c * 32)).then_inc(sem["summed"], 1)
                    if s + 2 < STATE:
                        spread(s + 2)
                pe.wait_ge(sem["sums_ready"], 1)
                pe.wait_ge(sem["spread_copied"], STATE)
                for c in range(KC):
                    nc.tensor.matmul(st.ps[:, Y_BANKS[c], :], st.w_c[:, c * P:(c + 1) * P], sums[:, :],
                                     start=True, stop=True).then_inc(sem["y_psum"], 1)

                def project(j, chunks):
                    for k in chunks:
                        last = nc.tensor.matmul(st.ps[:, j, :], yT[:, k, j * P:(j + 1) * P], st.w_o[:, k, :],
                                                start=False, stop=(k == KC - 1))
                    return last
                pe.wait_ge(sem["y_ready"], 1)
                for j in range(NT):
                    project(j, range(1))
                pe.wait_ge(sem["y_ready"], KC)
                for j in range(NT):
                    project(j, range(1, KC)).then_inc(sem["out_psum"], 1)
                transpose_rows(nc, st, sem, pe)

            @block.scalar
            def _(act):
                load_log_exp(nc)
                for c in range(KC):
                    act.wait_ge(sem["xp_psum"], c + 1)
                    nc.scalar.activation(xpT[:, c, :], st.ps[:, c, :], ACT.Identity,
                                         bias=st.b_in[:, c:c + 1]).then_inc(sem["xp_ready"], 1)
                act.wait_ge(sem["z_psum"], 1)
                nc.scalar.activation(absz, st.ps[0:STATE, 7, :], ACT.Abs).then_inc(sem["soft"], 1)
                act.wait_ge(sem["soft"], 1)
                nc.scalar.activation(expz, absz, ACT.Exp, scale=-1.0).then_inc(sem["soft"], 1)
                act.wait_ge(sem["soft"], 2)
                nc.scalar.activation(logz, expz, ACT.Ln, bias=st.one[0:STATE, 0:1]).then_inc(sem["soft"], 1)
                for s in range(STATE):
                    act.wait_ge(sem["spread_psum"], s + 1)
                    if s >= 2:
                        act.wait_ge(sem["product"], shared_out((s - 1) * KC))
                        act.wait_ge(sem["own_product"], (s - 1) * KC - shared_out((s - 1) * KC))
                    nc.scalar.activation(dbc[:, s % 2, :], st.ps[:, 5 + s % 2, :], ACT.Copy
                                         ).then_inc(sem["spread_copied"], 1)
                norm_scale(nc, st, sem, act)
                keep_transposed(nc, st, sem, act)

            @block.gpsimd
            def _(pool):
                for s in range(STATE):
                    pool.wait_ge(sem["spread_copied"], s + 1)
                    for c in range(KC):
                        i = s * KC + c
                        if by_vector(i):
                            continue
                        if i >= RING:
                            pool.wait_ge(sem["scanned"], i - RING + 1)
                        nc.gpsimd.tensor_tensor(u[:, i % RING, :], xpT[:, c, :], dbc[:, s % 2, :], ALU.mult
                                                ).then_inc(sem["product"], 1)

            @block.vector
            def _(dve):
                dve.wait_ge(sem["soft"], 3)
                nc.vector.scalar_tensor_tensor(delta[:, :], st.ps[0:STATE, 7, :], 0.0, logz,
                                               ALU.max, ALU.add).then_inc(sem["delta_ready"], 1)
                def own_product(i):
                    s, c = i // KC, i % KC
                    dve.wait_ge(sem["spread_copied"], s + 1)
                    if i >= RING:
                        dve.wait_ge(sem["scanned"], i - RING + 1)
                    nc.vector.tensor_tensor(u[:, i % RING, :], xpT[:, c, :], dbc[:, s % 2, :], ALU.mult
                                            ).then_inc(sem["own_product"], 1)

                for i in range(STATE * KC):
                    s, c = i // KC, i % KC
                    if i + 1 < STATE * KC and by_vector(i + 1):
                        own_product(i + 1)
                    if by_vector(i):
                        dve.wait_ge(sem["own_product"], i + 1 - shared_out(i + 1))
                    else:
                        dve.wait_ge(sem["product"], shared_out(i + 1))
                    if i >= RING:
                        dve.wait_ge(sem["summed"], i - RING + 1)
                    nc.vector.tensor_tensor_scan(
                        h[:, i % RING, :], st.decay[:, c, s:s + 1].to_broadcast([P, S]),
                        u[:, i % RING, :], 0.0, ALU.mult, ALU.add).then_inc(sem["scanned"], 1)
                dve.wait_ge(sem["summed"], STATE * KC)
                nc.vector.tensor_copy(sums[:, :], st.ps[:, 4, :]).then_inc(sem["sums_ready"], 1)
                for c in range(KC):
                    dve.wait_ge(sem["y_psum"], c + 1)
                    nc.vector.scalar_tensor_tensor(yT[:, c, :], xpT[:, c, :], st.d_param[:, c:c + 1],
                                                   st.ps[:, Y_BANKS[c], :], ALU.mult, ALU.add
                                                   ).then_inc(sem["y_ready"], 1)
                dve.wait_ge(sem["x_loaded"], 16)

                def row(j):
                    dve.wait_ge(sem["out_psum"], j + 1)
                    nc.vector.scalar_tensor_tensor(st.r[:, j, :], st.x[:, j, :], 2.0, st.ps[:, j, :],
                                                   ALU.mult, ALU.add).then_inc(sem["row_ready"], 1)
                norm_rows(nc, st, sem, dve, row)
        run_pass(nc, body)


def similarity_pass(nc, st, sem, T):
    with ExitStack() as ctx:
        sb = lambda name, shape, dt=F32: ctx.enter_context(nc.sbuf_tensor(name, shape, dt))
        kv = sb("kv", [P, NT, CTX])
        kvT = sb("kvT", [P, S])
        mixT = sb("mixT", [P, S])
        simil = sb("simil", [P, NT, S])
        simil_n = sb("simil_n", [P, NT, S])
        simil_g = sb("simil_g", [P, NT, S])
        nmax = sb("nmax", [P, NT])
        esum = sb("esum", [P, NT])
        rsum = sb("rsum", [P, NT])
        s_stats = sb("s_stats", [P, NT, 6])
        s_mv = sb("s_mv", [P, NT, 2])
        s_ln = sb("s_ln", [P, NT])
        s_rstd = sb("s_rstd", [P, NT])
        SCALE = float(E) ** -0.5
        gamma = sb("gamma", [P, S])
        beta = sb("beta", [P, S])

        def body(block):
            @block.sync
            def _(sp):
                for t, src in ((gamma, T["gamma"]), (beta, T["beta"])):
                    sp.dma_start(t[:, :], src.partition_broadcast(P)).then_inc(sem["affine_loaded"], 16)

            @block.tensor
            def _(pe):
                for j in range(NT):
                    out = st.ps[:, 0, j * P:(j + 1) * P]
                    nc.tensor.matmul(out, st.ctxT[:, j * P:(j + 1) * P], st.w_k[:, :], start=True, stop=False)
                    last = nc.tensor.matmul(out, st.ones[96:97, 0:P], st.bias_rows[96:97, 0:CTX],
                                            start=False, stop=True, tile_position=(96, 0))
                last.then_inc(sem["kv_psum"], 1)
                nc.tensor.matmul(st.ps[:, 1, :], st.w_k[:, :], st.ctxT[:, :], start=True, stop=True
                                 ).then_inc(sem["kvT_psum"], 1)
                pe.wait_ge(sem["kv_ready"], 1)
                for j in range(NT):
                    last = nc.tensor.matmul(st.ps[:, 2, :], kv[:, j, :], st.xT[:, j, :],
                                            start=(j == 0), stop=(j == NT - 1))
                last.then_inc(sem["mix_psum"], 1)
                pe.wait_ge(sem["kvT_ready"], 1)
                pe.wait_ge(sem["mix_ready"], 1)
                for j in range(NT):
                    nc.tensor.matmul(st.ps[:, 4 + j, :], mixT[:, j * P:(j + 1) * P], kvT[:, :],
                                     start=True, stop=True).then_inc(sem["sim_psum"], 1)
                transpose_rows(nc, st, sem, pe)

            @block.scalar
            def _(act):
                load_log_exp(nc)
                act.wait_ge(sem["kv_psum"], 1)
                nc.scalar.activation(kv[:, :, :], st.ps[:, 0, :].rearrange("p (j c) -> p j c", j=NT), ACT.Copy
                                     ).then_inc(sem["kv_ready"], 1)
                act.wait_ge(sem["kvT_psum"], 1)
                nc.scalar.activation(kvT[:, :], st.ps[:, 1, :], ACT.Identity, bias=st.b_k[:, 0:1]
                                     ).then_inc(sem["kvT_ready"], 1)
                for j in range(NT):
                    act.wait_ge(sem["sim_var"], j + 1)
                    nc.scalar.activation(s_ln[:, j:j + 1], s_mv[:, j, 1:2], ACT.Ln, bias=st.eps[:, 1:2]
                                         ).then_inc(sem["sim_rstd"], 1)
                    act.wait_ge(sem["sim_rstd"], 2 * j + 1)
                    nc.scalar.activation(s_rstd[:, j:j + 1], s_ln[:, j:j + 1], ACT.Exp, scale=-0.5
                                         ).then_inc(sem["sim_rstd"], 1)
                for j in range(NT):
                    act.wait_ge(sem["sim_max"], j + 1)
                    nc.scalar.activation(simil[:, j, :], simil_g[:, j, :], ACT.Exp, bias=nmax[:, j:j + 1],
                                         accum_out=esum[:, j:j + 1]).then_inc(sem["sim_exp"], 1)
                norm_scale(nc, st, sem, act)
                keep_transposed(nc, st, sem, act)

            @block.vector
            def _(dve):
                dve.wait_ge(sem["mix_psum"], 1)
                nc.vector.tensor_scalar(mixT[:, :], st.ps[:, 2, :], SCALE, None, ALU.mult).then_inc(sem["mix_ready"], 1)
                dve.wait_ge(sem["affine_loaded"], 32)
                for j in range(NT):
                    dve.wait_ge(sem["sim_psum"], j + 1)
                    nc.vector.bn_stats(s_stats[:, j, :], st.ps[:, 4 + j, :]).then_inc(sem["sim_stats"], 1)
                    dve.wait_ge(sem["sim_stats"], j + 1)
                    nc.vector.bn_aggr(s_mv[:, j, :], s_stats[:, j, :]).then_inc(sem["sim_var"], 1)
                    dve.wait_ge(sem["sim_var"], j + 1)
                    nc.vector.scalar_tensor_tensor(simil_n[:, j, :], st.ps[:, 4 + j, :], s_mv[:, j, 0:1], gamma[:, :],
                                                   ALU.subtract, ALU.mult).then_inc(sem["sim_gamma"], 1)
                for j in range(NT):
                    dve.wait_ge(sem["sim_rstd"], 2 * j + 2)
                    dve.wait_ge(sem["sim_gamma"], j + 1)
                    nc.vector.scalar_tensor_tensor(simil_g[:, j, :], simil_n[:, j, :], s_rstd[:, j:j + 1], beta[:, :],
                                                   ALU.mult, ALU.add).then_inc(sem["sim_affine"], 1)
                    dve.wait_ge(sem["sim_affine"], j + 1)
                    nc.vector.tensor_reduce(nmax[:, j:j + 1], simil_g[:, j, :], AX_X, ALU.max, negate=True
                                            ).then_inc(sem["sim_max"], 1)

                def row(j):
                    dve.wait_ge(sem["sim_exp"], j + 1)
                    nc.vector.reciprocal(rsum[:, j:j + 1], esum[:, j:j + 1]).then_inc(sem["sim_recip"], 1)
                    dve.wait_ge(sem["sim_recip"], j + 1)
                    nc.vector.scalar_tensor_tensor(st.r[:, j, :], simil[:, j, :], rsum[:, j:j + 1], st.x[:, j, :],
                                                   ALU.mult, ALU.add).then_inc(sem["row_ready"], 1)
                norm_rows(nc, st, sem, dve, row)
        run_pass(nc, body)


def load_transposed(nc, st, T, b, eng, done):
    eng.dma_start(st.xT_in[:, :, :], T["xT"][bass.ds(b, 1), :, :].rearrange("a (k p) t -> p (a k) t", p=P)
                  ).then_inc(done, 16)


def two_expert_pass(nc, st, sem, T, b):
    with ExitStack() as ctx:
        sb = lambda name, shape, dt=F32: ctx.enter_context(nc.sbuf_tensor(name, shape, dt))
        h0T = sb("h0T", [P, NF, S])
        h1T = sb("h1T", [P, NF, S])
        scores = sb("scores", [P, 2 * NT])
        first = sb("first", [P, NT])
        second = sb("second", [P, NT])
        bias_0b = sb("bias_0b", [P, E])
        bias_1b = sb("bias_1b", [P, E])
        half = sb("half_bias", [P, E])

        def body(block):
            @block.sync
            def _(sp):
                for t, src in ((bias_0b, T["b_0b"]), (bias_1b, T["b_1b"])):
                    sp.dma_start(t[:, :], src.partition_broadcast(P)).then_inc(sem["bias_loaded"], 16)
                load_transposed(nc, st, T, (b + 1) % NB, sp, sem["xT_loaded"])
                sp.wait_ge(sem["xT_loaded"], 16)

            @block.gpsimd
            def _(pool):
                pool.wait_ge(sem["choice"], 2)
                pool.wait_ge(sem["bias_loaded"], 32)
                for j in range(NT):
                    if j:
                        pool.wait_ge(sem["biased"], 3 * j)
                    nc.gpsimd.tensor_tensor(half[:, :], bias_0b[:, :], first[:, j:j + 1].to_broadcast([P, E]), ALU.mult
                                            ).then_inc(sem["biased"], 1)
                    nc.gpsimd.tensor_tensor(st.r[:, j, :], bias_1b[:, :], second[:, j:j + 1].to_broadcast([P, E]),
                                            ALU.mult).then_inc(sem["biased"], 1)
                    pool.wait_ge(sem["biased"], 3 * j + 2)
                    nc.gpsimd.tensor_tensor(st.r[:, j, :], st.r[:, j, :], half[:, :], ALU.add
                                            ).then_inc(sem["biased"], 1)

            @block.tensor
            def _(pe):
                for j in range(NT):
                    for k in range(KC):
                        last = nc.tensor.matmul(st.ps[:, 7, 2 * j:2 * j + 2], st.xT[:, k, j * P:(j + 1) * P],
                                                st.w_g[:, k, :], start=(k == 0), stop=(k == KC - 1))
                last.then_inc(sem["score_psum"], 1)
                for f in range(NF):
                    for n, (w, used) in enumerate(((st.w_0a, sem["h0_ready"]), (st.w_1a, sem["h1_ready"]))):
                        bank = 2 * (f % 2) + n
                        if f >= 2:
                            pe.wait_ge(used, f - 1)
                        for k in range(KC):
                            last = nc.tensor.matmul(st.ps[:, bank, :], w[:, k, f * P:(f + 1) * P], st.xT[:, k, :],
                                                    start=(k == 0), stop=(k == KC - 1))
                        last.then_inc((sem["h0_psum"], sem["h1_psum"])[n], 1)
                pe.wait_ge(sem["h0_ready"], NF)
                pe.wait_ge(sem["score_ready"], 1)
                for j in range(NT):
                    if j >= 2:
                        pe.wait_ge(sem["row_ready"], j - 1)
                    project_rows(nc, st.ps[:, 4 + j % 2, :], h0T, j, st.w_0b, range(NF), NF
                                 ).then_inc(sem["out_psum"], 1)
                    pe.wait_ge(sem["h1_ready"], NF)
                    project_rows(nc, st.ps[:, 6 + j % 2, :], h1T, j, st.w_1b, range(NF), NF
                                 ).then_inc(sem["out_psum"], 1)
                transpose_rows(nc, st, sem, pe, first=0)

            @block.scalar
            def _(act):
                for f in range(NF):
                    act.wait_ge(sem["h0_psum"], f + 1)
                    nc.scalar.activation(h0T[:, f, :], st.ps[:, 2 * (f % 2), :], ACT.Gelu,
                                         bias=st.b_0a[:, f:f + 1]).then_inc(sem["h0_ready"], 1)
                load_log_exp(nc)
                norm_scale(nc, st, sem, act)
                keep_transposed(nc, st, sem, act, first=0)

            @block.vector
            def _(dve):
                dve.wait_ge(sem["score_psum"], 1)
                nc.vector.tensor_copy(scores[:, :], st.ps[:, 7, 0:2 * NT]).then_inc(sem["score_ready"], 1)
                dve.wait_ge(sem["score_ready"], 1)
                pair = scores[:, :].rearrange("p (j e) -> p j e", e=2)
                nc.vector.tensor_tensor(first[:, :], pair[:, :, 0], pair[:, :, 1], ALU.is_ge).then_inc(sem["choice"], 1)
                dve.wait_ge(sem["choice"], 1)
                nc.vector.tensor_scalar(second[:, :], first[:, :], -1.0, 1.0, ALU.mult, ALU.add
                                        ).then_inc(sem["choice"], 1)
                for f in range(NF):
                    dve.wait_ge(sem["h1_psum"], f + 1)
                    nc.vector.tensor_scalar(h1T[:, f, :], st.ps[:, 2 * (f % 2) + 1, :], st.b_1a[:, f:f + 1], 0.0,
                                            ALU.add, ALU.max).then_inc(sem["h1_ready"], 1)
                for j in range(NT):
                    dve.wait_ge(sem["biased"], 3 * j + 3)
                    nc.vector.tensor_tensor(st.r[:, j, :], st.r[:, j, :], st.x[:, j, :], ALU.add
                                            ).then_inc(sem["residual"], 1)

                def row(j):
                    dve.wait_ge(sem["residual"], j + 1)
                    dve.wait_ge(sem["out_psum"], 2 * j + 1)
                    nc.vector.scalar_tensor_tensor(st.r[:, j, :], st.ps[:, 4 + j % 2, :], first[:, j:j + 1],
                                                   st.r[:, j, :], ALU.mult, ALU.add).then_inc(sem["half_row"], 1)
                    dve.wait_ge(sem["half_row"], j + 1)
                    dve.wait_ge(sem["out_psum"], 2 * j + 2)
                    nc.vector.scalar_tensor_tensor(st.r[:, j, :], st.ps[:, 6 + j % 2, :], second[:, j:j + 1],
                                                   st.r[:, j, :], ALU.mult, ALU.add).then_inc(sem["row_ready"], 1)
                norm_rows(nc, st, sem, dve, row)
        run_pass(nc, body)


def by_head(ap, heads):
    return ap.rearrange("p (h d) -> p h d", h=heads)


def polynomial_pass(nc, st, sem):
    QK = 2 * E
    NH2 = 2 * HEADS
    HALF = HD // 2
    STEPS = 2 * KC * NT
    SQ = 3
    with ExitStack() as ctx:
        sb = lambda name, shape, dt=F32: ctx.enter_context(nc.sbuf_tensor(name, shape, dt))
        v = sb("v", [P, NT, E])
        qT = sb("qT", [P, KC, S])
        kT = sb("kT", [P, KC, S])
        hsum = sb("hsum", [P, NH2])
        hmean = sb("hmean", [P, NH2])
        hvar = sb("hvar", [P, NH2])
        hln = sb("hln", [P, NH2])
        hrstd = sb("hrstd", [P, NH2])
        sq = sb("sq", [P, SQ, 2 * S])
        turned = [sq[:, n, :] for n in range(2)]
        other = [st.r[:, 2 * n:2 * n + 2, :].rearrange("p a d -> p (a d)") for n in range(2)]
        rden = sb("rden", [P, 2, P])
        oT = qT

        def body(block):
            @block.tensor
            def _(pe):
                def project(j, n, bank, done):
                    for k in range(KC):
                        last = nc.tensor.matmul(st.ps[:, bank, :], st.xT[:, k, j * P:(j + 1) * P],
                                                st.w_qkv[:, k, n * E:(n + 1) * E], start=(k == 0), stop=(k == KC - 1))
                    last.then_inc(done, 1)

                def project_qk(j):
                    if j >= 2:
                        pe.wait_ge(sem["qk_rotated"], 3 * (j - 1))
                    for n in range(2):
                        project(j, n, 2 * (j % 2) + n, sem["qk_rows"])

                def project_v(j):
                    if j >= 2:
                        pe.wait_ge(sem["v_ready"], j - 1)
                    project(j, 2, 4 + j % 2, sem["v_rows"])

                def turn(j):
                    pe.wait_ge(sem["qk_normed"], j + 1)
                    if j >= 1:
                        pe.wait_ge(sem["qkT_ready"], 2 * j)
                    for n in range(2):
                        for k in range(KC):
                            at = n * E + k * P
                            last = nc.tensor.transpose(st.ps[:, 6 + n, k * P:(k + 1) * P], other[j % 2][:, at:at + P],
                                                       st.ident[:, :])
                        last.then_inc(sem["qkT_psum"], 1)

                project_qk(0)
                project_qk(1)
                for j in range(2, NT):
                    project_qk(j)
                    turn(j - 2)
                project_v(0)
                turn(NT - 2)
                for j in range(1, NT - 1):
                    project_v(j)
                turn(NT - 1)
                project_v(NT - 1)
                pe.wait_ge(sem["qkT_ready"], 2 * NT)
                pe.wait_ge(sem["v_ready"], NT)

                def weigh(n):
                    g, pair, i = n // 8, n // 4 % 2, n % 4
                    w = S - i * P
                    pe.wait_ge(sem["weighed"], n + 1)
                    for q in range(2):
                        hh = 2 * pair + q
                        part = slice(hh * HD, (hh + 1) * HD)
                        a = sq[:, n % SQ, q * S:q * S + w]
                        head = g * HG + hh
                        nc.tensor.matmul(st.ps[part, 4 + 2 * (g % 2), i * P:S], v[:, i, head * HD:(head + 1) * HD], a,
                                         start=(i == 0), stop=(i == NT - 1), tile_position=(0, hh * HD))
                        last = nc.tensor.matmul(st.ps[part, 5 + 2 * (g % 2), i * P:S], st.ones[:, 0:HD], a,
                                                start=(i == 0), stop=(i == NT - 1), tile_position=(0, hh * HD))
                    last.then_inc(sem["pv_done"], 1)

                for n in range(STEPS + 2):
                    if n < STEPS:
                        g, pair, i = n // 8, n // 4 % 2, n % 4
                        if n >= 2:
                            pe.wait_ge(sem["squared"], n - 1)
                        for q in range(2):
                            part = slice((2 * pair + q) * HD, (2 * pair + q + 1) * HD)
                            last = nc.tensor.matmul(st.ps[:, 2 * (n % 2) + q, 0:S - i * P],
                                                    kT[part, g, i * P:(i + 1) * P], qT[part, g, i * P:S],
                                                    start=True, stop=True, tile_position=((2 * pair + q) * HD, 0))
                        last.then_inc(sem["qk_psum"], 1)
                    if n >= 2:
                        if n - 2 >= 16 and (n - 2) % 8 == 0:
                            pe.wait_ge(sem["o_ready"], NT * ((n - 2) // 8 - 1))
                        weigh(n - 2)
                project_attended(nc, st, sem, pe, oT, st.w_oatt)
                transpose_rows(nc, st, sem, pe)

            @block.scalar
            def _(act):
                load_log_exp(nc)
                def keep_v(j):
                    act.wait_ge(sem["v_rows"], j + 1)
                    nc.scalar.activation(v[:, j, :], st.ps[:, 4 + j % 2, :], ACT.Copy).then_inc(sem["v_ready"], 1)

                def scale(j):
                    act.wait_ge(sem["qk_centred"], j + 1)
                    nc.scalar.activation(turned[j % 2], other[j % 2], ACT.Square).then_inc(sem["qk_square"], 1)
                    act.wait_ge(sem["qk_var"], j + 1)
                    nc.scalar.activation(hln[:, :], hvar[:, :], ACT.Ln, scale=1.0 / HD, bias=st.eps[:, 0:1]
                                         ).then_inc(sem["qk_rstd"], 1)
                    act.wait_ge(sem["qk_rstd"], 2 * j + 1)
                    nc.scalar.activation(hrstd[:, :], hln[:, :], ACT.Exp, scale=-0.5).then_inc(sem["qk_rstd"], 1)

                def keep_qk(j):
                    for n, dst in enumerate((qT, kT)):
                        act.wait_ge(sem["qkT_psum"], 2 * j + n + 1)
                        nc.scalar.activation(dst[:, :, j * P:(j + 1) * P],
                                             st.ps[:, 6 + n, :].rearrange("p (k t) -> p k t", k=KC), ACT.Identity,
                                             bias=st.head_ln[:, 1:2], scale=st.head_ln[:, 0:1]
                                             ).then_inc(sem["qkT_ready"], 1)

                scale(0)
                scale(1)
                for j in range(2, NT):
                    keep_qk(j - 2)
                    if j == NT - 1:
                        keep_v(0)
                    scale(j)
                keep_qk(NT - 2)
                for j in range(1, NT - 1):
                    keep_v(j)
                keep_qk(NT - 1)
                keep_v(NT - 1)
                for n in range(STEPS):
                    w = S - n % 4 * P
                    act.wait_ge(sem["qk_psum"], n + 1)
                    if n >= SQ:
                        act.wait_ge(sem["pv_done"], n - SQ + 1)
                    dst = sq[:, n % SQ, :].rearrange("p (q t) -> p q t", q=2)
                    b0 = 2 * (n % 2)
                    nc.scalar.activation(dst[:, :, 0:w], st.ps[:, b0:b0 + 2, 0:w], ACT.Square).then_inc(sem["squared"], 1)
                norm_scale(nc, st, sem, act)
                keep_transposed(nc, st, sem, act)

            @block.gpsimd
            def _(pool):
                for j in range(NT):
                    mine, rest = turned[j % 2], other[j % 2]
                    pool.wait_ge(sem["qk_rotated"], 3 * j + 3)
                    nc.gpsimd.tensor_tensor(mine, mine, rest, ALU.add).then_inc(sem["qk_rope"], 1)
                    pool.wait_ge(sem["qk_rope"], j + 1)
                    pool.wait_ge(sem["qk_mean"], j + 1)
                    nc.gpsimd.tensor_tensor(by_head(rest, NH2), by_head(mine, NH2),
                                            hmean[:, :].unsqueeze(2).to_broadcast([P, NH2, HD]), ALU.add
                                            ).then_inc(sem["qk_centred"], 1)
                for n in range(STEPS):
                    pool.wait_ge(sem["squared"], n + 1)
                    diag = sq[:, n % SQ, :].rearrange("p (q t) -> p q t", q=2)[:, :, 0:P]
                    nc.gpsimd.affine_select(out=diag, in_=diag, compare_op=ALU.is_ge, fill=0.0, base=0,
                                            pattern=[[0, 2], [1, P]], channel_multiplier=-1).then_inc(sem["masked"], 1)

            @block.vector
            def _(dve):
                def rotate(j):
                    dve.wait_ge(sem["qk_rows"], 2 * j + 2)
                    if j >= 2:
                        dve.wait_ge(sem["qkT_psum"], 2 * (j - 1))
                    qk = st.ps[:, 2 * (j % 2):2 * (j % 2) + 2, :].rearrange("p n (h d) -> p (n h) d", h=HEADS)
                    cos = st.cos[:, j, :].unsqueeze(1).to_broadcast([P, NH2, HD])
                    sin = st.sin[:, j, :].unsqueeze(1).to_broadcast([P, NH2, HALF])
                    msin = st.msin[:, j, :].unsqueeze(1).to_broadcast([P, NH2, HALF])
                    cosines, sines = by_head(turned[j % 2], NH2), by_head(other[j % 2], NH2)
                    nc.vector.tensor_tensor(cosines, qk, cos, ALU.mult).then_inc(sem["qk_rotated"], 1)
                    nc.vector.tensor_tensor(sines[:, :, 0:HALF], qk[:, :, HALF:HD], msin, ALU.mult
                                            ).then_inc(sem["qk_rotated"], 1)
                    nc.vector.tensor_tensor(sines[:, :, HALF:HD], qk[:, :, 0:HALF], sin, ALU.mult
                                            ).then_inc(sem["qk_rotated"], 1)

                def mean(j):
                    dve.wait_ge(sem["qk_rope"], j + 1)
                    nc.vector.tensor_reduce(hsum[:, :], by_head(turned[j % 2], NH2), AX_X, ALU.add
                                            ).then_inc(sem["qk_sum"], 1)
                    dve.wait_ge(sem["qk_sum"], j + 1)
                    nc.vector.tensor_scalar(hmean[:, :], hsum[:, :], -1.0 / HD, None, ALU.mult).then_inc(sem["qk_mean"], 1)

                def variance(j):
                    dve.wait_ge(sem["qk_square"], j + 1)
                    nc.vector.tensor_reduce(hvar[:, :], by_head(turned[j % 2], NH2), AX_X, ALU.add
                                            ).then_inc(sem["qk_var"], 1)

                def normalise(j):
                    dve.wait_ge(sem["qk_rstd"], 2 * j + 2)
                    rows = by_head(other[j % 2], NH2)
                    nc.vector.tensor_tensor(rows, rows, hrstd[:, :].unsqueeze(2).to_broadcast([P, NH2, HD]), ALU.mult
                                            ).then_inc(sem["qk_normed"], 1)

                rotate(0)
                mean(0)
                rotate(1)
                for j in range(1, NT + 1):
                    variance(j - 1)
                    if j < NT:
                        mean(j)
                    normalise(j - 1)
                    if j + 1 < NT:
                        rotate(j + 1)
                for n in range(STEPS):
                    w = S - n % 4 * P
                    dve.wait_ge(sem["masked"], n + 1)
                    part = sq[:, n % SQ, :].rearrange("p (q t) -> p q t", q=2)[:, :, 0:w]
                    nc.vector.tensor_tensor(part, part, part, ALU.mult).then_inc(sem["weighed"], 1)
                    if n >= 8 and 2 <= n % 8 < 2 + NT:
                        attended(nc, st, sem, dve, oT, rden, n // 8 * 8, n // 8 - 1, n % 8 - 2)
                for j in range(NT):
                    attended(nc, st, sem, dve, oT, rden, STEPS, KC - 1, j)

                def row(j):
                    dve.wait_ge(sem["out_psum"], j + 1)
                    nc.vector.tensor_tensor(st.r[:, j, :], st.x[:, j, :], st.ps[:, j, :], ALU.add
                                            ).then_inc(sem["row_ready"], 1)
                norm_rows(nc, st, sem, dve, row)
        run_pass(nc, body)


def softmax_pass(nc, st, sem, T, b):
    HALF = HD // 2
    KVH = CTX // HD
    SCALE = float(HD) ** -0.5
    with ExitStack() as ctx:
        sb = lambda name, shape, dt=F32: ctx.enter_context(nc.sbuf_tensor(name, shape, dt))
        kT = sb("kT2", [P, KVH, S])
        qT = sb("qT2", [P, KC, S])
        ssum = sb("ssum", [P, 2 * NT])
        sln = sb("sln", [P, 2 * NT])
        srstd = sb("srstd", [P, 2 * NT])
        pr = sb("pr", [P, 3, S])
        pT = sb("pT", [P, 2, NT, S])
        kn, kt1, kt2 = ([pT[:, 0, 2 * p, n * CTX:(n + 1) * CTX] for p in range(2)] for n in range(3))
        krep = [pT[:, 0, 2 * p + 1, :].rearrange("p (g r d) -> p g r d", g=KVH, r=HG) for p in range(2)]
        qn, t1, t2, qr = ((pT[:, 1, n, :], st.r[:, n, :]) for n in range(4))
        nmx = sb("nmx", [P, 4])
        nbias = sb("nbias", [P, 4])
        rden = sb("rden2", [P, 2, P])
        oT = qT
        NSTEP = HEADS * NT

        def body(block):
            @block.tensor
            def _(pe):
                for j in range(NT):
                    bank = 4 + 2 * (j % 2)
                    pe.wait_ge(sem["krep_ready"], j + 1)
                    if j >= 2:
                        pe.wait_ge(sem["qkT_ready"], 2 * (j - 1))
                    for g in range(KVH):
                        last = nc.tensor.transpose(st.ps[:, bank, g * P:(g + 1) * P],
                                                   krep[j % 2][:, g, :, :].rearrange("p r d -> p (r d)"), st.ident[:, :])
                    last.then_inc(sem["qkT_psum"], 1)
                    pe.wait_ge(sem["q_rope"], j + 1)
                    for k in range(KC):
                        last = nc.tensor.transpose(st.ps[:, bank + 1, k * P:(k + 1) * P],
                                                   qr[j % 2][:, k * P:(k + 1) * P], st.ident[:, :])
                    last.then_inc(sem["qkT_psum"], 1)
                pe.wait_ge(sem["qkT_ready"], 2 * NT)

                def score(n):
                    head, j = n // NT, n % NT
                    g, hh = head // HG, head % HG
                    part = slice(hh * HD, (hh + 1) * HD)
                    w = (j + 1) * P
                    if n >= 2:
                        pe.wait_ge(sem["exped"], n - 1)
                    nc.tensor.matmul(st.ps[:, n % 2, 0:w], qT[part, g, j * P:(j + 1) * P], kT[part, g, 0:w],
                                     start=True, stop=False, tile_position=(hh * HD, 0))
                    nc.tensor.matmul(st.ps[:, n % 2, j * P:w], st.ident_b[:, :], st.causal_b[:, :],
                                     start=False, stop=True).then_inc(sem["qk_psum"], 1)

                def turn(n):
                    j = n % NT
                    pe.wait_ge(sem["exped"], n + 1)
                    if n >= 2:
                        pe.wait_ge(sem["pT_ready"], n - 1)
                    for i in range(j + 1):
                        last = nc.tensor.transpose(st.ps[:, 2 + n % 2, i * P:(i + 1) * P],
                                                   pr[:, n % 3, i * P:(i + 1) * P], st.ident[:, :])
                    last.then_inc(sem["pT_psum"], 1)

                def weigh(head):
                    g, hh = head // HG, head % HG
                    part = slice(hh * HD, (hh + 1) * HD)
                    pe.wait_ge(sem["pT_ready"], NT * (head + 1))
                    if hh == 0 and g >= 2:
                        pe.wait_ge(sem["o_ready"], NT * (g - 1))
                    for i in range(NT):
                        a = pT[:, head % 2, i, i * P:S]
                        nc.tensor.matmul(st.ps[part, 4 + 2 * (g % 2), i * P:S], st.ctx[:, i, g * HD:(g + 1) * HD], a,
                                         start=(i == 0), stop=(i == NT - 1), tile_position=(0, hh * HD))
                        last = nc.tensor.matmul(st.ps[part, 5 + 2 * (g % 2), i * P:S], st.ones[:, 0:HD], a,
                                                start=(i == 0), stop=(i == NT - 1), tile_position=(0, hh * HD))
                    last.then_inc(sem["pv_done"], 1)

                score(0)
                for n in range(NSTEP):
                    if n + 1 < NSTEP:
                        score(n + 1)
                    turn(n)
                    if n % NT == 1 and n > NT:
                        weigh(n // NT - 1)
                weigh(HEADS - 1)
                project_attended(nc, st, sem, pe, oT, st.w_oxatt)
                transpose_rows(nc, st, sem, pe)

            @block.scalar
            def _(act):
                load_log_exp(nc)
                for j in range(NT):
                    two = slice(2 * j, 2 * j + 2)
                    nc.scalar.activation(qT[:, j, 0:CTX], st.ctx[:, j, :], ACT.Square, scale=float(CTX) ** -0.5,
                                         accum_out=ssum[:, 2 * j:2 * j + 1]).then_inc(sem["rms_sum"], 1)
                    nc.scalar.activation(kT[:, j, :], st.x[:, j, :], ACT.Square, scale=float(E) ** -0.5,
                                         accum_out=ssum[:, 2 * j + 1:2 * j + 2]).then_inc(sem["rms_sum"], 1)
                    act.wait_ge(sem["rms_sum"], 2 * j + 2)
                    nc.scalar.activation(sln[:, two], ssum[:, two], ACT.Ln, bias=st.eps[:, 0:1]).then_inc(sem["rms_rstd"], 1)
                    act.wait_ge(sem["rms_rstd"], 2 * j + 1)
                    nc.scalar.activation(srstd[:, two], sln[:, two], ACT.Exp, scale=-0.5).then_inc(sem["rms_rstd"], 1)

                def repeat(j):
                    act.wait_ge(sem["k_rope"], j + 1)
                    if j >= 2:
                        act.wait_ge(sem["qkT_psum"], 2 * (j - 2) + 1)
                    nc.scalar.activation(krep[j % 2], by_head(kn[j % 2], KVH).unsqueeze(2).to_broadcast([P, KVH, HG, HD]),
                                         ACT.Copy).then_inc(sem["krep_ready"], 1)

                def keep_qk(j):
                    for n, dst in enumerate((kT, qT)):
                        act.wait_ge(sem["qkT_psum"], 2 * j + n + 1)
                        nc.scalar.activation(dst[:, :, j * P:(j + 1) * P],
                                             st.ps[:, 4 + 2 * (j % 2) + n, :].rearrange("p (k t) -> p k t", k=KC), ACT.Copy
                                             ).then_inc(sem["qkT_ready"], 1)

                repeat(0)
                for j in range(1, NT):
                    repeat(j)
                    keep_qk(j - 1)
                keep_qk(NT - 1)
                for n in range(NSTEP):
                    w = (n % NT + 1) * P
                    act.wait_ge(sem["bias_ready"], n + 1)
                    if n >= 3:
                        act.wait_ge(sem["pT_psum"], n - 2)
                    nc.scalar.activation(pr[:, n % 3, 0:w], st.ps[:, n % 2, 0:w], ACT.Exp, scale=SCALE,
                                         bias=nbias[:, n % 4:n % 4 + 1]).then_inc(sem["exped"], 1)
                norm_scale(nc, st, sem, act)
                keep_transposed(nc, st, sem, act)

            @block.gpsimd
            def _(pool):
                for j in range(NT):
                    p = j % 2
                    pool.wait_ge(sem["k_turned"], 3 * j + 3)
                    nc.gpsimd.tensor_tensor(kn[p], kt1[p], kt2[p], ALU.add).then_inc(sem["k_rope"], 1)
                    pool.wait_ge(sem["q_turned"], 3 * j + 3)
                    if j >= 2:
                        pool.wait_ge(sem["qkT_psum"], 2 * (j - 2) + 2)
                    nc.gpsimd.tensor_tensor(qr[p], t1[p], t2[p], ALU.add).then_inc(sem["q_rope"], 1)

            @block.vector
            def _(dve):
                def rope(src, a, c, heads, sems, j):
                    cos = st.cos[:, j, :].unsqueeze(1).to_broadcast([P, heads, HD])
                    sin = st.sin[:, j, :].unsqueeze(1).to_broadcast([P, heads, HALF])
                    msin = st.msin[:, j, :].unsqueeze(1).to_broadcast([P, heads, HALF])
                    x, y, z = by_head(src, heads), by_head(a, heads), by_head(c, heads)
                    nc.vector.tensor_tensor(y, x, cos, ALU.mult).then_inc(sems, 1)
                    nc.vector.tensor_tensor(z[:, :, 0:HALF], x[:, :, HALF:HD], msin, ALU.mult).then_inc(sems, 1)
                    nc.vector.tensor_tensor(z[:, :, HALF:HD], x[:, :, 0:HALF], sin, ALU.mult).then_inc(sems, 1)

                for j in range(NT):
                    p = j % 2
                    dve.wait_ge(sem["rms_rstd"], 2 * j + 2)
                    if j >= 2:
                        dve.wait_ge(sem["krep_ready"], j - 1)
                        dve.wait_ge(sem["q_rope"], j - 1)
                    nc.vector.scalar_tensor_tensor(kn[p], st.ctx[:, j, :], srstd[:, 2 * j:2 * j + 1], st.k_norm[:, :],
                                                   ALU.mult, ALU.mult).then_inc(sem["rms_done"], 1)
                    nc.vector.scalar_tensor_tensor(qn[p], st.x[:, j, :], srstd[:, 2 * j + 1:2 * j + 2],
                                                   st.q_norm[:, :], ALU.mult, ALU.mult).then_inc(sem["rms_done"], 1)
                    dve.wait_ge(sem["rms_done"], 2 * j + 2)
                    rope(kn[p], kt1[p], kt2[p], KVH, sem["k_turned"], j)
                    rope(qn[p], t1[p], t2[p], HEADS, sem["q_turned"], j)

                def row_max(n):
                    w = (n % NT + 1) * P
                    dve.wait_ge(sem["qk_psum"], n + 1)
                    if n >= 4:
                        dve.wait_ge(sem["exped"], n - 3)
                    nc.vector.tensor_reduce(nmx[:, n % 4:n % 4 + 1], st.ps[:, n % 2, 0:w], AX_X, ALU.max, negate=True
                                            ).then_inc(sem["max_ready"], 1)
                    dve.wait_ge(sem["max_ready"], n + 1)
                    nc.vector.tensor_scalar(nbias[:, n % 4:n % 4 + 1], nmx[:, n % 4:n % 4 + 1], SCALE, None, ALU.mult
                                            ).then_inc(sem["bias_ready"], 1)

                def keep(n):
                    head, j = n // NT, n % NT
                    dve.wait_ge(sem["pT_psum"], n + 1)
                    if head >= 2 and j == 0:
                        dve.wait_ge(sem["pv_done"], head - 1)
                    nc.vector.tensor_copy(pT[:, head % 2, 0:j + 1, j * P:(j + 1) * P],
                                          st.ps[:, 2 + n % 2, 0:(j + 1) * P].rearrange("p (i t) -> p i t", t=P)
                                          ).then_inc(sem["pT_ready"], 1)

                row_max(0)
                for n in range(NSTEP):
                    if n + 1 < NSTEP:
                        row_max(n + 1)
                    keep(n)
                    if n >= NT * HG and 3 <= n % (NT * HG) < 3 + NT:
                        g = n // (NT * HG) - 1
                        attended(nc, st, sem, dve, oT, rden, HG * (g + 1), g, n % (NT * HG) - 3)
                for j in range(NT):
                    attended(nc, st, sem, dve, oT, rden, HEADS, KC - 1, j)

                def row(j):
                    dve.wait_ge(sem["out_psum"], j + 1)
                    nc.vector.tensor_tensor(st.r[:, j, :], st.x[:, j, :], st.ps[:, j, :], ALU.add
                                            ).then_inc(sem["row_ready"], 1)
                norm_rows(nc, st, sem, dve, row)

            @block.sync
            def _(sp):
                sp.wait_ge(sem["x_ready"], NT)
                sp.dma_start(T["x5"][bass.ds(b, 1), :, :].rearrange("a (j p) d -> p (a j) d", p=P), st.x[:, :, :]
                             ).then_inc(sem["rows_stored"], 16)
                sp.wait_ge(sem["xt_ready"], NT)
                sp.dma_start(T["x5T"][bass.ds(b, 1), :, :].rearrange("a (k p) t -> p (a k) t", p=P), st.xT[:, :, :]
                             ).then_inc(sem["rows_stored"], 16)
        run_pass(nc, body)


def signals(nc, ctx, names):
    return {n: ctx.enter_context(nc.semaphore(n)) for n in names}


def cleared_signals(nc, ctx, names):
    sem = signals(nc, ctx, names)
    nums = [h.num for h in sem.values()]
    assert nums == list(range(nums[0], nums[0] + len(nums))), nums
    sem["all"] = range(nums[0], nums[-1] + 1)
    return sem


LAYER_SIGNALS = """x_loaded xT_loaded ctx_loaded row_ready stats_ready var_ready rstd_ready x_ready xt_psum xt_ready
xp_psum xp_ready z_psum soft delta_ready spread_psum spread_copied product scanned own_product summed sums_ready affine_loaded bias_loaded biased residual y_psum y_ready
out_psum kvT_psum kvT_ready kv_psum kv_ready mix_psum mix_ready sim_psum sim_stats sim_var sim_rstd
sim_gamma sim_affine sim_max sim_exp sim_recip score_psum score_ready choice h0_psum h0_ready h1_psum
h1_ready half_row qk_rows v_rows v_ready qk_rotated qk_rope qk_sum qk_mean qk_centred qk_square qk_var qk_rstd qk_normed
qkT_psum qkT_ready qk_psum squared masked weighed pv_done den_ready o_ready rms_sum rms_rstd rms_done k_turned
k_rope krep_ready q_turned q_rope max_ready bias_ready exped pT_psum pT_ready stored""".split()


LASTING_SIGNALS = "weights_loaded later_loaded made rows_stored".split()


def clear(nc, sem, block):
    @block.sync
    def _(sp):
        sp.sem_clear(sem["all"])


def layers(nc, T, upto=5):
    with ExitStack() as ctx:
        sb = lambda name, shape, dt=F32: ctx.enter_context(nc.sbuf_tensor(name, shape, dt))
        st = Held()
        sem = cleared_signals(nc, ctx, LAYER_SIGNALS + LASTING_SIGNALS)
        lasting = range(sem["all"][-1] + 1 - len(LASTING_SIGNALS), sem["all"][-1] + 1)
        sem["all"] = range(sem["all"][0], lasting[0])
        st.ps = ctx.enter_context(nc.psum_tensor("ps", [P, 8, 512], F32))
        loads = []

        def held(name, shape, src):
            t = sb(name, shape)
            loads.append((name, t[(slice(None),) * len(shape)], src))
            return t

        weights = lambda a: a.rearrange("(k p) n -> p k n", p=P)
        st.w_in = held("w_in", [P, KC, E], weights(T["w_in"]))
        st.w_b = held("w_b", [P, KC, STATE], weights(T["w_b"]))
        st.w_c = held("w_c", [P, E], T["w_c"])
        st.w_o = held("w_o", [P, KC, E], weights(T["w_o"]))
        st.w_k = held("w_k", [P, CTX], T["w_k"])
        st.w_g = held("w_g", [P, KC, 2], weights(T["w_g"]))
        st.w_0a = held("w_0a", [P, KC, FF], weights(T["w_0a"]))
        st.w_1a = held("w_1a", [P, KC, FF], weights(T["w_1a"]))
        st.w_0b = held("w_0b", [P, NF, E], weights(T["w_0b"]))
        st.w_1b = held("w_1b", [P, NF, E], weights(T["w_1b"]))
        st.w_qkv = held("w_qkv", [P, KC, 3 * E], weights(T["w_qkv"]))
        st.w_oatt = held("w_oatt", [P, KC, E], weights(T["w_oatt"]))
        st.w_oxatt = held("w_oxatt", [P, KC, E], weights(T["w_oxatt"]))
        st.bias_rows = held("bias_rows", [P, E], T["bias_rows"])
        st.b_in = held("b_in", [P, KC], T["b_in"])
        st.d_param = held("d_param", [P, KC], T["d_param"])
        st.b_0a = held("b_0a", [P, NF], T["b_0a"])
        st.b_1a = held("b_1a", [P, NF], T["b_1a"])
        st.b_k = held("b_k", [P, 1], T["b_k"])
        st.head_ln = held("head_ln", [P, 2], T["head_ln"])
        a_in = held("a_in", [P, KC, STATE], T["a_in"])
        st.q_norm = held("q_norm", [P, E], T["q_norm"].partition_broadcast(P))
        st.k_norm = held("k_norm", [P, CTX], T["k_norm"].partition_broadcast(P))
        st.ident = held("ident", [P, P], T["ident"])
        st.ones_at = held("ones_at", [P, 64], T["ones_at"])
        st.cos = held("cos", [P, NT, HD], T["cos"])
        st.sin = held("sin", [P, NT, HD // 2], T["sin"])
        st.msin = held("msin", [P, NT, HD // 2], T["msin"])
        st.ones = sb("ones", [P, P])
        st.one = sb("one", [P, 1])
        st.zeros = sb("zeros", [P, P])
        st.eps = sb("eps", [P, 2])
        st.ident_b = sb("ident_b", [P, P], BF16)
        st.causal_b = sb("causal_b", [P, P], BF16)
        st.decay = sb("decay", [P, KC, STATE])
        st.x = sb("x_rows", [P, NT, E])
        st.xT = sb("x_rowsT", [P, KC, S])
        st.r = sb("r_rows", [P, NT, E])
        causal, a_exp = st.r[:, 0, 0:P], st.r[:, 1, 0:KC * STATE].rearrange("p (k n) -> p k n", k=KC)
        loads.append(("causal", causal, T["causal"]))
        st.xT_in = sb("x_inT", [P, KC, S])
        st.ctx = sb("ctx_rows", [P, NT, CTX])
        st.ctxT = sb("ctx_T", [P, S])
        st.stats = sb("stats", [P, NT, 6])
        st.meanvar = sb("meanvar", [P, NT, 2])
        st.lnvar = sb("lnvar", [P, NT])
        st.rstd = sb("rstd", [P, NT])

        early_names = ("w_in", "w_b", "w_c", "w_o", "bias_rows", "b_in", "d_param", "a_in", "ident", "causal", "ones_at")
        early = [(t, src) for name, t, src in loads if name in early_names]
        rest = [(t, src) for name, t, src in loads if name not in early_names]
        st.later = len(rest)
        with nc.Block() as block:
            @block.sync
            def _(sp):
                sp.sem_inc(sem["rows_stored"], 32)
                load_transposed(nc, st, T, 0, sp, sem["weights_loaded"])
                for t, src in early:
                    sp.dma_start(t, src).then_inc(sem["weights_loaded"], 16)
                for t, src in rest:
                    sp.dma_start(t, src).then_inc(sem["later_loaded"], 16)
                sp.wait_ge(sem["weights_loaded"], 16 * (1 + len(early)))

            @block.scalar
            def _(act):
                load_log_exp(nc)
                act.wait_ge(sem["weights_loaded"], 16 * (1 + len(early)))
                nc.scalar.activation(a_exp[:, :, :], a_in[:, :, :], ACT.Exp, scale=-1.0).then_inc(sem["made"], 1)
                nc.scalar.activation(st.ident_b[:, :], st.ident[:, :], ACT.Copy)
                nc.scalar.activation(st.causal_b[:, :], causal, ACT.Copy)

            @block.vector
            def _(dve):
                nc.vector.memset(st.ones[:, :], 1.0)
                nc.vector.memset(st.one[:, :], 1.0)
                nc.vector.memset(st.zeros[:, :], 0.0)
                nc.vector.memset(st.eps[:, 0:1], LN_EPS)
                nc.vector.memset(st.eps[:, 1:2], SIM_EPS)
                dve.wait_ge(sem["made"], 1)
                nc.vector.tensor_scalar(a_exp[:, :, :], a_exp[:, :, :], 1.0, None, ALU.add).then_inc(sem["made"], 1)
                dve.wait_ge(sem["made"], 2)
                nc.vector.reciprocal(st.decay[:, :, :], a_exp[:, :, :])

        with nc.Fori(0, NB) as b:
            def again():
                with nc.Block() as block:
                    clear(nc, sem, block)
            recurrence_pass(nc, st, sem, T, b)
            again()
            if upto >= 2:
                similarity_pass(nc, st, sem, T)
                again()
            if upto >= 3:
                two_expert_pass(nc, st, sem, T, b)
                again()
            if upto >= 4:
                polynomial_pass(nc, st, sem)
                again()
            if upto >= 5:
                softmax_pass(nc, st, sem, T, b)
                again()
            else:
                with nc.Block() as block:
                    @block.sync
                    def _(sp):
                        sp.dma_start(T["x5"][bass.ds(b, 1), :, :].rearrange("a (j p) d -> p (a j) d", p=P), st.x[:, :, :]
                                     ).then_inc(sem["rows_stored"], 32)
                again()
        with nc.Block() as block:
            @block.sync
            def _(sp):
                sp.wait_ge(sem["rows_stored"], 32 + 32 * NB)
        with nc.Block() as block:
            @block.sync
            def _(sp):
                sp.sem_clear(lasting)


DISPATCH_SIGNALS = """x5T_loaded x5_loaded const_loaded shared_loaded logits_psum logits_ready top_ready index_ready
less_max exp_top top_sum top_recip weight_ready index_real onehot chosen prefix_psum step_ready
tiles_real tiles_int tiles_shift tiles_ready ends_ready starts_ready base_ready pos_part pos_ready picked slot_real
slot_ready passed passed_sum table_part table_psum expert_ready scattered gate_psum up_psum
silu_ready hidden_ready down_psum shared_ready ones_made""".split()


def dispatch_pass(nc, T, M):
    with ExitStack() as ctx:
        sb = lambda name, shape, dt=F32: ctx.enter_context(nc.sbuf_tensor(name, shape, dt))
        sem = signals(nc, ctx, DISPATCH_SIGNALS)
        ps = ctx.enter_context(nc.psum_tensor("ps_dispatch", [P, 8, 512], F32))
        xT = sb("x5T_all", [P, KC, TOK])
        x = sb("x5_all", [P, TT, E])
        router = sb("router", [P, KC, EXPERTS])
        before = sb("before", [P, P])
        iota = sb("iota", [P, EXPERTS])
        tile_no = sb("tile_no", [P, 3])
        ident = sb("ident_d", [P, P])
        ones = sb("ones_d", [P, P])
        ws_gate = sb("ws_gate", [P, KC, FF])
        ws_up = sb("ws_up", [P, KC, FF])
        ws_down = sb("ws_down", [P, NF, E])
        logits = sb("logits", [P, TT, EXPERTS])
        top = sb("top", [P, TT, 8])
        index = sb("index", [P, TT, 8], U32)
        index_f = sb("index_f", [P, TT, 8])
        e_top = sb("e_top", [P, TT, TOP])
        e_sum = sb("e_sum", [P, TT])
        onehot = sb("onehot", [P, TOP, TT, EXPERTS])
        chosen = sb("chosen", [P, 3, TT * EXPERTS])
        count = sb("count", [P, 2, TT, EXPERTS])
        pos = sb("pos", [P, TT, EXPERTS])
        picked = sb("picked", [P, 2, TT, EXPERTS])
        slot_f = sb("slot_f", [P, TT, TOP])
        need_f = sb("need_f", [P, EXPERTS])
        need_i = sb("need_i", [P, 2, EXPERTS], I32)
        need = sb("need", [P, EXPERTS])
        used = sb("used", [P, EXPERTS])
        ends = sb("ends", [P, EXPERTS])
        starts = sb("starts", [P, EXPERTS])
        base = sb("base", [P, EXPERTS])
        passed = sb("passed", [P, 4, EXPERTS])
        sums = sb("passed_sums", [P, 4])
        table = sb("table", [P, 4])
        gate = sb("gate", [P, 2, S])
        hidden = sb("hidden", [P, NF, S])
        x5T = T["x5T"].rearrange("b (k p) t -> b p k t", p=P)
        x5 = T["x5"].rearrange("b (j p) d -> b p j d", p=P)

        with nc.Block() as block:
            @block.sync
            def _(sp):
                for b in range(NB):
                    sp.dma_start(xT[:, :, b * S:(b + 1) * S], x5T[b]).then_inc(sem["x5T_loaded"], 16)
                consts = ((router[:, :, :], T["router"].rearrange("(k p) n -> p k n", p=P)), (before[:, :], T["before"]),
                          (iota[:, :], T["iota"]), (tile_no[:, :], T["tile_no"]), (ident[:, :], T["ident"]))
                for t, src in consts:
                    sp.dma_start(t, src).then_inc(sem["const_loaded"], 16)
                for b in range(NB):
                    sp.dma_start(x[:, b * NT:(b + 1) * NT, :], x5[b]).then_inc(sem["x5_loaded"], 16)
                for t, src in ((ws_gate, T["ws_gate"]), (ws_up, T["ws_up"]), (ws_down, T["ws_down"])):
                    sp.dma_start(t[:, :, :], src.rearrange("(k p) n -> p k n", p=P)).then_inc(sem["shared_loaded"], 16)
                sp.wait_ge(sem["shared_loaded"], 48)

            @block.tensor
            def _(pe):
                pe.wait_ge(sem["x5T_loaded"], 16 * NB)
                pe.wait_ge(sem["const_loaded"], 16 * 5)
                for i in range(TT):
                    for k in range(KC):
                        last = nc.tensor.matmul(ps[:, 0, i * EXPERTS:(i + 1) * EXPERTS], xT[:, k, i * P:(i + 1) * P],
                                                router[:, k, :], start=(k == 0), stop=(k == KC - 1))
                last.then_inc(sem["logits_psum"], 1)
                pe.wait_ge(sem["ones_made"], 1)
                pe.wait_ge(sem["chosen"], 3)
                nc.tensor.matmul(ps[:, 1, :], before[:, :], chosen[:, 2, :], start=True, stop=True)
                nc.tensor.matmul(ps[:, 2, :], ones[:, :], chosen[:, 2, :], start=True, stop=True
                                 ).then_inc(sem["prefix_psum"], 1)
                pe.wait_ge(sem["table_part"], 3)
                pe.wait_ge(sem["passed_sum"], 4)
                nc.tensor.transpose(ps[0:4, 3, 0:P], table[:, :], ident[:, :]).then_inc(sem["table_psum"], 1)
                pe.wait_ge(sem["shared_loaded"], 48)
                with pe.Fori(0, NB) as n:
                    block_T = xT[:, :, bass.ds(n * S, S)]
                    for f in range(NF):
                        pe.wait_ge(sem["hidden_ready"], n * NF + f + 1)
                        for w, bank, s in ((ws_gate, 4, sem["gate_psum"]), (ws_up, 6, sem["up_psum"])):
                            for k in range(KC):
                                last = nc.tensor.matmul(ps[:, bank + f % 2, :], w[:, k, f * P:(f + 1) * P],
                                                        block_T[:, k, :], start=(k == 0), stop=(k == KC - 1))
                            last.then_inc(s, 1)
                    pe.wait_ge(sem["hidden_ready"], n * NF + NF + 2)
                    for j in range(NT):
                        pe.wait_ge(sem["shared_ready"], n * NT + j + 1)
                        for f in range(NF):
                            last = nc.tensor.matmul(ps[:, j % 2, :], hidden[:, f, j * P:(j + 1) * P], ws_down[:, f, :],
                                                    start=(f == 0), stop=(f == NF - 1))
                        last.then_inc(sem["down_psum"], 1)

            @block.scalar
            def _(act):
                act.wait_ge(sem["less_max"], 1)
                nc.scalar.activation(e_top[:, :, :], e_top[:, :, :], ACT.Exp).then_inc(sem["exp_top"], 1)
                with act.Fori(0, NB) as n:
                    for f in range(NF):
                        act.wait_ge(sem["gate_psum"], n * NF + f + 1)
                        act.wait_ge(sem["hidden_ready"], n * NF + f + 1)
                        nc.scalar.activation(gate[:, f % 2, :], ps[:, 4 + f % 2, :], ACT.Silu
                                             ).then_inc(sem["silu_ready"], 1)

            @block.gpsimd
            def _(pool):
                nc.gpsimd.memset(ones[:, :], 1.0).then_inc(sem["ones_made"], 1)
                pool.wait_ge(sem["slot_ready"], 1)
                pool.wait_ge(sem["x5_loaded"], 16 * NB)
                for i in range(TT):
                    for k in range(TOP):
                        nc.gpsimd.indirect_dma_start(
                            T["expert_rows"], bass.IndirectOffsetOnAxis(ap=M.slots[:, i, k:k + 1], axis=0),
                            x[:, i, :], None).then_inc(sem["scattered"], 16)
                pool.wait_ge(sem["scattered"], 16 * TT * TOP)

            @block.vector
            def _(dve):
                flat3 = lambda t: t.rearrange("p i e -> p (i e)")
                dve.wait_ge(sem["logits_psum"], 1)
                nc.vector.tensor_copy(flat3(logits[:, :, :]), ps[:, 0, :]).then_inc(sem["logits_ready"], 1)
                dve.wait_ge(sem["logits_ready"], 1)
                for i in range(TT):
                    nc.vector.max(top[:, i, :], logits[:, i, :]).then_inc(sem["top_ready"], 1)
                dve.wait_ge(sem["top_ready"], TT)
                nc.vector.tensor_tensor(e_top[:, :, :], top[:, :, 0:TOP], top[:, :, 0:1].to_broadcast([P, TT, TOP]),
                                        ALU.subtract).then_inc(sem["less_max"], 1)
                for i in range(TT):
                    nc.vector.max_index(index[:, i, :], top[:, i, :], logits[:, i, :]).then_inc(sem["index_ready"], 1)
                dve.wait_ge(sem["index_ready"], TT)
                nc.vector.tensor_copy(index_f[:, :, :], index[:, :, :]).then_inc(sem["index_real"], 1)
                dve.wait_ge(sem["index_real"], 1)
                experts = iota[:, :].unsqueeze(1).to_broadcast([P, TT, EXPERTS])
                dve.wait_ge(sem["const_loaded"], 16 * 5)
                for k in range(TOP):
                    nc.vector.tensor_tensor(onehot[:, k, :, :], experts,
                                            index_f[:, :, k:k + 1].to_broadcast([P, TT, EXPERTS]), ALU.is_equal
                                            ).then_inc(sem["onehot"], 1)
                dve.wait_ge(sem["onehot"], TOP)
                for n in range(3):
                    before_n = onehot[:, 0, :, :] if n == 0 else chosen[:, n - 1, :].rearrange(
                        "p (i e) -> p i e", e=EXPERTS)
                    if n:
                        dve.wait_ge(sem["chosen"], n)
                    nc.vector.tensor_tensor(chosen[:, n, :].rearrange("p (i e) -> p i e", e=EXPERTS), before_n,
                                            onehot[:, n + 1, :, :], ALU.add).then_inc(sem["chosen"], 1)
                dve.wait_ge(sem["exp_top"], 1)
                nc.vector.tensor_reduce(e_sum[:, :], e_top[:, :, :], AX_X, ALU.add).then_inc(sem["top_sum"], 1)
                dve.wait_ge(sem["top_sum"], 1)
                nc.vector.reciprocal(e_sum[:, :], e_sum[:, :]).then_inc(sem["top_recip"], 1)
                dve.wait_ge(sem["top_recip"], 1)
                nc.vector.tensor_tensor(M.weights[:, :, :], e_top[:, :, :],
                                        e_sum[:, :].unsqueeze(2).to_broadcast([P, TT, TOP]), ALU.mult
                                        ).then_inc(sem["weight_ready"], 1)
                dve.wait_ge(sem["prefix_psum"], 1)
                nc.vector.tensor_copy(flat3(count[:, 0, :, :]), ps[:, 2, :]).then_inc(sem["step_ready"], 1)
                for n in range(4):
                    d = 1 << n
                    src, dst = count[:, n % 2, :, :], count[:, (n + 1) % 2, :, :]
                    dve.wait_ge(sem["step_ready"], 2 * n + 1)
                    nc.vector.tensor_tensor(dst[:, d:TT, :], src[:, d:TT, :], src[:, 0:TT - d, :], ALU.add
                                            ).then_inc(sem["step_ready"], 1)
                    nc.vector.tensor_copy(dst[:, 0:d, :], src[:, 0:d, :]).then_inc(sem["step_ready"], 1)
                dve.wait_ge(sem["step_ready"], 9)
                nc.vector.tensor_scalar(need_f[:, :], count[:, 0, TT - 1, :], float(P - 1), None, ALU.add
                                        ).then_inc(sem["tiles_real"], 1)
                dve.wait_ge(sem["tiles_real"], 1)
                nc.vector.tensor_copy(need_i[:, 0, :], need_f[:, :]).then_inc(sem["tiles_int"], 1)
                dve.wait_ge(sem["tiles_int"], 1)
                nc.vector.tensor_scalar(need_i[:, 1, :], need_i[:, 0, :], 7, None, ALU.arith_shift_right
                                        ).then_inc(sem["tiles_shift"], 1)
                dve.wait_ge(sem["tiles_shift"], 1)
                nc.vector.tensor_copy(need[:, :], need_i[:, 1, :]).then_inc(sem["tiles_ready"], 1)
                dve.wait_ge(sem["tiles_ready"], 1)
                dve.wait_ge(sem["ones_made"], 1)
                nc.vector.tensor_scalar(used[:, :], need[:, :], 0.0, None, ALU.is_gt).then_inc(sem["tiles_ready"], 1)
                nc.vector.tensor_tensor_scan(ends[:, :], ones[:, 0:EXPERTS], need[:, :], 0.0, ALU.mult, ALU.add
                                             ).then_inc(sem["ends_ready"], 1)
                dve.wait_ge(sem["ends_ready"], 1)
                nc.vector.tensor_tensor(starts[:, :], ends[:, :], need[:, :], ALU.subtract).then_inc(sem["starts_ready"], 1)
                dve.wait_ge(sem["starts_ready"], 1)
                nc.vector.tensor_scalar(base[:, :], starts[:, :], float(P), None, ALU.mult).then_inc(sem["base_ready"], 1)
                within = ps[:, 1, :].rearrange("p (i e) -> p i e", e=EXPERTS)
                nc.vector.tensor_copy(pos[:, 0, :], within[:, 0, :]).then_inc(sem["pos_part"], 1)
                nc.vector.tensor_tensor(pos[:, 1:TT, :], within[:, 1:TT, :], count[:, 0, 0:TT - 1, :], ALU.add
                                        ).then_inc(sem["pos_part"], 1)
                dve.wait_ge(sem["base_ready"], 1)
                dve.wait_ge(sem["pos_part"], 2)
                nc.vector.tensor_tensor(pos[:, :, :], pos[:, :, :],
                                        base[:, :].unsqueeze(1).to_broadcast([P, TT, EXPERTS]), ALU.add
                                        ).then_inc(sem["pos_ready"], 1)
                dve.wait_ge(sem["pos_ready"], 1)
                for k in range(TOP):
                    if k >= 2:
                        dve.wait_ge(sem["slot_real"], k - 1)
                    nc.vector.tensor_tensor(picked[:, k % 2, :, :], onehot[:, k, :, :], pos[:, :, :], ALU.mult
                                            ).then_inc(sem["picked"], 1)
                    dve.wait_ge(sem["picked"], k + 1)
                    nc.vector.tensor_reduce(slot_f[:, :, k], picked[:, k % 2, :, :], AX_X, ALU.add
                                            ).then_inc(sem["slot_real"], 1)
                dve.wait_ge(sem["slot_real"], TOP)
                nc.vector.tensor_copy(M.slots[:, :, :], slot_f[:, :, :]).then_inc(sem["slot_ready"], 1)
                dve.wait_ge(sem["tiles_ready"], 2)
                for n in range(2):
                    nc.vector.tensor_scalar(passed[:, n, :], ends[:, :], tile_no[:, n:n + 1], None, ALU.is_le
                                            ).then_inc(sem["passed"], 1)
                dve.wait_ge(sem["passed"], 2)
                for n in range(2):
                    nc.vector.tensor_tensor(passed[:, 2 + n, :], passed[:, n, :], used[:, :], ALU.mult
                                            ).then_inc(sem["passed"], 1)
                dve.wait_ge(sem["passed"], 4)
                nc.vector.tensor_reduce(sums[:, :], passed[:, :, :], AX_X, ALU.add).then_inc(sem["passed"], 1)
                dve.wait_ge(sem["passed"], 5)
                nc.vector.tensor_scalar(table[:, 0:1], sums[:, 0:1], float(EXPERTS - 1), None, ALU.min
                                        ).then_inc(sem["passed_sum"], 1)
                nc.vector.tensor_copy(table[:, 1:2], sums[:, 2:3]).then_inc(sem["passed_sum"], 1)
                nc.vector.tensor_tensor(table[:, 3:4], sums[:, 2:3], sums[:, 3:4], ALU.not_equal
                                        ).then_inc(sem["passed_sum"], 1)
                dve.wait_ge(sem["passed_sum"], 3)
                nc.vector.tensor_tensor(table[:, 2:3], table[:, 3:4], tile_no[:, 2:3], ALU.max
                                        ).then_inc(sem["passed_sum"], 1)
                nc.vector.tensor_copy(sums[:, 0:1], table[:, 3:4]).then_inc(sem["table_part"], 3)
                dve.wait_ge(sem["table_psum"], 1)
                nc.vector.tensor_copy(M.tile_info[:, :], ps[0:4, 3, 0:P]).then_inc(sem["expert_ready"], 1)
                dve.wait_ge(sem["expert_ready"], 1)
                nc.vector.tensor_scalar(M.ring_at[:, :], M.tile_info[:, :], WRING - 1, None, ALU.bitwise_and
                                        ).then_inc(sem["expert_ready"], 1)
                dve.sem_inc(sem["hidden_ready"], 2)
                dve.sem_inc(sem["shared_ready"], 2)
                dve.wait_ge(sem["x5_loaded"], 16 * NB)
                with dve.Fori(0, NB) as n:
                    for f in range(NF):
                        if f == 0:
                            dve.wait_ge(sem["shared_ready"], n * NT + 2)
                        dve.wait_ge(sem["silu_ready"], n * NF + f + 1)
                        dve.wait_ge(sem["up_psum"], n * NF + f + 1)
                        nc.vector.tensor_tensor(hidden[:, f, :], gate[:, f % 2, :], ps[:, 6 + f % 2, :], ALU.mult
                                                ).then_inc(sem["hidden_ready"], 1)
                    for j in range(NT):
                        dve.wait_ge(sem["down_psum"], n * NT + j + 1)
                        nc.vector.tensor_tensor(M.acc[:, bass.ds(n * NT + j, 1), :].rearrange("p a d -> p (a d)"),
                                                x[:, bass.ds(n * NT + j, 1), :].rearrange("p a d -> p (a d)"),
                                                ps[:, j % 2, :], ALU.add).then_inc(sem["shared_ready"], 1)


EXPERT_SIGNALS = """w_loaded row_loaded0 row_loaded1 row_turned rowT_ready gu_psum silu_done h_rows h_turned hT_ready
y_psum y_ready y_stored0 y_stored1 ident_loaded""".split()
PEEL = 4


def expert_pass(nc, T, M):
    with ExitStack() as ctx:
        sb = lambda name, shape, dt=F32: ctx.enter_context(nc.sbuf_tensor(name, shape, dt))
        sem = signals(nc, ctx, EXPERT_SIGNALS)
        ps = ctx.enter_context(nc.psum_tensor("ps_expert", [P, 8, 512], F32))
        ident = sb("ident_e", [P, P])
        w_gu = sb("w_gu", [P, WRING, KC, 2 * INNER])
        w_dn = sb("w_dn", [P, WRING, 2, E])
        rows = sb("rows", [P, 2, E])
        rowsT = sb("rowsT", [P, 2, KC, P])
        silu = sb("silu", [P, 2, INNER])
        h = sb("h_exp", [P, 2, INNER])
        hT = sb("hT_exp", [HALF_IN, 2, 2, P])
        y = sb("y_exp", [P, 2, E])
        row_loaded = (sem["row_loaded0"], sem["row_loaded1"])
        y_stored = (sem["y_stored0"], sem["y_stored1"])
        w_gate = T["w_gate"].rearrange("e (k p) n -> e p k n", p=P)
        w_up = T["w_up"].rearrange("e (k p) n -> e p k n", p=P)
        w_down = T["w_down"].rearrange("e (k p) n -> e p k n", p=HALF_IN)

        def steps(eng, step):
            for q in range(PEEL):
                step(q // 2, q % 2)
            with eng.Fori(PEEL // 2, (TILES - PEEL) // 2) as i:
                for p in range(2):
                    step(i, p)
            for q in range(TILES - PEEL, TILES):
                step(q // 2, q % 2)

        def after(i, p, d):
            at, parity = (p + d) // 2, (p + d) % 2
            if isinstance(i, int):
                q = 2 * i + p + d
                return (i + at, parity) if 0 <= q < TILES else None
            return i + at, parity

        def later(i, n):
            return not isinstance(i, int) or i >= n

        number = lambda i, p: 2 * i + p

        with nc.Block() as block:
            @block.sync
            def _(sp):
                sp.dma_start(ident[:, :], T["ident"]).then_inc(sem["ident_loaded"], 16)
                sp.wait_ge(sem["ident_loaded"], 16)

                def weights(i, p):
                    q = number(i, p)
                    expert = sp.value_load(M.tile_info[0:1, bass.ds(q, 1)], min_val=0, max_val=EXPERTS - 1)
                    at = sp.value_load(M.ring_at[1:2, bass.ds(q, 1)], min_val=0, max_val=WRING - 1)
                    fresh = sp.value_load(M.tile_info[2:3, bass.ds(q, 1)], min_val=0, max_val=1)
                    if later(i, WRING // 2):
                        sp.wait_ge(sem["y_psum"], q - WRING + 1)
                    if later(i, 1) or p:
                        sp.wait_ge(sem["w_loaded"], 48 * (q - 1) + 48)
                    new = fresh > 0
                    for src, lo in ((w_gate, 0), (w_up, INNER)):
                        sp.dma_start(w_gu[:, bass.ds(at, 1), :, lo:lo + INNER].rearrange("p a k n -> p (a k) n"),
                                     src[bass.ds(expert, 1), :, :, :].rearrange("a p k n -> p (a k) n"), cond=new
                                     ).then_inc(sem["w_loaded"], 16)
                    sp.dma_start(w_dn[0:HALF_IN, bass.ds(at, 1), :, :].rearrange("p a k n -> p (a k) n"),
                                 w_down[bass.ds(expert, 1), :, :, :].rearrange("a p k n -> p (a k) n"), cond=new
                                 ).then_inc(sem["w_loaded"], 16)
                steps(sp, weights)

            @block.tensor
            def _(pe):
                def ring(i, p):
                    return pe.value_load(M.ring_at[1:2, bass.ds(number(i, p), 1)], min_val=0, max_val=WRING - 1)

                def turn_rows(i, p):
                    pe.wait_ge(row_loaded[p], 16 * (i + 1))
                    if later(i, 1):
                        pe.wait_ge(sem["rowT_ready"], number(i, p) - 1)
                    for k in range(KC):
                        last = nc.tensor.transpose(ps[:, p, k * P:(k + 1) * P], rows[:, p, k * P:(k + 1) * P],
                                                   ident[:, :])
                    last.then_inc(sem["row_turned"], 1)

                def gate_up(i, p):
                    at = ring(i, p)
                    pe.wait_ge(sem["w_loaded"], 48 * (number(i, p) + 1))
                    pe.wait_ge(sem["rowT_ready"], number(i, p) + 1)
                    if later(i, 1):
                        pe.wait_ge(sem["h_rows"], number(i, p) - 1)
                    for k in range(KC):
                        last = nc.tensor.matmul(ps[:, 2 + p, 0:2 * INNER], rowsT[:, p, k, :],
                                                w_gu[:, bass.ds(at, 1), k, :].rearrange("p a n -> p (a n)"),
                                                start=(k == 0), stop=(k == KC - 1))
                    last.then_inc(sem["gu_psum"], 1)

                def turn_h(i, p):
                    pe.wait_ge(sem["h_rows"], number(i, p) + 1)
                    if later(i, 1):
                        pe.wait_ge(sem["hT_ready"], number(i, p) - 1)
                    for c in range(2):
                        last = nc.tensor.transpose(ps[0:HALF_IN, 4 + p, c * P:(c + 1) * P],
                                                   h[:, p, c * HALF_IN:(c + 1) * HALF_IN], ident[:, :])
                    last.then_inc(sem["h_turned"], 1)

                def down(i, p):
                    at = ring(i, p)
                    pe.wait_ge(sem["hT_ready"], number(i, p) + 1)
                    if later(i, 1):
                        pe.wait_ge(sem["y_ready"], number(i, p) - 1)
                    for c in range(2):
                        last = nc.tensor.matmul(ps[:, 6 + p, :], hT[:, p, c, :],
                                                w_dn[0:HALF_IN, bass.ds(at, 1), c, :].rearrange("p a n -> p (a n)"),
                                                start=(c == 0), stop=(c == 1))
                    last.then_inc(sem["y_psum"], 1)

                def step(i, p):
                    if after(i, p, -1):
                        down(*after(i, p, -1))
                    turn_h(i, p)
                    if after(i, p, 2):
                        turn_rows(*after(i, p, 2))
                    if after(i, p, 1):
                        gate_up(*after(i, p, 1))

                pe.wait_ge(sem["ident_loaded"], 16)
                turn_rows(0, 0)
                turn_rows(0, 1)
                gate_up(0, 0)
                steps(pe, step)
                down(TILES // 2 - 1, 1)

            @block.vector
            def _(dve):
                def keep_rows(i, p):
                    dve.wait_ge(sem["row_turned"], number(i, p) + 1)
                    if later(i, 1):
                        dve.wait_ge(sem["gu_psum"], number(i, p) - 1)
                    nc.vector.tensor_copy(rowsT[:, p, :, :], ps[:, p, :].rearrange("p (k t) -> p k t", k=KC)
                                          ).then_inc(sem["rowT_ready"], 1)

                def step(i, p):
                    dve.wait_ge(sem["silu_done"], number(i, p) + 1)
                    if later(i, 1):
                        dve.wait_ge(sem["h_turned"], number(i, p) - 1)
                    nc.vector.tensor_tensor(h[:, p, :], silu[:, p, :], ps[:, 2 + p, INNER:2 * INNER], ALU.mult
                                            ).then_inc(sem["h_rows"], 1)
                    dve.wait_ge(sem["h_turned"], number(i, p) + 1)
                    if later(i, 1):
                        dve.wait_ge(sem["y_psum"], number(i, p) - 1)
                    nc.vector.tensor_copy(hT[:, p, :, :], ps[0:HALF_IN, 4 + p, 0:2 * P].rearrange(
                        "p (c t) -> p c t", c=2)).then_inc(sem["hT_ready"], 1)
                    if after(i, p, 2):
                        keep_rows(*after(i, p, 2))

                keep_rows(0, 0)
                keep_rows(0, 1)
                steps(dve, step)

            @block.scalar
            def _(act):
                def out_rows(i, p):
                    act.wait_ge(sem["y_psum"], number(i, p) + 1)
                    if later(i, 1):
                        act.wait_ge(y_stored[p], 16 * i)
                    nc.scalar.activation(y[:, p, :], ps[:, 6 + p, :], ACT.Copy).then_inc(sem["y_ready"], 1)

                def step(i, p):
                    act.wait_ge(sem["gu_psum"], number(i, p) + 1)
                    if later(i, 1):
                        act.wait_ge(sem["h_rows"], number(i, p) - 1)
                    nc.scalar.activation(silu[:, p, :], ps[:, 2 + p, 0:INNER], ACT.Silu).then_inc(sem["silu_done"], 1)
                    if after(i, p, -1):
                        out_rows(*after(i, p, -1))
                steps(act, step)
                out_rows(TILES // 2 - 1, 1)

            @block.gpsimd
            def _(pool):
                def load(i, p):
                    if later(i, 1):
                        pool.wait_ge(sem["row_turned"], number(i, p) - 1)
                    pool.dma_start(rows[:, p, :], T["expert_rows"][bass.ds(number(i, p) * P, P), :]
                                   ).then_inc(row_loaded[p], 16)

                def store(i, p):
                    pool.wait_ge(sem["y_ready"], number(i, p) + 1)
                    pool.dma_start(T["expert_out"][bass.ds(number(i, p) * P, P), :], y[:, p, :]
                                   ).then_inc(y_stored[p], 16)

                def step(i, p):
                    if after(i, p, 3):
                        load(*after(i, p, 3))
                    if after(i, p, -1):
                        store(*after(i, p, -1))
                load(0, 0)
                load(0, 1)
                load(1, 0)
                steps(pool, step)
                store(TILES // 2 - 1, 1)
                for s in y_stored:
                    pool.wait_ge(s, 16 * (TILES // 2))


COMBINE_SIGNALS = """slots_now part_ready row_ready stats_ready var_ready rstd_ready x_ready out_stored
weights_now""".split()
AT_ONCE = 2


def combine_pass(nc, T, M, sem, gathered):
    tiles = AT_ONCE * NT
    with ExitStack() as ctx:
        sb = lambda name, shape, dt=F32: ctx.enter_context(nc.sbuf_tensor(name, shape, dt))
        st = Held()
        slots = sb("slots_b", [P, tiles, TOP], U32)
        weights = sb("weights_b", [P, tiles, TOP])
        got = sb("got", [P, tiles, TOP, E])
        part = sb("part", [P, 2, TOP - 1, E])
        st.r = sb("r_out", [P, tiles, E])
        st.x = sb("x_out", [P, tiles, E])
        st.stats = sb("stats_o", [P, tiles, 6])
        st.meanvar = sb("meanvar_o", [P, tiles, 2])
        st.lnvar = sb("lnvar_o", [P, tiles])
        st.rstd = sb("rstd_o", [P, tiles])
        st.eps = sb("eps_o", [P, 1])
        with nc.Block() as block:
            @block.vector
            def _(dve):
                nc.vector.memset(st.eps[:, :], LN_EPS)
        with nc.Fori(0, NB // AT_ONCE) as turn:
            with nc.Block() as block:
                @block.gpsimd
                def _(pool):
                    pool.wait_ge(sem["slots_now"], 1)
                    for j in range(tiles):
                        for k in range(TOP):
                            nc.gpsimd.indirect_dma_start(
                                got[:, j, k, :], None, T["expert_out"],
                                bass.IndirectOffsetOnAxis(ap=slots[:, j, k:k + 1], axis=0)
                                ).then_inc(gathered[j], 16)

                @block.vector
                def _(dve):
                    nc.vector.tensor_copy(slots[:, :, :], M.slots[:, bass.ds(turn * tiles, tiles), :]
                                          ).then_inc(sem["slots_now"], 1)
                    nc.vector.tensor_copy(weights[:, :, :], M.weights[:, bass.ds(turn * tiles, tiles), :]
                                          ).then_inc(sem["weights_now"], 1)
                    dve.wait_ge(sem["weights_now"], 1)

                    def row(j):
                        dve.wait_ge(gathered[j], (turn + 1) * (16 * TOP))
                        for k in range(TOP):
                            if k:
                                dve.wait_ge(sem["part_ready"], (TOP - 1) * j + k)
                                before = part[:, j % 2, k - 1, :]
                            else:
                                before = M.acc[:, bass.ds(turn * tiles + j, 1), :].rearrange("p a d -> p (a d)")
                            dst, s = ((part[:, j % 2, k, :], sem["part_ready"]) if k < TOP - 1
                                      else (st.r[:, j, :], sem["row_ready"]))
                            nc.vector.scalar_tensor_tensor(dst, got[:, j, k, :], weights[:, j, k:k + 1], before,
                                                           ALU.mult, ALU.add).then_inc(s, 1)
                    norm_rows(nc, st, sem, dve, row, tiles)

                @block.scalar
                def _(act):
                    load_log_exp(nc)
                    norm_scale(nc, st, sem, act, tiles)

                @block.sync
                def _(sp):
                    for n in range(AT_ONCE):
                        sp.wait_ge(sem["x_ready"], NT * (n + 1))
                        sp.dma_start(T["out"][bass.ds(turn * AT_ONCE + n, 1), :, :].rearrange(
                            "a (j p) d -> p (a j) d", p=P), st.x[:, n * NT:(n + 1) * NT, :]).then_inc(sem["out_stored"], 16)
                    sp.wait_ge(sem["out_stored"], 16 * AT_ONCE)
            with nc.Block() as block:
                clear(nc, sem, block)


def mixture(nc, T):
    with ExitStack() as ctx:
        M = Held()
        combine_sem = cleared_signals(nc, ctx, COMBINE_SIGNALS)
        gathered = [ctx.enter_context(nc.semaphore(f"gathered{j}")) for j in range(AT_ONCE * NT)]
        M.acc = ctx.enter_context(nc.sbuf_tensor("acc", [P, TT, E], F32))
        M.slots = ctx.enter_context(nc.sbuf_tensor("slots", [P, TT, TOP], U32))
        M.weights = ctx.enter_context(nc.sbuf_tensor("weights", [P, TT, TOP], F32))
        M.tile_info = ctx.enter_context(nc.sbuf_tensor("tile_info", [4, P], I32))
        M.ring_at = ctx.enter_context(nc.sbuf_tensor("ring_at", [4, P], I32))
        dispatch_pass(nc, T, M)
        expert_pass(nc, T, M)
        combine_pass(nc, T, M, combine_sem, gathered)


def program(nc, T):
    layers(nc, T)
    mixture(nc, T)


def layout(inputs):
    import numpy as np
    A = {k: np.asarray(v) for k, v in inputs.items()}
    flat = np.ascontiguousarray
    columns = lambda v, n: flat(v.reshape(n, P).T)
    t = np.arange(S, dtype=np.float32)
    inv_freq = (np.float32(1.0) / np.float32(10000.0) ** (np.arange(0, HD, 2, dtype=np.float32) / np.float32(HD))
                ).astype(np.float32)
    angle = (t[:, None] * inv_freq[None, :]).astype(np.float32)
    tiles = lambda a: flat(a.astype(np.float32).reshape(NT, P, -1).transpose(1, 0, 2))
    w_c = np.zeros((P, E), np.float32)
    for c in range(KC):
        w_c[32 * c:32 * c + STATE] = A["L0_attn_C_w"].T
    bias_rows = np.zeros((P, E), np.float32)
    for at, name in ((0, "L0_attn_proj_out_b"), (96, "L0_xattn_b_k")):
        bias_rows[at, :A[name].shape[0]] = A[name]
    ones_at = np.zeros((P, 64), np.float32)
    ones_at[:, 32] = 1.0
    rows = np.arange(P)
    return {
        "x": flat(A["x"]), "xT": flat(A["x"].transpose(0, 2, 1)),
        "ctx": flat(A["ctx_512"]), "ctxT": flat(A["ctx_512"].transpose(0, 2, 1)),
        "w_in": flat(A["L0_attn_proj_in_w"].T), "w_b": flat(A["L0_attn_B_w"].T), "w_c": w_c,
        "w_o": flat(A["L0_attn_proj_out_w"].T), "w_k": flat(A["L0_xattn_W_k"].T), "w_g": flat(A["L0_ffn_Wg"].T),
        "w_0a": flat(A["L0_ffn_W0a"].T), "w_1a": flat(A["L0_ffn_W1a"].T),
        "w_0b": flat(A["L0_ffn_W0b"].T), "w_1b": flat(A["L0_ffn_W1b"].T),
        "w_qkv": flat(A["L1_attn_w_qkv"]), "w_oatt": flat(A["L1_attn_w_out"]),
        "w_oxatt": flat(A["L1_xattn_w_out"].T), "bias_rows": bias_rows,
        "b_in": columns(A["L0_attn_proj_in_b"], KC), "d_param": columns(A["L0_attn_D_param"], KC),
        "b_0a": columns(A["L0_ffn_b0a"], NF), "b_1a": columns(A["L0_ffn_b1a"], NF),
        "b_0b": flat(A["L0_ffn_b0b"]), "b_1b": flat(A["L0_ffn_b1b"]),
        "b_k": columns(A["L0_xattn_b_k"], 1),
        "head_ln": flat(np.stack([np.tile(A["L1_attn_ln_scale"], HG), np.tile(A["L1_attn_ln_bias"], HG)], 1)),
        "a_in": flat(A["L0_attn_A"].reshape(KC, P, STATE).transpose(1, 0, 2)),
        "gamma": flat(A["L0_xattn_ln_gamma"]), "beta": flat(A["L0_xattn_ln_beta"]),
        "q_norm": flat(A["L1_xattn_q_norm_w"]), "k_norm": flat(A["L1_xattn_k_norm_w"]),
        "ident": np.eye(P, dtype=np.float32),
        "causal": np.where(rows[None, :] > rows[:, None], np.float32(-1e30), np.float32(0.0)),
        "ones_at": ones_at,
        "router": flat(A["L1_ffn_router_w"]), "w_gate": flat(A["L1_ffn_w_gate"]), "w_up": flat(A["L1_ffn_w_up"]),
        "w_down": flat(A["L1_ffn_w_down"]), "ws_gate": flat(A["L1_ffn_ws_gate"]), "ws_up": flat(A["L1_ffn_ws_up"]),
        "ws_down": flat(A["L1_ffn_ws_down"]),
        "before": (rows[:, None] < rows[None, :]).astype(np.float32),
        "iota": np.tile(np.arange(EXPERTS, dtype=np.float32), (P, 1)),
        "tile_no": np.stack([rows, rows - 1, rows == 0], 1).astype(np.float32),
        "cos": tiles(np.concatenate([np.cos(angle), np.cos(angle)], 1)),
        "sin": tiles(np.sin(angle)), "msin": tiles(-np.sin(angle)),
    }


def kernel(**inputs):
    import numpy as _np
    import concourse.bacc as _bacc
    from concourse import mybir as _mybir
    from concourse.bass_utils import run_bass_kernel_spmd as _run

    nc = _bacc.Bacc("TRN2", target_bir_lowering=False, num_devices=1)
    arrays, tensors = {}, {}
    for name, a in layout(inputs).items():
        arrays[f"in_{name}"] = a
        tensors[name] = nc.dram_tensor(f"in_{name}", a.shape, _mybir.dt.from_np(a.dtype), kind="ExternalInput").ap()
    tensors["out"] = nc.dram_tensor("out", (NB, S, E), F32, kind="ExternalOutput").ap()
    for name, shape in (("x5", (NB, S, E)), ("x5T", (NB, E, S)), ("expert_rows", (SLOTS, E)), ("expert_out", (SLOTS, E))):
        tensors[name] = nc.dram_tensor(name, shape, F32, kind="Internal").ap()
    program(nc, tensors)
    r = _run(nc, [arrays], core_ids=[0])
    return r.results[0]["out"]
```

```python
from contextlib import ExitStack

import concourse.bass as bass
from concourse import mybir

F32 = mybir.dt.float32
BF16 = mybir.dt.bfloat16
I32 = mybir.dt.int32
U32 = mybir.dt.uint32
ALU = mybir.AluOpType
ACT = mybir.ActivationFunctionType
AX_X = mybir.AxisListType.X

P = 128
NB, S, E = 4, 512, 512
NT, KC = S // P, E // P
STATE = 16
CTX = 128
FF = 1024
NF = FF // P
HEADS, HD = 16, 32
HG = P // HD
RING = 4
EXPERTS, TOP = 32, 4
INNER = 192
HALF_IN = INNER // 2
TOK = NB * S
TT = TOK // P
TILES = TOK * TOP // P + EXPERTS
SLOTS = TILES * P
WRING = 4
LN_EPS = 1e-5
SIM_EPS = 1e-6


class Held:
    pass


def run_pass(nc, body):
    with nc.Block() as block:
        body(block)


def load_log_exp(nc):
    nc.scalar.preload_act_table_set("natural_log_exp_and_others")


def norm_rows(nc, st, sem, eng, row, tiles=NT):
    def finish(j):
        eng.wait_ge(sem["rstd_ready"], 2 * j + 2)
        nc.vector.tensor_scalar(st.x[:, j, :], st.r[:, j, :], st.meanvar[:, j, 0:1], st.rstd[:, j:j + 1],
                                ALU.subtract, ALU.mult).then_inc(sem["x_ready"], 1)
    for j in range(tiles):
        row(j)
        eng.wait_ge(sem["row_ready"], j + 1)
        nc.vector.bn_stats(st.stats[:, j, :], st.r[:, j, :]).then_inc(sem["stats_ready"], 1)
        eng.wait_ge(sem["stats_ready"], j + 1)
        nc.vector.bn_aggr(st.meanvar[:, j, :], st.stats[:, j, :]).then_inc(sem["var_ready"], 1)
        if j:
            finish(j - 1)
    finish(tiles - 1)


def norm_scale(nc, st, sem, eng, tiles=NT, first=None):
    for j in range(tiles):
        if first is not None:
            first(j)
        eng.wait_ge(sem["var_ready"], j + 1)
        nc.scalar.activation(st.lnvar[:, j:j + 1], st.meanvar[:, j, 1:2], ACT.Ln, bias=st.eps[:, 0:1]
                             ).then_inc(sem["rstd_ready"], 1)
        eng.wait_ge(sem["rstd_ready"], 2 * j + 1)
        nc.scalar.activation(st.rstd[:, j:j + 1], st.lnvar[:, j:j + 1], ACT.Exp, scale=-0.5
                             ).then_inc(sem["rstd_ready"], 1)


def keep_transposed(nc, st, sem, eng, first=4):
    for j in range(NT):
        eng.wait_ge(sem["xt_psum"], j + 1)
        nc.scalar.activation(st.xT[:, :, j * P:(j + 1) * P],
                             st.ps[:, first + j, :].rearrange("p (k t) -> p k t", k=KC), ACT.Copy).then_inc(sem["xt_ready"], 1)


def transpose_rows(nc, st, sem, eng, first=4):
    for j in range(NT):
        eng.wait_ge(sem["x_ready"], j + 1)
        for k in range(KC):
            last = nc.tensor.transpose(st.ps[:, first + j, k * P:(k + 1) * P], st.x[:, j, k * P:(k + 1) * P],
                                       st.ident[:, :])
        last.then_inc(sem["xt_psum"], 1)


def project_rows(nc, out, lhs, j, weights, chunks, total):
    for k in chunks:
        last = nc.tensor.matmul(out, lhs[:, k, j * P:(j + 1) * P], weights[:, k, :],
                                start=(k == 0), stop=(k == total - 1))
    return last


def project_attended(nc, st, sem, eng, oT, weights):
    eng.wait_ge(sem["o_ready"], NT * (KC - 1))
    project = lambda j, chunks: project_rows(nc, st.ps[:, j, :], oT, j, weights, chunks, KC)
    project(0, range(KC - 1))
    for j in range(NT):
        if j + 1 < NT:
            project(j + 1, range(KC - 1))
        eng.wait_ge(sem["o_ready"], NT * (KC - 1) + j + 1)
        project(j, range(KC - 1, KC)).then_inc(sem["out_psum"], 1)


def attended(nc, st, sem, eng, oT, rden, pv_needed, g, j, bank, pieces=((0, P, 0),)):
    at = slice(j * P, (j + 1) * P)
    n = NT * g + j
    eng.wait_ge(sem["pv_done"], pv_needed)
    nc.vector.reciprocal(rden[:, n % 2, :], st.ps[:, bank + 1, at]).then_inc(sem["den_ready"], 1)
    eng.wait_ge(sem["den_ready"], n + 1)
    for lo, size, there in pieces:
        last = nc.vector.tensor_tensor(oT[lo:lo + size, g, at], st.ps[lo:lo + size, bank, at],
                                       rden[there:there + size, n % 2, :], ALU.mult)
    last.then_inc(sem["o_ready"], 1)


def by_vector(i):
    return i % 7 in (1, 3, 6)


def shared_out(i):
    return sum(not by_vector(n) for n in range(i))


def recurrence_pass(nc, st, sem, T, b):
    with ExitStack() as ctx:
        sb = lambda name, shape, dt=F32: ctx.enter_context(nc.sbuf_tensor(name, shape, dt))
        xpT = sb("xpT", [P, KC, S])
        delta = sb("delta", [STATE, S])
        dbc = sb("dbc", [P, 2, S])
        u = sb("u", [P, RING, S])
        h = sb("h", [P, RING, S])
        sums = sb("sums", [P, S])
        Y_BANKS = (7, 5, 6, 4)
        yT = h
        absz, expz, logz = (u[0:STATE, n, :] for n in range(3))

        def body(block):
            @block.sync
            def _(sp):
                sp.wait_ge(sem["rows_stored"], b * 32 + 32)
                sp.dma_start(st.x[:, :, :], T["x"][bass.ds(b, 1), :, :].rearrange("a (j p) d -> p (a j) d", p=P)
                             ).then_inc(sem["x_loaded"], 16)
                sp.dma_start(st.ctxT[:, :], T["ctxT"][bass.ds(b, 1), :, :].rearrange("a c t -> c (a t)")
                             ).then_inc(sem["ctx_loaded"], 16)
                sp.dma_start(st.ctx[:, :, :], T["ctx"][bass.ds(b, 1), :, :].rearrange("a (j p) c -> p (a j) c", p=P)
                             ).then_inc(sem["ctx_loaded"], 16)
                part = T["expert_rows"][bass.ds(b * (SLOTS // NB), SLOTS // NB), :].rearrange("(p q) (k d) -> p (q k) d", p=P, k=KC)
                sp.dma_start(part, st.zeros[:, :].unsqueeze(1).to_broadcast([P, TILES // NB * KC, P])
                             ).then_inc(sem["stored"], 16)
                sp.wait_ge(sem["ctx_loaded"], 32)
                sp.wait_ge(sem["stored"], 16)
                sp.wait_ge(sem["later_loaded"], 16 * st.later)

            @block.tensor
            def _(pe):
                for c in range(KC):
                    for k in range(KC):
                        last = nc.tensor.matmul(st.ps[:, c, :], st.w_in[:, k, c * P:(c + 1) * P], st.xT_in[:, k, :],
                                                start=(k == 0), stop=(k == KC - 1))
                    last.then_inc(sem["xp_psum"], 1)
                for k in range(KC):
                    pe.wait_ge(sem["xp_ready"], k + 1)
                    last = nc.tensor.matmul(st.ps[0:STATE, 7, :], st.w_b[:, k, :], xpT[:, k, :],
                                            start=(k == 0), stop=(k == KC - 1))
                last.then_inc(sem["z_psum"], 1)
                pe.wait_ge(sem["delta_ready"], 1)

                def spread(s):
                    if s >= 2:
                        pe.wait_ge(sem["spread_copied"], s - 1)
                    nc.tensor.matmul(st.ps[:, 5 + s % 2, :], st.ident[0:STATE, s:s + 1].to_broadcast([STATE, P]), delta[:, :],
                                     start=True, stop=True).then_inc(sem["spread_psum"], 1)

                spread(0)
                spread(1)
                for j in range(NT):
                    nc.tensor.matmul(st.ps[:, j, :], st.ones[0:1, 0:P], st.bias_rows[0:1, :], start=True, stop=False)
                for s in range(STATE):
                    for c in range(KC):
                        i = s * KC + c
                        pe.wait_ge(sem["scanned"], i + 1)
                        nc.tensor.matmul(st.ps[c * 32:(c + 1) * 32, 4, :], st.ones_at[:, 32 - s:64 - s],
                                         h[:, i % RING, :], start=(s == 0), stop=(s == STATE - 1),
                                         tile_position=(0, c * 32)).then_inc(sem["summed"], 1)
                    if s + 2 < STATE:
                        spread(s + 2)
                pe.wait_ge(sem["sums_ready"], 1)
                pe.wait_ge(sem["spread_copied"], STATE)
                for c in range(KC):
                    nc.tensor.matmul(st.ps[:, Y_BANKS[c], :], st.w_c[:, c * P:(c + 1) * P], sums[:, :],
                                     start=True, stop=True).then_inc(sem["y_psum"], 1)

                def project(j, chunks):
                    for k in chunks:
                        last = nc.tensor.matmul(st.ps[:, j, :], yT[:, k, j * P:(j + 1) * P], st.w_o[:, k, :],
                                                start=False, stop=(k == KC - 1))
                    return last
                pe.wait_ge(sem["y_ready"], 1)
                for j in range(NT):
                    project(j, range(1))
                pe.wait_ge(sem["y_ready"], KC)
                for j in range(NT):
                    project(j, range(1, KC)).then_inc(sem["out_psum"], 1)
                transpose_rows(nc, st, sem, pe)

            @block.scalar
            def _(act):
                load_log_exp(nc)
                for c in range(KC):
                    act.wait_ge(sem["xp_psum"], c + 1)
                    nc.scalar.activation(xpT[:, c, :], st.ps[:, c, :], ACT.Identity,
                                         bias=st.b_in[:, c:c + 1]).then_inc(sem["xp_ready"], 1)
                act.wait_ge(sem["z_psum"], 1)
                nc.scalar.activation(absz, st.ps[0:STATE, 7, :], ACT.Abs).then_inc(sem["soft"], 1)
                act.wait_ge(sem["soft"], 1)
                nc.scalar.activation(expz, absz, ACT.Exp, scale=-1.0).then_inc(sem["soft"], 1)
                act.wait_ge(sem["soft"], 2)
                nc.scalar.activation(logz, expz, ACT.Ln, bias=st.one[0:STATE, 0:1]).then_inc(sem["soft"], 1)
                for s in range(STATE):
                    act.wait_ge(sem["spread_psum"], s + 1)
                    if s >= 2:
                        act.wait_ge(sem["product"], shared_out((s - 1) * KC))
                        act.wait_ge(sem["own_product"], (s - 1) * KC - shared_out((s - 1) * KC))
                    nc.scalar.activation(dbc[:, s % 2, :], st.ps[:, 5 + s % 2, :], ACT.Copy
                                         ).then_inc(sem["spread_copied"], 1)
                norm_scale(nc, st, sem, act)
                keep_transposed(nc, st, sem, act)

            @block.gpsimd
            def _(pool):
                for s in range(STATE):
                    pool.wait_ge(sem["spread_copied"], s + 1)
                    for c in range(KC):
                        i = s * KC + c
                        if by_vector(i):
                            continue
                        if i >= RING:
                            pool.wait_ge(sem["scanned"], i - RING + 1)
                        nc.gpsimd.tensor_tensor(u[:, i % RING, :], xpT[:, c, :], dbc[:, s % 2, :], ALU.mult
                                                ).then_inc(sem["product"], 1)

            @block.vector
            def _(dve):
                dve.wait_ge(sem["soft"], 3)
                nc.vector.scalar_tensor_tensor(delta[:, :], st.ps[0:STATE, 7, :], 0.0, logz,
                                               ALU.max, ALU.add).then_inc(sem["delta_ready"], 1)
                def own_product(i):
                    s, c = i // KC, i % KC
                    dve.wait_ge(sem["spread_copied"], s + 1)
                    if i >= RING:
                        dve.wait_ge(sem["scanned"], i - RING + 1)
                    nc.vector.tensor_tensor(u[:, i % RING, :], xpT[:, c, :], dbc[:, s % 2, :], ALU.mult
                                            ).then_inc(sem["own_product"], 1)

                for i in range(STATE * KC):
                    s, c = i // KC, i % KC
                    if i + 1 < STATE * KC and by_vector(i + 1):
                        own_product(i + 1)
                    if by_vector(i):
                        dve.wait_ge(sem["own_product"], i + 1 - shared_out(i + 1))
                    else:
                        dve.wait_ge(sem["product"], shared_out(i + 1))
                    if i >= RING:
                        dve.wait_ge(sem["summed"], i - RING + 1)
                    nc.vector.tensor_tensor_scan(
                        h[:, i % RING, :], st.decay[:, c, s:s + 1].to_broadcast([P, S]),
                        u[:, i % RING, :], 0.0, ALU.mult, ALU.add).then_inc(sem["scanned"], 1)
                dve.wait_ge(sem["summed"], STATE * KC)
                nc.vector.tensor_copy(sums[:, :], st.ps[:, 4, :]).then_inc(sem["sums_ready"], 1)
                for c in range(KC):
                    dve.wait_ge(sem["y_psum"], c + 1)
                    nc.vector.scalar_tensor_tensor(yT[:, c, :], xpT[:, c, :], st.d_param[:, c:c + 1],
                                                   st.ps[:, Y_BANKS[c], :], ALU.mult, ALU.add
                                                   ).then_inc(sem["y_ready"], 1)
                dve.wait_ge(sem["x_loaded"], 16)

                def row(j):
                    dve.wait_ge(sem["out_psum"], j + 1)
                    nc.vector.scalar_tensor_tensor(st.r[:, j, :], st.x[:, j, :], 2.0, st.ps[:, j, :],
                                                   ALU.mult, ALU.add).then_inc(sem["row_ready"], 1)
                norm_rows(nc, st, sem, dve, row)
        run_pass(nc, body)


def similarity_pass(nc, st, sem, T):
    with ExitStack() as ctx:
        sb = lambda name, shape, dt=F32: ctx.enter_context(nc.sbuf_tensor(name, shape, dt))
        kv = sb("kv", [P, NT, CTX])
        kvT = sb("kvT", [P, S])
        mixT = sb("mixT", [P, S])
        simil = sb("simil", [P, NT, S])
        simil_n = sb("simil_n", [P, NT, S])
        simil_g = sb("simil_g", [P, NT, S])
        nmax = sb("nmax", [P, NT])
        esum = sb("esum", [P, NT])
        rsum = sb("rsum", [P, NT])
        s_stats = sb("s_stats", [P, NT, 6])
        s_mv = sb("s_mv", [P, NT, 2])
        s_ln = sb("s_ln", [P, NT])
        s_rstd = sb("s_rstd", [P, NT])
        SCALE = float(E) ** -0.5
        gamma = sb("gamma", [P, S])
        beta = sb("beta", [P, S])

        def body(block):
            @block.sync
            def _(sp):
                for t, src in ((gamma, T["gamma"]), (beta, T["beta"])):
                    sp.dma_start(t[:, :], src.partition_broadcast(P)).then_inc(sem["affine_loaded"], 16)

            @block.tensor
            def _(pe):
                for j in range(NT):
                    out = st.ps[:, 0, j * P:(j + 1) * P]
                    nc.tensor.matmul(out, st.ctxT[:, j * P:(j + 1) * P], st.w_k[:, :], start=True, stop=False)
                    last = nc.tensor.matmul(out, st.ones[96:97, 0:P], st.bias_rows[96:97, 0:CTX],
                                            start=False, stop=True, tile_position=(96, 0))
                last.then_inc(sem["kv_psum"], 1)
                nc.tensor.matmul(st.ps[:, 1, :], st.w_k[:, :], st.ctxT[:, :], start=True, stop=True
                                 ).then_inc(sem["kvT_psum"], 1)
                pe.wait_ge(sem["kv_ready"], 1)
                for j in range(NT):
                    last = nc.tensor.matmul(st.ps[:, 2, :], kv[:, j, :], st.xT[:, j, :],
                                            start=(j == 0), stop=(j == NT - 1))
                last.then_inc(sem["mix_psum"], 1)
                pe.wait_ge(sem["kvT_ready"], 1)
                pe.wait_ge(sem["mix_ready"], 1)
                for j in range(NT):
                    nc.tensor.matmul(st.ps[:, 4 + j, :], mixT[:, j * P:(j + 1) * P], kvT[:, :],
                                     start=True, stop=True).then_inc(sem["sim_psum"], 1)
                transpose_rows(nc, st, sem, pe)

            @block.scalar
            def _(act):
                load_log_exp(nc)
                act.wait_ge(sem["kv_psum"], 1)
                nc.scalar.activation(kv[:, :, :], st.ps[:, 0, :].rearrange("p (j c) -> p j c", j=NT), ACT.Copy
                                     ).then_inc(sem["kv_ready"], 1)
                act.wait_ge(sem["kvT_psum"], 1)
                nc.scalar.activation(kvT[:, :], st.ps[:, 1, :], ACT.Identity, bias=st.b_k[:, 0:1]
                                     ).then_inc(sem["kvT_ready"], 1)
                for j in range(NT):
                    act.wait_ge(sem["sim_var"], j + 1)
                    nc.scalar.activation(s_ln[:, j:j + 1], s_mv[:, j, 1:2], ACT.Ln, bias=st.eps[:, 1:2]
                                         ).then_inc(sem["sim_rstd"], 1)
                    act.wait_ge(sem["sim_rstd"], 2 * j + 1)
                    nc.scalar.activation(s_rstd[:, j:j + 1], s_ln[:, j:j + 1], ACT.Exp, scale=-0.5
                                         ).then_inc(sem["sim_rstd"], 1)
                for j in range(NT):
                    act.wait_ge(sem["sim_max"], j + 1)
                    nc.scalar.activation(simil[:, j, :], simil_g[:, j, :], ACT.Exp, bias=nmax[:, j:j + 1],
                                         accum_out=esum[:, j:j + 1]).then_inc(sem["sim_exp"], 1)
                norm_scale(nc, st, sem, act)
                keep_transposed(nc, st, sem, act)

            @block.vector
            def _(dve):
                dve.wait_ge(sem["mix_psum"], 1)
                nc.vector.tensor_scalar(mixT[:, :], st.ps[:, 2, :], SCALE, None, ALU.mult).then_inc(sem["mix_ready"], 1)
                dve.wait_ge(sem["affine_loaded"], 32)
                for j in range(NT):
                    dve.wait_ge(sem["sim_psum"], j + 1)
                    nc.vector.bn_stats(s_stats[:, j, :], st.ps[:, 4 + j, :]).then_inc(sem["sim_stats"], 1)
                    dve.wait_ge(sem["sim_stats"], j + 1)
                    nc.vector.bn_aggr(s_mv[:, j, :], s_stats[:, j, :]).then_inc(sem["sim_var"], 1)
                    dve.wait_ge(sem["sim_var"], j + 1)
                    nc.vector.scalar_tensor_tensor(simil_n[:, j, :], st.ps[:, 4 + j, :], s_mv[:, j, 0:1], gamma[:, :],
                                                   ALU.subtract, ALU.mult).then_inc(sem["sim_gamma"], 1)
                for j in range(NT):
                    dve.wait_ge(sem["sim_rstd"], 2 * j + 2)
                    dve.wait_ge(sem["sim_gamma"], j + 1)
                    nc.vector.scalar_tensor_tensor(simil_g[:, j, :], simil_n[:, j, :], s_rstd[:, j:j + 1], beta[:, :],
                                                   ALU.mult, ALU.add).then_inc(sem["sim_affine"], 1)
                    dve.wait_ge(sem["sim_affine"], j + 1)
                    nc.vector.tensor_reduce(nmax[:, j:j + 1], simil_g[:, j, :], AX_X, ALU.max, negate=True
                                            ).then_inc(sem["sim_max"], 1)

                def row(j):
                    dve.wait_ge(sem["sim_exp"], j + 1)
                    nc.vector.reciprocal(rsum[:, j:j + 1], esum[:, j:j + 1]).then_inc(sem["sim_recip"], 1)
                    dve.wait_ge(sem["sim_recip"], j + 1)
                    nc.vector.scalar_tensor_tensor(st.r[:, j, :], simil[:, j, :], rsum[:, j:j + 1], st.x[:, j, :],
                                                   ALU.mult, ALU.add).then_inc(sem["row_ready"], 1)
                norm_rows(nc, st, sem, dve, row)
        run_pass(nc, body)


def load_transposed(nc, st, T, b, eng, done):
    eng.dma_start(st.xT_in[:, :, :], T["xT"][bass.ds(b, 1), :, :].rearrange("a (k p) t -> p (a k) t", p=P)
                  ).then_inc(done, 16)


def two_expert_pass(nc, st, sem, T, b):
    with ExitStack() as ctx:
        sb = lambda name, shape, dt=F32: ctx.enter_context(nc.sbuf_tensor(name, shape, dt))
        h0T = sb("h0T", [P, NF, S])
        h1T = sb("h1T", [P, NF, S])
        scores = sb("scores", [P, 2 * NT])
        first = sb("first", [P, NT])
        second = sb("second", [P, NT])
        bias_0b = sb("bias_0b", [P, E])
        bias_1b = sb("bias_1b", [P, E])
        half = sb("half_bias", [P, E])

        def body(block):
            @block.sync
            def _(sp):
                for t, src in ((bias_0b, T["b_0b"]), (bias_1b, T["b_1b"])):
                    sp.dma_start(t[:, :], src.partition_broadcast(P)).then_inc(sem["bias_loaded"], 16)
                load_transposed(nc, st, T, (b + 1) % NB, sp, sem["xT_loaded"])
                sp.wait_ge(sem["xT_loaded"], 16)

            @block.gpsimd
            def _(pool):
                pool.wait_ge(sem["choice"], 2)
                pool.wait_ge(sem["bias_loaded"], 32)
                for j in range(NT):
                    if j:
                        pool.wait_ge(sem["biased"], 3 * j)
                    nc.gpsimd.tensor_tensor(half[:, :], bias_0b[:, :], first[:, j:j + 1].to_broadcast([P, E]), ALU.mult
                                            ).then_inc(sem["biased"], 1)
                    nc.gpsimd.tensor_tensor(st.r[:, j, :], bias_1b[:, :], second[:, j:j + 1].to_broadcast([P, E]),
                                            ALU.mult).then_inc(sem["biased"], 1)
                    pool.wait_ge(sem["biased"], 3 * j + 2)
                    nc.gpsimd.tensor_tensor(st.r[:, j, :], st.r[:, j, :], half[:, :], ALU.add
                                            ).then_inc(sem["biased"], 1)

            @block.tensor
            def _(pe):
                for j in range(NT):
                    for k in range(KC):
                        last = nc.tensor.matmul(st.ps[:, 7, 2 * j:2 * j + 2], st.xT[:, k, j * P:(j + 1) * P],
                                                st.w_g[:, k, :], start=(k == 0), stop=(k == KC - 1))
                last.then_inc(sem["score_psum"], 1)
                for f in range(NF):
                    for n, (w, used) in enumerate(((st.w_0a, sem["h0_ready"]), (st.w_1a, sem["h1_ready"]))):
                        bank = 2 * (f % 2) + n
                        if f >= 2:
                            pe.wait_ge(used, f - 1)
                        for k in range(KC):
                            last = nc.tensor.matmul(st.ps[:, bank, :], w[:, k, f * P:(f + 1) * P], st.xT[:, k, :],
                                                    start=(k == 0), stop=(k == KC - 1))
                        last.then_inc((sem["h0_psum"], sem["h1_psum"])[n], 1)
                pe.wait_ge(sem["h0_ready"], NF)
                pe.wait_ge(sem["score_ready"], 1)
                for j in range(NT):
                    if j >= 2:
                        pe.wait_ge(sem["row_ready"], j - 1)
                    project_rows(nc, st.ps[:, 4 + j % 2, :], h0T, j, st.w_0b, range(NF), NF
                                 ).then_inc(sem["out_psum"], 1)
                    pe.wait_ge(sem["h1_ready"], NF)
                    project_rows(nc, st.ps[:, 6 + j % 2, :], h1T, j, st.w_1b, range(NF), NF
                                 ).then_inc(sem["out_psum"], 1)
                transpose_rows(nc, st, sem, pe, first=0)

            @block.scalar
            def _(act):
                for f in range(NF):
                    act.wait_ge(sem["h0_psum"], f + 1)
                    nc.scalar.activation(h0T[:, f, :], st.ps[:, 2 * (f % 2), :], ACT.Gelu,
                                         bias=st.b_0a[:, f:f + 1]).then_inc(sem["h0_ready"], 1)
                load_log_exp(nc)
                norm_scale(nc, st, sem, act)
                keep_transposed(nc, st, sem, act, first=0)

            @block.vector
            def _(dve):
                dve.wait_ge(sem["score_psum"], 1)
                nc.vector.tensor_copy(scores[:, :], st.ps[:, 7, 0:2 * NT]).then_inc(sem["score_ready"], 1)
                dve.wait_ge(sem["score_ready"], 1)
                pair = scores[:, :].rearrange("p (j e) -> p j e", e=2)
                nc.vector.tensor_tensor(first[:, :], pair[:, :, 0], pair[:, :, 1], ALU.is_ge).then_inc(sem["choice"], 1)
                dve.wait_ge(sem["choice"], 1)
                nc.vector.tensor_scalar(second[:, :], first[:, :], -1.0, 1.0, ALU.mult, ALU.add
                                        ).then_inc(sem["choice"], 1)
                for f in range(NF):
                    dve.wait_ge(sem["h1_psum"], f + 1)
                    nc.vector.tensor_scalar(h1T[:, f, :], st.ps[:, 2 * (f % 2) + 1, :], st.b_1a[:, f:f + 1], 0.0,
                                            ALU.add, ALU.max).then_inc(sem["h1_ready"], 1)
                for j in range(NT):
                    dve.wait_ge(sem["biased"], 3 * j + 3)
                    nc.vector.tensor_tensor(st.r[:, j, :], st.r[:, j, :], st.x[:, j, :], ALU.add
                                            ).then_inc(sem["residual"], 1)

                def row(j):
                    dve.wait_ge(sem["residual"], j + 1)
                    dve.wait_ge(sem["out_psum"], 2 * j + 1)
                    nc.vector.scalar_tensor_tensor(st.r[:, j, :], st.ps[:, 4 + j % 2, :], first[:, j:j + 1],
                                                   st.r[:, j, :], ALU.mult, ALU.add).then_inc(sem["half_row"], 1)
                    dve.wait_ge(sem["half_row"], j + 1)
                    dve.wait_ge(sem["out_psum"], 2 * j + 2)
                    nc.vector.scalar_tensor_tensor(st.r[:, j, :], st.ps[:, 6 + j % 2, :], second[:, j:j + 1],
                                                   st.r[:, j, :], ALU.mult, ALU.add).then_inc(sem["row_ready"], 1)
                norm_rows(nc, st, sem, dve, row)
        run_pass(nc, body)


def by_head(ap, heads):
    return ap.rearrange("p (h d) -> p h d", h=heads)


def polynomial_pass(nc, st, sem):
    QK = 2 * E
    NH2 = 2 * HEADS
    HALF = HD // 2
    STEPS = 2 * KC * NT
    SQ = 3
    with ExitStack() as ctx:
        sb = lambda name, shape, dt=F32: ctx.enter_context(nc.sbuf_tensor(name, shape, dt))
        v = sb("v", [P, NT, E])
        qT = sb("qT", [P, KC, S])
        kT = sb("kT", [P, KC, S])
        hsum = sb("hsum", [P, NH2])
        hmean = sb("hmean", [P, NH2])
        hvar = sb("hvar", [P, NH2])
        hln = sb("hln", [P, NH2])
        hrstd = sb("hrstd", [P, NH2])
        sq = sb("sq", [P, SQ, 2 * S])
        turned = [sq[:, n, :] for n in range(2)]
        other = [st.r[:, 2 * n:2 * n + 2, :].rearrange("p a d -> p (a d)") for n in range(2)]
        rden = sb("rden", [P, 2, P])
        oT = qT

        def body(block):
            @block.tensor
            def _(pe):
                def project(j, n, bank, done):
                    for k in range(KC):
                        last = nc.tensor.matmul(st.ps[:, bank, :], st.xT[:, k, j * P:(j + 1) * P],
                                                st.w_qkv[:, k, n * E:(n + 1) * E], start=(k == 0), stop=(k == KC - 1))
                    last.then_inc(done, 1)

                def project_qk(j):
                    if j >= 2:
                        pe.wait_ge(sem["qk_rotated"], 3 * (j - 1))
                    for n in range(2):
                        project(j, n, 2 * (j % 2) + n, sem["qk_rows"])

                def project_v(j):
                    if j >= 2:
                        pe.wait_ge(sem["v_ready"], j - 1)
                    project(j, 2, 4 + j % 2, sem["v_rows"])

                def turn(j):
                    pe.wait_ge(sem["qk_normed"], j + 1)
                    if j >= 1:
                        pe.wait_ge(sem["qkT_ready"], 2 * j)
                    for n in range(2):
                        for k in range(KC):
                            at = n * E + k * P
                            last = nc.tensor.transpose(st.ps[:, 6 + n, k * P:(k + 1) * P], other[j % 2][:, at:at + P],
                                                       st.ident[:, :])
                        last.then_inc(sem["qkT_psum"], 1)

                project_qk(0)
                project_qk(1)
                for j in range(2, NT):
                    project_qk(j)
                    turn(j - 2)
                project_v(0)
                turn(NT - 2)
                for j in range(1, NT - 1):
                    project_v(j)
                turn(NT - 1)
                project_v(NT - 1)
                pe.wait_ge(sem["qkT_ready"], 2 * NT)
                pe.wait_ge(sem["v_ready"], NT)

                def weigh(n):
                    g, pair, i = n // 8, n // 4 % 2, n % 4
                    w = S - i * P
                    pe.wait_ge(sem["weighed"], n + 1)
                    for bank in (4 + 2 * (g % 2), 5 + 2 * (g % 2)):
                        for hh in (2 * pair, 2 * pair + 1):
                            head, q = g * HG + hh, hh % 2
                            weights = v[:, i, head * HD:(head + 1) * HD] if bank % 2 == 0 else st.ones[:, 0:HD]
                            last = nc.tensor.matmul(st.ps[hh * HD:(hh + 1) * HD, bank, i * P:S], weights,
                                                    sq[:, n % SQ, q * S:q * S + w], start=(i == 0), stop=(i == NT - 1),
                                                    tile_position=(0, hh * HD))
                    last.then_inc(sem["pv_done"], 1)

                for n in range(STEPS + 2):
                    if n < STEPS:
                        g, pair, i = n // 8, n // 4 % 2, n % 4
                        if n >= 2:
                            pe.wait_ge(sem["squared"], n - 1)
                        for q in range(2):
                            part = slice((2 * pair + q) * HD, (2 * pair + q + 1) * HD)
                            last = nc.tensor.matmul(st.ps[:, 2 * (n % 2) + q, 0:S - i * P],
                                                    kT[part, g, i * P:(i + 1) * P], qT[part, g, i * P:S],
                                                    start=True, stop=True, tile_position=((2 * pair + q) * HD, 0))
                        last.then_inc(sem["qk_psum"], 1)
                    if n >= 2:
                        if n - 2 >= 16 and (n - 2) % 8 == 0:
                            pe.wait_ge(sem["o_ready"], NT * ((n - 2) // 8 - 1))
                        weigh(n - 2)
                project_attended(nc, st, sem, pe, oT, st.w_oatt)
                transpose_rows(nc, st, sem, pe)

            @block.scalar
            def _(act):
                load_log_exp(nc)
                def keep_v(j):
                    act.wait_ge(sem["v_rows"], j + 1)
                    nc.scalar.activation(v[:, j, :], st.ps[:, 4 + j % 2, :], ACT.Copy).then_inc(sem["v_ready"], 1)

                def scale(j):
                    act.wait_ge(sem["qk_centred"], j + 1)
                    nc.scalar.activation(turned[j % 2], other[j % 2], ACT.Square).then_inc(sem["qk_square"], 1)
                    act.wait_ge(sem["qk_var"], j + 1)
                    nc.scalar.activation(hln[:, :], hvar[:, :], ACT.Ln, scale=1.0 / HD, bias=st.eps[:, 0:1]
                                         ).then_inc(sem["qk_rstd"], 1)
                    act.wait_ge(sem["qk_rstd"], 2 * j + 1)
                    nc.scalar.activation(hrstd[:, :], hln[:, :], ACT.Exp, scale=-0.5).then_inc(sem["qk_rstd"], 1)

                def keep_qk(j):
                    for n, dst in enumerate((qT, kT)):
                        act.wait_ge(sem["qkT_psum"], 2 * j + n + 1)
                        nc.scalar.activation(dst[:, :, j * P:(j + 1) * P],
                                             st.ps[:, 6 + n, :].rearrange("p (k t) -> p k t", k=KC), ACT.Identity,
                                             bias=st.head_ln[:, 1:2], scale=st.head_ln[:, 0:1]
                                             ).then_inc(sem["qkT_ready"], 1)

                scale(0)
                scale(1)
                for j in range(2, NT):
                    keep_qk(j - 2)
                    if j == NT - 1:
                        keep_v(0)
                    scale(j)
                keep_qk(NT - 2)
                for j in range(1, NT - 1):
                    keep_v(j)
                keep_qk(NT - 1)
                keep_v(NT - 1)
                for n in range(STEPS):
                    w = S - n % 4 * P
                    act.wait_ge(sem["qk_psum"], n + 1)
                    if n >= SQ:
                        act.wait_ge(sem["pv_done"], n - SQ + 1)
                    dst = sq[:, n % SQ, :].rearrange("p (q t) -> p q t", q=2)
                    b0 = 2 * (n % 2)
                    nc.scalar.activation(dst[:, :, 0:w], st.ps[:, b0:b0 + 2, 0:w], ACT.Square).then_inc(sem["squared"], 1)
                norm_scale(nc, st, sem, act)
                keep_transposed(nc, st, sem, act)

            @block.gpsimd
            def _(pool):
                for j in range(NT):
                    mine, rest = turned[j % 2], other[j % 2]
                    pool.wait_ge(sem["qk_rotated"], 3 * j + 3)
                    nc.gpsimd.tensor_tensor(mine, mine, rest, ALU.add).then_inc(sem["qk_rope"], 1)
                    pool.wait_ge(sem["qk_rope"], j + 1)
                    pool.wait_ge(sem["qk_mean"], j + 1)
                    nc.gpsimd.tensor_tensor(by_head(rest, NH2), by_head(mine, NH2),
                                            hmean[:, :].unsqueeze(2).to_broadcast([P, NH2, HD]), ALU.add
                                            ).then_inc(sem["qk_centred"], 1)
                for n in range(STEPS):
                    pool.wait_ge(sem["squared"], n + 1)
                    diag = sq[:, n % SQ, :].rearrange("p (q t) -> p q t", q=2)[:, :, 0:P]
                    nc.gpsimd.affine_select(out=diag, in_=diag, compare_op=ALU.is_ge, fill=0.0, base=0,
                                            pattern=[[0, 2], [1, P]], channel_multiplier=-1).then_inc(sem["masked"], 1)

            @block.vector
            def _(dve):
                def rotate(j):
                    dve.wait_ge(sem["qk_rows"], 2 * j + 2)
                    if j >= 2:
                        dve.wait_ge(sem["qkT_psum"], 2 * (j - 1))
                    qk = st.ps[:, 2 * (j % 2):2 * (j % 2) + 2, :].rearrange("p n (h d) -> p (n h) d", h=HEADS)
                    cos = st.cos[:, j, :].unsqueeze(1).to_broadcast([P, NH2, HD])
                    sin = st.sin[:, j, :].unsqueeze(1).to_broadcast([P, NH2, HALF])
                    msin = st.msin[:, j, :].unsqueeze(1).to_broadcast([P, NH2, HALF])
                    cosines, sines = by_head(turned[j % 2], NH2), by_head(other[j % 2], NH2)
                    nc.vector.tensor_tensor(cosines, qk, cos, ALU.mult).then_inc(sem["qk_rotated"], 1)
                    nc.vector.tensor_tensor(sines[:, :, 0:HALF], qk[:, :, HALF:HD], msin, ALU.mult
                                            ).then_inc(sem["qk_rotated"], 1)
                    nc.vector.tensor_tensor(sines[:, :, HALF:HD], qk[:, :, 0:HALF], sin, ALU.mult
                                            ).then_inc(sem["qk_rotated"], 1)

                def mean(j):
                    dve.wait_ge(sem["qk_rope"], j + 1)
                    nc.vector.tensor_reduce(hsum[:, :], by_head(turned[j % 2], NH2), AX_X, ALU.add
                                            ).then_inc(sem["qk_sum"], 1)
                    dve.wait_ge(sem["qk_sum"], j + 1)
                    nc.vector.tensor_scalar(hmean[:, :], hsum[:, :], -1.0 / HD, None, ALU.mult).then_inc(sem["qk_mean"], 1)

                def variance(j):
                    dve.wait_ge(sem["qk_square"], j + 1)
                    nc.vector.tensor_reduce(hvar[:, :], by_head(turned[j % 2], NH2), AX_X, ALU.add
                                            ).then_inc(sem["qk_var"], 1)

                def normalise(j):
                    dve.wait_ge(sem["qk_rstd"], 2 * j + 2)
                    rows = by_head(other[j % 2], NH2)
                    nc.vector.tensor_tensor(rows, rows, hrstd[:, :].unsqueeze(2).to_broadcast([P, NH2, HD]), ALU.mult
                                            ).then_inc(sem["qk_normed"], 1)

                rotate(0)
                mean(0)
                rotate(1)
                for j in range(1, NT + 1):
                    variance(j - 1)
                    if j < NT:
                        mean(j)
                    normalise(j - 1)
                    if j + 1 < NT:
                        rotate(j + 1)
                for n in range(STEPS):
                    w = S - n % 4 * P
                    dve.wait_ge(sem["masked"], n + 1)
                    part = sq[:, n % SQ, :].rearrange("p (q t) -> p q t", q=2)[:, :, 0:w]
                    nc.vector.tensor_tensor(part, part, part, ALU.mult).then_inc(sem["weighed"], 1)
                    if n >= 8 and 2 <= n % 8 < 2 + NT:
                        attended(nc, st, sem, dve, oT, rden, n // 8 * 8, n // 8 - 1, n % 8 - 2, 4 + 2 * ((n // 8 - 1) % 2))
                for j in range(NT):
                    attended(nc, st, sem, dve, oT, rden, STEPS, KC - 1, j, 4 + 2 * ((KC - 1) % 2))

                def row(j):
                    dve.wait_ge(sem["out_psum"], j + 1)
                    nc.vector.tensor_tensor(st.r[:, j, :], st.x[:, j, :], st.ps[:, j, :], ALU.add
                                            ).then_inc(sem["row_ready"], 1)
                norm_rows(nc, st, sem, dve, row)
        run_pass(nc, body)


def softmax_pass(nc, st, sem, T, b):
    HALF = HD // 2
    KVH = CTX // HD
    SCALE = float(HD) ** -0.5
    with ExitStack() as ctx:
        sb = lambda name, shape, dt=F32: ctx.enter_context(nc.sbuf_tensor(name, shape, dt))
        kT = sb("kT2", [P, KVH, S])
        qT = sb("qT2", [P, KC, S])
        ssum = sb("ssum", [P, 2 * NT])
        sln = sb("sln", [P, 2 * NT])
        srstd = sb("srstd", [P, 2 * NT])
        pr = sb("pr", [P, 3, S])
        pT = sb("pT", [P, 2, NT, S])
        kn, kt1, kt2 = ([pT[:, 0, 2 * p, n * CTX:(n + 1) * CTX] for p in range(2)] for n in range(3))
        krep = [pT[:, 0, 2 * p + 1, :].rearrange("p (g r d) -> p g r d", g=KVH, r=HG) for p in range(2)]
        qn, t1, t2, qr = ((pT[:, 1, n, :], st.r[:, n, :]) for n in range(4))
        nmx = sb("nmx", [P, 4])
        rden = sb("rden2", [P, 2, P])
        oT = qT
        NSTEP = HEADS * NT
        AHEAD = 2
        TURN_BANKS = (3, 6)
        ATTEND_AT = {2: (0,), 3: (1, 2), 4: (3,)}
        SHIFTED = ((0, P // 2, P // 2), (P // 2, P // 2, 0))

        def body(block):
            @block.tensor
            def _(pe):
                for j in range(NT):
                    bank = 4 + 2 * (j % 2)
                    pe.wait_ge(sem["krep_ready"], j + 1)
                    if j >= 2:
                        pe.wait_ge(sem["qkT_ready"], 2 * (j - 1))
                    for g in range(KVH):
                        last = nc.tensor.transpose(st.ps[:, bank, g * P:(g + 1) * P],
                                                   krep[j % 2][:, g, :, :].rearrange("p r d -> p (r d)"), st.ident[:, :])
                    last.then_inc(sem["qkT_psum"], 1)
                    pe.wait_ge(sem["q_rope"], j + 1)
                    for k in range(KC):
                        last = nc.tensor.transpose(st.ps[:, bank + 1, k * P:(k + 1) * P],
                                                   qr[j % 2][:, k * P:(k + 1) * P], st.ident[:, :])
                    last.then_inc(sem["qkT_psum"], 1)
                pe.wait_ge(sem["qkT_ready"], 2 * NT)

                def score(n):
                    head, j = n // NT, n % NT
                    g, hh = head // HG, head % HG
                    part = slice(hh * HD, (hh + 1) * HD)
                    w = (j + 1) * P
                    if n >= AHEAD + 1:
                        pe.wait_ge(sem["exped"], n - AHEAD)
                    nc.tensor.matmul(st.ps[:, n % 3, 0:w], qT[part, g, j * P:(j + 1) * P], kT[part, g, 0:w],
                                     start=True, stop=False, tile_position=(hh * HD, 0))
                    nc.tensor.matmul(st.ps[:, n % 3, j * P:w], st.ident_b[:, :], st.causal_b[:, :],
                                     start=False, stop=True).then_inc(sem["qk_psum"], 1)

                def turn(n):
                    j = n % NT
                    pe.wait_ge(sem["exped"], n + 1)
                    if n >= 2:
                        pe.wait_ge(sem["pT_ready"], n - 1)
                    for i in range(j + 1):
                        last = nc.tensor.transpose(st.ps[:, TURN_BANKS[n % 2], i * P:(i + 1) * P],
                                                   pr[:, n % 3, i * P:(i + 1) * P], st.ident[:, :])
                    last.then_inc(sem["pT_psum"], 1)

                def weigh(head):
                    g, hh = head // HG, head % HG
                    part = slice(hh * HD, (hh + 1) * HD)
                    sum_at = (hh * HD + P // 2) % P
                    pe.wait_ge(sem["pT_ready"], NT * (head + 1))
                    if hh == 0 and g >= 1:
                        pe.wait_ge(sem["o_ready"], NT * g)
                    for i in range(NT):
                        a = pT[:, head % 2, i, i * P:S]
                        nc.tensor.matmul(st.ps[part, 4, i * P:S], st.ctx[:, i, g * HD:(g + 1) * HD], a,
                                         start=(i == 0), stop=(i == NT - 1), tile_position=(0, hh * HD))
                        last = nc.tensor.matmul(st.ps[sum_at:sum_at + HD, 5, i * P:S], st.ones[:, 0:HD], a,
                                                start=(i == 0), stop=(i == NT - 1), tile_position=(0, sum_at))
                    last.then_inc(sem["pv_done"], 1)

                for n in range(AHEAD):
                    score(n)
                for n in range(NSTEP):
                    if n + AHEAD < NSTEP:
                        score(n + AHEAD)
                    turn(n)
                    if n % NT == 1 and n > NT:
                        weigh(n // NT - 1)
                weigh(HEADS - 1)
                project_attended(nc, st, sem, pe, oT, st.w_oxatt)
                transpose_rows(nc, st, sem, pe)

            @block.scalar
            def _(act):
                load_log_exp(nc)
                for j in range(NT):
                    two = slice(2 * j, 2 * j + 2)
                    nc.scalar.activation(qT[:, j, 0:CTX], st.ctx[:, j, :], ACT.Square, scale=float(CTX) ** -0.5,
                                         accum_out=ssum[:, 2 * j:2 * j + 1]).then_inc(sem["rms_sum"], 1)
                    nc.scalar.activation(kT[:, j, :], st.x[:, j, :], ACT.Square, scale=float(E) ** -0.5,
                                         accum_out=ssum[:, 2 * j + 1:2 * j + 2]).then_inc(sem["rms_sum"], 1)
                    act.wait_ge(sem["rms_sum"], 2 * j + 2)
                    nc.scalar.activation(sln[:, two], ssum[:, two], ACT.Ln, bias=st.eps[:, 0:1]).then_inc(sem["rms_rstd"], 1)
                    act.wait_ge(sem["rms_rstd"], 2 * j + 1)
                    nc.scalar.activation(srstd[:, two], sln[:, two], ACT.Exp, scale=-0.5).then_inc(sem["rms_rstd"], 1)

                def repeat(j):
                    act.wait_ge(sem["k_rope"], j + 1)
                    if j >= 2:
                        act.wait_ge(sem["qkT_psum"], 2 * (j - 2) + 1)
                    nc.scalar.activation(krep[j % 2], by_head(kn[j % 2], KVH).unsqueeze(2).to_broadcast([P, KVH, HG, HD]),
                                         ACT.Copy).then_inc(sem["krep_ready"], 1)

                def keep_qk(j):
                    for n, (dst, scale) in enumerate(((kT, 1.0), (qT, SCALE))):
                        act.wait_ge(sem["qkT_psum"], 2 * j + n + 1)
                        nc.scalar.activation(dst[:, :, j * P:(j + 1) * P],
                                             st.ps[:, 4 + 2 * (j % 2) + n, :].rearrange("p (k t) -> p k t", k=KC), ACT.Copy,
                                             scale=scale).then_inc(sem["qkT_ready"], 1)

                repeat(0)
                for j in range(1, NT):
                    repeat(j)
                    keep_qk(j - 1)
                keep_qk(NT - 1)
                for n in range(NSTEP):
                    w = (n % NT + 1) * P
                    act.wait_ge(sem["max_ready"], n + 1)
                    if n >= 3:
                        act.wait_ge(sem["pT_psum"], n - 2)
                    nc.scalar.activation(pr[:, n % 3, 0:w], st.ps[:, n % 3, 0:w], ACT.Exp,
                                         bias=nmx[:, n % 4:n % 4 + 1]).then_inc(sem["exped"], 1)
                norm_scale(nc, st, sem, act)
                keep_transposed(nc, st, sem, act)

            @block.gpsimd
            def _(pool):
                for j in range(NT):
                    p = j % 2
                    pool.wait_ge(sem["k_turned"], 3 * j + 3)
                    nc.gpsimd.tensor_tensor(kn[p], kt1[p], kt2[p], ALU.add).then_inc(sem["k_rope"], 1)
                    pool.wait_ge(sem["q_turned"], 3 * j + 3)
                    if j >= 2:
                        pool.wait_ge(sem["qkT_psum"], 2 * (j - 2) + 2)
                    nc.gpsimd.tensor_tensor(qr[p], t1[p], t2[p], ALU.add).then_inc(sem["q_rope"], 1)

            @block.vector
            def _(dve):
                def rope(src, a, c, heads, sems, j):
                    cos = st.cos[:, j, :].unsqueeze(1).to_broadcast([P, heads, HD])
                    sin = st.sin[:, j, :].unsqueeze(1).to_broadcast([P, heads, HALF])
                    msin = st.msin[:, j, :].unsqueeze(1).to_broadcast([P, heads, HALF])
                    x, y, z = by_head(src, heads), by_head(a, heads), by_head(c, heads)
                    nc.vector.tensor_tensor(y, x, cos, ALU.mult).then_inc(sems, 1)
                    nc.vector.tensor_tensor(z[:, :, 0:HALF], x[:, :, HALF:HD], msin, ALU.mult).then_inc(sems, 1)
                    nc.vector.tensor_tensor(z[:, :, HALF:HD], x[:, :, 0:HALF], sin, ALU.mult).then_inc(sems, 1)

                for j in range(NT):
                    p = j % 2
                    dve.wait_ge(sem["rms_rstd"], 2 * j + 2)
                    if j >= 2:
                        dve.wait_ge(sem["krep_ready"], j - 1)
                        dve.wait_ge(sem["q_rope"], j - 1)
                    nc.vector.scalar_tensor_tensor(kn[p], st.ctx[:, j, :], srstd[:, 2 * j:2 * j + 1], st.k_norm[:, :],
                                                   ALU.mult, ALU.mult).then_inc(sem["rms_done"], 1)
                    nc.vector.scalar_tensor_tensor(qn[p], st.x[:, j, :], srstd[:, 2 * j + 1:2 * j + 2],
                                                   st.q_norm[:, :], ALU.mult, ALU.mult).then_inc(sem["rms_done"], 1)
                    dve.wait_ge(sem["rms_done"], 2 * j + 2)
                    rope(kn[p], kt1[p], kt2[p], KVH, sem["k_turned"], j)
                    rope(qn[p], t1[p], t2[p], HEADS, sem["q_turned"], j)

                def row_max(n):
                    w = (n % NT + 1) * P
                    dve.wait_ge(sem["qk_psum"], n + 1)
                    if n >= 4:
                        dve.wait_ge(sem["exped"], n - 3)
                    nc.vector.tensor_reduce(nmx[:, n % 4:n % 4 + 1], st.ps[:, n % 3, 0:w], AX_X, ALU.max, negate=True
                                            ).then_inc(sem["max_ready"], 1)

                def keep(n):
                    head, j = n // NT, n % NT
                    dve.wait_ge(sem["pT_psum"], n + 1)
                    if head >= 2 and j == 0:
                        dve.wait_ge(sem["pv_done"], head - 1)
                    nc.vector.tensor_copy(pT[:, head % 2, 0:j + 1, j * P:(j + 1) * P],
                                          st.ps[:, TURN_BANKS[n % 2], 0:(j + 1) * P].rearrange("p (i t) -> p i t", t=P)
                                          ).then_inc(sem["pT_ready"], 1)

                for n in range(AHEAD):
                    row_max(n)
                for n in range(NSTEP):
                    if n + AHEAD < NSTEP:
                        row_max(n + AHEAD)
                    keep(n)
                    if n >= NT * HG and n % (NT * HG) in ATTEND_AT:
                        g = n // (NT * HG) - 1
                        for j in ATTEND_AT[n % (NT * HG)]:
                            attended(nc, st, sem, dve, oT, rden, HG * (g + 1), g, j, 4, SHIFTED)
                for j in range(NT):
                    attended(nc, st, sem, dve, oT, rden, HEADS, KC - 1, j, 4, SHIFTED)

                def row(j):
                    dve.wait_ge(sem["out_psum"], j + 1)
                    nc.vector.tensor_tensor(st.r[:, j, :], st.x[:, j, :], st.ps[:, j, :], ALU.add
                                            ).then_inc(sem["row_ready"], 1)
                norm_rows(nc, st, sem, dve, row)

            @block.sync
            def _(sp):
                sp.wait_ge(sem["x_ready"], NT)
                sp.dma_start(T["x5"][bass.ds(b, 1), :, :].rearrange("a (j p) d -> p (a j) d", p=P), st.x[:, :, :]
                             ).then_inc(sem["rows_stored"], 16)
                sp.wait_ge(sem["xt_ready"], NT)
                sp.dma_start(T["x5T"][bass.ds(b, 1), :, :].rearrange("a (k p) t -> p (a k) t", p=P), st.xT[:, :, :]
                             ).then_inc(sem["rows_stored"], 16)
        run_pass(nc, body)


def signals(nc, ctx, names, of=""):
    return {n: ctx.enter_context(nc.semaphore(of + n)) for n in names}


def cleared_signals(nc, ctx, names):
    sem = signals(nc, ctx, names)
    nums = [h.num for h in sem.values()]
    assert nums == list(range(nums[0], nums[0] + len(nums))), nums
    sem["all"] = range(nums[0], nums[-1] + 1)
    return sem


LAYER_SIGNALS = """x_loaded xT_loaded ctx_loaded row_ready stats_ready var_ready rstd_ready x_ready xt_psum xt_ready
xp_psum xp_ready z_psum soft delta_ready spread_psum spread_copied product scanned own_product summed sums_ready affine_loaded bias_loaded biased residual y_psum y_ready
out_psum kvT_psum kvT_ready kv_psum kv_ready mix_psum mix_ready sim_psum sim_stats sim_var sim_rstd
sim_gamma sim_affine sim_max sim_exp sim_recip score_psum score_ready choice h0_psum h0_ready h1_psum
h1_ready half_row qk_rows v_rows v_ready qk_rotated qk_rope qk_sum qk_mean qk_centred qk_square qk_var qk_rstd qk_normed
qkT_psum qkT_ready qk_psum squared masked weighed pv_done den_ready o_ready rms_sum rms_rstd rms_done k_turned
k_rope krep_ready q_turned q_rope max_ready exped pT_psum pT_ready stored""".split()


LASTING_SIGNALS = "weights_loaded later_loaded made rows_stored".split()


def clear(nc, sem, block):
    @block.sync
    def _(sp):
        sp.sem_clear(sem["all"])


def layers(nc, T):
    with ExitStack() as ctx:
        sb = lambda name, shape, dt=F32: ctx.enter_context(nc.sbuf_tensor(name, shape, dt))
        st = Held()
        sem = cleared_signals(nc, ctx, LAYER_SIGNALS + LASTING_SIGNALS)
        lasting = range(sem["all"][-1] + 1 - len(LASTING_SIGNALS), sem["all"][-1] + 1)
        sem["all"] = range(sem["all"][0], lasting[0])
        st.ps = ctx.enter_context(nc.psum_tensor("ps", [P, 8, 512], F32))
        loads = []

        def held(name, shape, src):
            t = sb(name, shape)
            loads.append((name, t[(slice(None),) * len(shape)], src))
            return t

        weights = lambda a: a.rearrange("(k p) n -> p k n", p=P)
        st.w_in = held("w_in", [P, KC, E], weights(T["w_in"]))
        st.w_b = held("w_b", [P, KC, STATE], weights(T["w_b"]))
        st.w_c = held("w_c", [P, E], T["w_c"])
        st.w_o = held("w_o", [P, KC, E], weights(T["w_o"]))
        st.w_k = held("w_k", [P, CTX], T["w_k"])
        st.w_g = held("w_g", [P, KC, 2], weights(T["w_g"]))
        st.w_0a = held("w_0a", [P, KC, FF], weights(T["w_0a"]))
        st.w_1a = held("w_1a", [P, KC, FF], weights(T["w_1a"]))
        st.w_0b = held("w_0b", [P, NF, E], weights(T["w_0b"]))
        st.w_1b = held("w_1b", [P, NF, E], weights(T["w_1b"]))
        st.w_qkv = held("w_qkv", [P, KC, 3 * E], weights(T["w_qkv"]))
        st.w_oatt = held("w_oatt", [P, KC, E], weights(T["w_oatt"]))
        st.w_oxatt = held("w_oxatt", [P, KC, E], weights(T["w_oxatt"]))
        st.bias_rows = held("bias_rows", [P, E], T["bias_rows"])
        st.b_in = held("b_in", [P, KC], T["b_in"])
        st.d_param = held("d_param", [P, KC], T["d_param"])
        st.b_0a = held("b_0a", [P, NF], T["b_0a"])
        st.b_1a = held("b_1a", [P, NF], T["b_1a"])
        st.b_k = held("b_k", [P, 1], T["b_k"])
        st.head_ln = held("head_ln", [P, 2], T["head_ln"])
        a_in = held("a_in", [P, KC, STATE], T["a_in"])
        st.q_norm = held("q_norm", [P, E], T["q_norm"].partition_broadcast(P))
        st.k_norm = held("k_norm", [P, CTX], T["k_norm"].partition_broadcast(P))
        st.ident = held("ident", [P, P], T["ident"])
        st.ones_at = held("ones_at", [P, 64], T["ones_at"])
        st.cos = held("cos", [P, NT, HD], T["cos"])
        st.sin = held("sin", [P, NT, HD // 2], T["sin"])
        st.msin = held("msin", [P, NT, HD // 2], T["msin"])
        st.ones = sb("ones", [P, P])
        st.one = sb("one", [P, 1])
        st.zeros = sb("zeros", [P, P])
        st.eps = sb("eps", [P, 2])
        st.ident_b = sb("ident_b", [P, P], BF16)
        st.causal_b = sb("causal_b", [P, P], BF16)
        st.decay = sb("decay", [P, KC, STATE])
        st.x = sb("x_rows", [P, NT, E])
        st.xT = sb("x_rowsT", [P, KC, S])
        st.r = sb("r_rows", [P, NT, E])
        causal, a_exp = st.r[:, 0, 0:P], st.r[:, 1, 0:KC * STATE].rearrange("p (k n) -> p k n", k=KC)
        loads.append(("causal", causal, T["causal"]))
        st.xT_in = sb("x_inT", [P, KC, S])
        st.ctx = sb("ctx_rows", [P, NT, CTX])
        st.ctxT = sb("ctx_T", [P, S])
        st.stats = sb("stats", [P, NT, 6])
        st.meanvar = sb("meanvar", [P, NT, 2])
        st.lnvar = sb("lnvar", [P, NT])
        st.rstd = sb("rstd", [P, NT])

        early_names = ("w_in", "w_b", "w_c", "w_o", "bias_rows", "b_in", "d_param", "a_in", "ident", "causal", "ones_at")
        early = [(t, src) for name, t, src in loads if name in early_names]
        rest = [(t, src) for name, t, src in loads if name not in early_names]
        st.later = len(rest)
        with nc.Block() as block:
            @block.sync
            def _(sp):
                sp.sem_inc(sem["rows_stored"], 32)
                load_transposed(nc, st, T, 0, sp, sem["weights_loaded"])
                for t, src in early:
                    sp.dma_start(t, src).then_inc(sem["weights_loaded"], 16)
                for t, src in rest:
                    sp.dma_start(t, src).then_inc(sem["later_loaded"], 16)
                sp.wait_ge(sem["weights_loaded"], 16 * (1 + len(early)))

            @block.scalar
            def _(act):
                load_log_exp(nc)
                act.wait_ge(sem["weights_loaded"], 16 * (1 + len(early)))
                nc.scalar.activation(a_exp[:, :, :], a_in[:, :, :], ACT.Exp, scale=-1.0).then_inc(sem["made"], 1)
                nc.scalar.activation(st.ident_b[:, :], st.ident[:, :], ACT.Copy)
                nc.scalar.activation(st.causal_b[:, :], causal, ACT.Copy)

            @block.vector
            def _(dve):
                nc.vector.memset(st.ones[:, :], 1.0)
                nc.vector.memset(st.one[:, :], 1.0)
                nc.vector.memset(st.zeros[:, :], 0.0)
                nc.vector.memset(st.eps[:, 0:1], LN_EPS)
                nc.vector.memset(st.eps[:, 1:2], SIM_EPS)
                dve.wait_ge(sem["made"], 1)
                nc.vector.tensor_scalar(a_exp[:, :, :], a_exp[:, :, :], 1.0, None, ALU.add).then_inc(sem["made"], 1)
                dve.wait_ge(sem["made"], 2)
                nc.vector.reciprocal(st.decay[:, :, :], a_exp[:, :, :])

        with nc.Fori(0, NB) as b:
            def again():
                with nc.Block() as block:
                    clear(nc, sem, block)
            recurrence_pass(nc, st, sem, T, b)
            again()
            similarity_pass(nc, st, sem, T)
            again()
            two_expert_pass(nc, st, sem, T, b)
            again()
            polynomial_pass(nc, st, sem)
            again()
            softmax_pass(nc, st, sem, T, b)
            again()
        with nc.Block() as block:
            @block.sync
            def _(sp):
                sp.wait_ge(sem["rows_stored"], 32 + 32 * NB)
        with nc.Block() as block:
            @block.sync
            def _(sp):
                sp.sem_clear(lasting)


DISPATCH_SIGNALS = """first_loaded gate_up_loaded down_loaded x5T_loaded x5_loaded const_loaded logitsT_psum logitsT_ready logits_psum logits_ready top_ready index_ready
less_max exp_top top_sum top_recip weight_ready index_real onehot chosen prefix_psum step_ready
tiles_real tiles_int tiles_shift tiles_ready ends_ready starts_ready base_ready pos_part pos_ready picked slot_real
slot_ready passed passed_sum table_part table_psum expert_ready scattered gate_psum up_psum
silu_ready hidden_ready down_psum shared_ready ones_made""".split()



def shared_gate_up(nc, pe, sh, n, f, block_T):
    pe.wait_ge(sh.sem["hidden_ready"], n * NF + f + 1)
    for w, bank, s in ((sh.gate, 4, sh.sem["gate_psum"]), (sh.up, 6, sh.sem["up_psum"])):
        for k in range(KC):
            last = nc.tensor.matmul(sh.ps[:, bank + f % 2, :], w[:, k, f * P:(f + 1) * P],
                                    block_T[:, k, :], start=(k == 0), stop=(k == KC - 1))
        last.then_inc(s, 1)


def shared_silu(nc, act, sh, n, f):
    act.wait_ge(sh.sem["gate_psum"], n * NF + f + 1)
    act.wait_ge(sh.sem["hidden_ready"], n * NF + f + 1)
    nc.scalar.activation(sh.silu[:, f % 2, :], sh.ps[:, 4 + f % 2, :], ACT.Silu).then_inc(sh.sem["silu_ready"], 1)


def shared_hide(nc, dve, sh, n, f):
    dve.wait_ge(sh.sem["silu_ready"], n * NF + f + 1)
    dve.wait_ge(sh.sem["up_psum"], n * NF + f + 1)
    nc.vector.tensor_tensor(sh.hidden[:, f, :], sh.silu[:, f % 2, :], sh.ps[:, 6 + f % 2, :], ALU.mult
                            ).then_inc(sh.sem["hidden_ready"], 1)


def shared_down(nc, pe, sh, n, j):
    pe.wait_ge(sh.sem["shared_ready"], n * NT + j + 1)
    for f in range(NF):
        last = nc.tensor.matmul(sh.ps[:, j % 2, :], sh.hidden[:, f, j * P:(j + 1) * P], sh.down[:, f, :],
                                start=(f == 0), stop=(f == NF - 1))
    last.then_inc(sh.sem["down_psum"], 1)


def shared_add(nc, dve, sh, n, j, acc, row):
    dve.wait_ge(sh.sem["down_psum"], n * NT + j + 1)
    nc.vector.tensor_tensor(acc, row, sh.ps[:, j % 2, :], ALU.add).then_inc(sh.sem["shared_ready"], 1)


def dispatch_pass(nc, T, M):
    with ExitStack() as ctx:
        sb = lambda name, shape, dt=F32: ctx.enter_context(nc.sbuf_tensor(name, shape, dt))
        sem = signals(nc, ctx, DISPATCH_SIGNALS)
        ps = ctx.enter_context(nc.psum_tensor("ps_dispatch", [P, 8, 512], F32))
        xT = sb("x5T_most", [P, KC, TOK - S])
        x = sb("x5_most", [P, TT - NT, E])
        columns_of = lambda b: M.xT_last[:, :, :] if b == NB - 1 else xT[:, :, b * S:(b + 1) * S]
        router = sb("router", [P, KC, EXPERTS])
        before = sb("before", [P, P])
        iota = sb("iota", [P, EXPERTS])
        tile_no = sb("tile_no", [P, 3])
        ident = sb("ident_d", [P, P])
        ones = sb("ones_d", [P, P])
        sh = Held()
        sh.gate, sh.up, sh.down, sh.ps, sh.sem = M.ws_gate, M.ws_up, M.ws_down, ps, sem
        logitsT = sb("logitsT", [P, S])
        logits = sb("logits", [P, TT, EXPERTS])
        top = sb("top", [P, TT, 8])
        index = sb("index", [P, TT, 8], U32)
        index_f = sb("index_f", [P, TT, 8])
        e_top = sb("e_top", [P, TT, TOP])
        e_sum = sb("e_sum", [P, TT])
        onehot = sb("onehot", [P, TOP, TT, EXPERTS])
        chosen = sb("chosen", [P, 3, TT * EXPERTS])
        count = sb("count", [P, 2, TT, EXPERTS])
        pos = sb("pos", [P, TT, EXPERTS])
        picked = sb("picked", [P, 2, TT, EXPERTS])
        slot_f = sb("slot_f", [P, TT, TOP])
        need_f = sb("need_f", [P, EXPERTS])
        need_i = sb("need_i", [P, 2, EXPERTS], I32)
        need = sb("need", [P, EXPERTS])
        used = sb("used", [P, EXPERTS])
        ends = sb("ends", [P, EXPERTS])
        starts = sb("starts", [P, EXPERTS])
        base = sb("base", [P, EXPERTS])
        passed = sb("passed", [P, 4, EXPERTS])
        sums = sb("passed_sums", [P, 4])
        table = sb("table", [P, 4])
        sh.silu = sb("silu_gate", [P, 2, S])
        sh.hidden = sb("hidden", [P, NF, S])
        x5T = T["x5T"].rearrange("b (k p) t -> b p k t", p=P)
        x5 = T["x5"].rearrange("b (j p) d -> b p j d", p=P)

        with nc.Block() as block:
            @block.sync
            def _(sp):
                sp.dma_start(xT[:, :, 0:S], x5T[0]).then_inc(sem["first_loaded"], 16)
                halves = [slice(n * FF // 2, (n + 1) * FF // 2) for n in range(2)]
                for half, done in zip(halves, (sem["first_loaded"], sem["gate_up_loaded"])):
                    for t, src in ((sh.gate, T["ws_gate"]), (sh.up, T["ws_up"])):
                        sp.dma_start(t[:, :, half], src.rearrange("(k p) n -> p k n", p=P)[:, :, half]).then_inc(done, 16)
                for b in range(1, NB):
                    sp.dma_start(columns_of(b), x5T[b]).then_inc(sem["x5T_loaded"], 16)
                consts = ((router[:, :, :], T["router"].rearrange("(k p) n -> p k n", p=P)), (before[:, :], T["before"]),
                          (iota[:, :], T["iota"]), (tile_no[:, :], T["tile_no"]), (ident[:, :], T["ident"]))
                for t, src in consts:
                    sp.dma_start(t, src).then_inc(sem["const_loaded"], 16)
                for b in range(NB):
                    rows = M.x_last[:, :, :] if b == NB - 1 else x[:, b * NT:(b + 1) * NT, :]
                    sp.dma_start(rows, x5[b]).then_inc(sem["x5_loaded"], 16)
                sp.dma_start(sh.down[:, :, :], T["ws_down"].rearrange("(k p) n -> p k n", p=P)
                             ).then_inc(sem["down_loaded"], 16)
                sp.wait_ge(sem["down_loaded"], 16)

            @block.tensor
            def _(pe):
                block_T = lambda n: xT[:, :, bass.ds(n * S, S)]
                gate_up = lambda n, f: shared_gate_up(nc, pe, sh, n, f, block_T(n))
                down = lambda n, j: shared_down(nc, pe, sh, n, j)

                pe.wait_ge(sem["first_loaded"], 16 * 3)
                for f in range(4):
                    gate_up(0, f)
                pe.wait_ge(sem["gate_up_loaded"], 16 * 2)
                gate_up(0, 4)
                gate_up(0, 5)
                pe.wait_ge(sem["x5T_loaded"], 16 * (NB - 1))
                pe.wait_ge(sem["const_loaded"], 16 * 5)
                for k in range(KC):
                    for b in range(NB):
                        part = slice(b * EXPERTS, (b + 1) * EXPERTS)
                        last = nc.tensor.matmul(ps[part, 0, :], router[:, k, :], columns_of(b)[:, k, :],
                                                start=(k == 0), stop=(k == KC - 1), tile_position=(0, b * EXPERTS))
                last.then_inc(sem["logitsT_psum"], 1)
                pe.wait_ge(sem["logitsT_ready"], 1)
                for j in range(NT):
                    last = nc.tensor.transpose(ps[:, 1, j * P:(j + 1) * P], logitsT[:, j * P:(j + 1) * P], ident[:, :])
                last.then_inc(sem["logits_psum"], 1)
                gate_up(0, 6)
                gate_up(0, 7)
                pe.wait_ge(sem["ones_made"], 1)
                pe.wait_ge(sem["chosen"], 3)
                nc.tensor.matmul(ps[:, 3, :], before[:, :], chosen[:, 2, :], start=True, stop=True)
                nc.tensor.matmul(ps[:, 2, :], ones[:, :], chosen[:, 2, :], start=True, stop=True
                                 ).then_inc(sem["prefix_psum"], 1)
                pe.wait_ge(sem["hidden_ready"], NF + 2)
                pe.wait_ge(sem["down_loaded"], 16)
                down(0, 0)
                down(0, 1)
                pe.wait_ge(sem["table_part"], 3)
                pe.wait_ge(sem["passed_sum"], 4)
                nc.tensor.transpose(ps[0:4, 3, 0:P], table[:, :], ident[:, :]).then_inc(sem["table_psum"], 1)
                down(0, 2)
                down(0, 3)
                with pe.Fori(1, NB - 1) as n:
                    for f in range(NF):
                        gate_up(n, f)
                    pe.wait_ge(sem["hidden_ready"], n * NF + NF + 2)
                    for j in range(NT):
                        down(n, j)

            @block.scalar
            def _(act):
                silu = lambda n, f: shared_silu(nc, act, sh, n, f)
                for f in range(6):
                    silu(0, f)
                act.wait_ge(sem["logitsT_psum"], 1)
                nc.scalar.activation(logitsT[:, :], ps[:, 0, :], ACT.Copy).then_inc(sem["logitsT_ready"], 1)
                act.wait_ge(sem["less_max"], 1)
                nc.scalar.activation(e_top[:, :, :], e_top[:, :, :], ACT.Exp).then_inc(sem["exp_top"], 1)
                silu(0, 6)
                silu(0, 7)
                with act.Fori(1, NB - 1) as n:
                    for f in range(NF):
                        silu(n, f)

            @block.gpsimd
            def _(pool):
                nc.gpsimd.memset(ones[:, :], 1.0).then_inc(sem["ones_made"], 1)
                pool.wait_ge(sem["slot_ready"], 1)
                pool.wait_ge(sem["x5_loaded"], 16 * NB)
                for i in range(TT):
                    for k in range(TOP):
                        nc.gpsimd.indirect_dma_start(
                            T["expert_rows"], bass.IndirectOffsetOnAxis(ap=M.slots[:, i, k:k + 1], axis=0),
                            x[:, i, :] if i < TT - NT else M.x_last[:, i - (TT - NT), :], None
                            ).then_inc(sem["scattered"], 16)
                pool.wait_ge(sem["scattered"], 16 * TT * TOP)

            @block.vector
            def _(dve):
                flat3 = lambda t: t.rearrange("p i e -> p (i e)")

                tile = lambda t, at: t[:, bass.ds(at, 1), :].rearrange("p a d -> p (a d)")
                hide = lambda n, f: shared_hide(nc, dve, sh, n, f)
                add_shared = lambda n, j: shared_add(nc, dve, sh, n, j, tile(M.acc, n * NT + j), tile(x, n * NT + j))

                dve.sem_inc(sem["hidden_ready"], 2)
                dve.sem_inc(sem["shared_ready"], 2)
                for f in range(6):
                    hide(0, f)
                dve.wait_ge(sem["logits_psum"], 1)
                nc.vector.tensor_copy(logits[:, :, :].rearrange("p (b j) e -> p j b e", b=NB),
                                      ps[:, 1, :].rearrange("p (j b e) -> p j b e", j=NT, b=NB)
                                      ).then_inc(sem["logits_ready"], 1)
                dve.wait_ge(sem["logits_ready"], 1)
                for i in range(TT):
                    nc.vector.max(top[:, i, :], logits[:, i, :]).then_inc(sem["top_ready"], 1)
                dve.wait_ge(sem["top_ready"], TT)
                nc.vector.tensor_tensor(e_top[:, :, :], top[:, :, 0:TOP], top[:, :, 0:1].to_broadcast([P, TT, TOP]),
                                        ALU.subtract).then_inc(sem["less_max"], 1)
                for i in range(TT):
                    nc.vector.max_index(index[:, i, :], top[:, i, :], logits[:, i, :]).then_inc(sem["index_ready"], 1)
                dve.wait_ge(sem["index_ready"], TT)
                nc.vector.tensor_copy(index_f[:, :, :], index[:, :, :]).then_inc(sem["index_real"], 1)
                dve.wait_ge(sem["index_real"], 1)
                experts = iota[:, :].unsqueeze(1).to_broadcast([P, TT, EXPERTS])
                dve.wait_ge(sem["const_loaded"], 16 * 5)
                for k in range(TOP):
                    nc.vector.tensor_tensor(onehot[:, k, :, :], experts,
                                            index_f[:, :, k:k + 1].to_broadcast([P, TT, EXPERTS]), ALU.is_equal
                                            ).then_inc(sem["onehot"], 1)
                dve.wait_ge(sem["onehot"], TOP)
                for n in range(3):
                    before_n = onehot[:, 0, :, :] if n == 0 else chosen[:, n - 1, :].rearrange(
                        "p (i e) -> p i e", e=EXPERTS)
                    if n:
                        dve.wait_ge(sem["chosen"], n)
                    nc.vector.tensor_tensor(chosen[:, n, :].rearrange("p (i e) -> p i e", e=EXPERTS), before_n,
                                            onehot[:, n + 1, :, :], ALU.add).then_inc(sem["chosen"], 1)
                dve.wait_ge(sem["exp_top"], 1)
                nc.vector.tensor_reduce(e_sum[:, :], e_top[:, :, :], AX_X, ALU.add).then_inc(sem["top_sum"], 1)
                dve.wait_ge(sem["top_sum"], 1)
                nc.vector.reciprocal(e_sum[:, :], e_sum[:, :]).then_inc(sem["top_recip"], 1)
                dve.wait_ge(sem["top_recip"], 1)
                nc.vector.tensor_tensor(M.weights[:, :, :], e_top[:, :, :],
                                        e_sum[:, :].unsqueeze(2).to_broadcast([P, TT, TOP]), ALU.mult
                                        ).then_inc(sem["weight_ready"], 1)
                hide(0, 6)
                hide(0, 7)
                dve.wait_ge(sem["prefix_psum"], 1)
                nc.vector.tensor_copy(flat3(count[:, 0, :, :]), ps[:, 2, :]).then_inc(sem["step_ready"], 1)
                for n in range(4):
                    d = 1 << n
                    src, dst = count[:, n % 2, :, :], count[:, (n + 1) % 2, :, :]
                    dve.wait_ge(sem["step_ready"], 2 * n + 1)
                    nc.vector.tensor_tensor(dst[:, d:TT, :], src[:, d:TT, :], src[:, 0:TT - d, :], ALU.add
                                            ).then_inc(sem["step_ready"], 1)
                    nc.vector.tensor_copy(dst[:, 0:d, :], src[:, 0:d, :]).then_inc(sem["step_ready"], 1)
                dve.wait_ge(sem["step_ready"], 9)
                nc.vector.tensor_scalar(need_f[:, :], count[:, 0, TT - 1, :], float(P - 1), None, ALU.add
                                        ).then_inc(sem["tiles_real"], 1)
                dve.wait_ge(sem["tiles_real"], 1)
                nc.vector.tensor_copy(need_i[:, 0, :], need_f[:, :]).then_inc(sem["tiles_int"], 1)
                dve.wait_ge(sem["tiles_int"], 1)
                nc.vector.tensor_scalar(need_i[:, 1, :], need_i[:, 0, :], 7, None, ALU.arith_shift_right
                                        ).then_inc(sem["tiles_shift"], 1)
                dve.wait_ge(sem["tiles_shift"], 1)
                nc.vector.tensor_copy(need[:, :], need_i[:, 1, :]).then_inc(sem["tiles_ready"], 1)
                dve.wait_ge(sem["tiles_ready"], 1)
                dve.wait_ge(sem["ones_made"], 1)
                nc.vector.tensor_scalar(used[:, :], need[:, :], 0.0, None, ALU.is_gt).then_inc(sem["tiles_ready"], 1)
                nc.vector.tensor_tensor_scan(ends[:, :], ones[:, 0:EXPERTS], need[:, :], 0.0, ALU.mult, ALU.add
                                             ).then_inc(sem["ends_ready"], 1)
                dve.wait_ge(sem["ends_ready"], 1)
                nc.vector.tensor_tensor(starts[:, :], ends[:, :], need[:, :], ALU.subtract).then_inc(sem["starts_ready"], 1)
                dve.wait_ge(sem["starts_ready"], 1)
                nc.vector.tensor_scalar(base[:, :], starts[:, :], float(P), None, ALU.mult).then_inc(sem["base_ready"], 1)
                within = ps[:, 3, :].rearrange("p (i e) -> p i e", e=EXPERTS)
                nc.vector.tensor_copy(pos[:, 0, :], within[:, 0, :]).then_inc(sem["pos_part"], 1)
                nc.vector.tensor_tensor(pos[:, 1:TT, :], within[:, 1:TT, :], count[:, 0, 0:TT - 1, :], ALU.add
                                        ).then_inc(sem["pos_part"], 1)
                dve.wait_ge(sem["base_ready"], 1)
                dve.wait_ge(sem["pos_part"], 2)
                nc.vector.tensor_tensor(pos[:, :, :], pos[:, :, :],
                                        base[:, :].unsqueeze(1).to_broadcast([P, TT, EXPERTS]), ALU.add
                                        ).then_inc(sem["pos_ready"], 1)
                dve.wait_ge(sem["pos_ready"], 1)
                for k in range(TOP):
                    if k >= 2:
                        dve.wait_ge(sem["slot_real"], k - 1)
                    nc.vector.tensor_tensor(picked[:, k % 2, :, :], onehot[:, k, :, :], pos[:, :, :], ALU.mult
                                            ).then_inc(sem["picked"], 1)
                    dve.wait_ge(sem["picked"], k + 1)
                    nc.vector.tensor_reduce(slot_f[:, :, k], picked[:, k % 2, :, :], AX_X, ALU.add
                                            ).then_inc(sem["slot_real"], 1)
                dve.wait_ge(sem["slot_real"], TOP)
                nc.vector.tensor_copy(M.slots[:, :, :], slot_f[:, :, :]).then_inc(sem["slot_ready"], 1)
                dve.wait_ge(sem["tiles_ready"], 2)
                for n in range(2):
                    nc.vector.tensor_scalar(passed[:, n, :], ends[:, :], tile_no[:, n:n + 1], None, ALU.is_le
                                            ).then_inc(sem["passed"], 1)
                dve.wait_ge(sem["passed"], 2)
                for n in range(2):
                    nc.vector.tensor_tensor(passed[:, 2 + n, :], passed[:, n, :], used[:, :], ALU.mult
                                            ).then_inc(sem["passed"], 1)
                dve.wait_ge(sem["passed"], 4)
                nc.vector.tensor_reduce(sums[:, :], passed[:, :, :], AX_X, ALU.add).then_inc(sem["passed"], 1)
                dve.wait_ge(sem["passed"], 5)
                nc.vector.tensor_scalar(table[:, 0:1], sums[:, 0:1], float(EXPERTS - 1), None, ALU.min
                                        ).then_inc(sem["passed_sum"], 1)
                nc.vector.tensor_copy(table[:, 1:2], sums[:, 2:3]).then_inc(sem["passed_sum"], 1)
                nc.vector.tensor_tensor(table[:, 3:4], sums[:, 2:3], sums[:, 3:4], ALU.not_equal
                                        ).then_inc(sem["passed_sum"], 1)
                dve.wait_ge(sem["passed_sum"], 3)
                nc.vector.tensor_tensor(table[:, 2:3], table[:, 3:4], tile_no[:, 2:3], ALU.max
                                        ).then_inc(sem["passed_sum"], 1)
                nc.vector.tensor_copy(sums[:, 0:1], table[:, 3:4]).then_inc(sem["table_part"], 3)
                dve.wait_ge(sem["x5_loaded"], 16 * NB)
                add_shared(0, 0)
                add_shared(0, 1)
                dve.wait_ge(sem["table_psum"], 1)
                nc.vector.tensor_copy(M.tile_info[:, :], ps[0:4, 3, 0:P]).then_inc(sem["expert_ready"], 1)
                dve.wait_ge(sem["expert_ready"], 1)
                nc.vector.tensor_scalar(M.ring_at[:, :], M.tile_info[:, :], WRING - 1, None, ALU.bitwise_and
                                        ).then_inc(sem["expert_ready"], 1)
                add_shared(0, 2)
                add_shared(0, 3)
                with dve.Fori(1, NB - 1) as n:
                    dve.wait_ge(sem["shared_ready"], n * NT + 2)
                    for f in range(NF):
                        hide(n, f)
                    for j in range(NT):
                        add_shared(n, j)


EXPERT_SIGNALS = """w_loaded row_loaded0 row_loaded1 row_turned rowT_ready gu_psum silu_done h_rows h_turned hT_ready
y_psum y_ready y_stored0 y_stored1 ident_loaded""".split()
PEEL = 4


def expert_pass(nc, T, M):
    with ExitStack() as ctx:
        sb = lambda name, shape, dt=F32: ctx.enter_context(nc.sbuf_tensor(name, shape, dt))
        sem = signals(nc, ctx, EXPERT_SIGNALS)
        ps = ctx.enter_context(nc.psum_tensor("ps_expert", [P, 8, 512], F32))
        ident = sb("ident_e", [P, P])
        w_gu = sb("w_gu", [P, WRING, KC, 2 * INNER])
        w_dn = sb("w_dn", [P, WRING, 2, E])
        rows = sb("rows", [P, 2, E])
        rowsT = sb("rowsT", [P, 2, KC, P])
        silu = sb("silu", [P, 2, INNER])
        h = sb("h_exp", [P, 2, INNER])
        hT = sb("hT_exp", [HALF_IN, 2, 2, P])
        y = sb("y_exp", [P, 2, E])
        row_loaded = (sem["row_loaded0"], sem["row_loaded1"])
        y_stored = (sem["y_stored0"], sem["y_stored1"])
        w_gate = T["w_gate"].rearrange("e (k p) n -> e p k n", p=P)
        w_up = T["w_up"].rearrange("e (k p) n -> e p k n", p=P)
        w_down = T["w_down"].rearrange("e (k p) n -> e p k n", p=HALF_IN)

        def steps(eng, step):
            for q in range(PEEL):
                step(q // 2, q % 2)
            with eng.Fori(PEEL // 2, (TILES - PEEL) // 2) as i:
                for p in range(2):
                    step(i, p)
            for q in range(TILES - PEEL, TILES):
                step(q // 2, q % 2)

        def after(i, p, d):
            at, parity = (p + d) // 2, (p + d) % 2
            if isinstance(i, int):
                q = 2 * i + p + d
                return (i + at, parity) if 0 <= q < TILES else None
            return i + at, parity

        def later(i, n):
            return not isinstance(i, int) or i >= n

        number = lambda i, p: 2 * i + p

        with nc.Block() as block:
            @block.sync
            def _(sp):
                sp.dma_start(ident[:, :], T["ident"]).then_inc(sem["ident_loaded"], 16)
                sp.wait_ge(sem["ident_loaded"], 16)

                def weights(i, p):
                    q = number(i, p)
                    expert = sp.value_load(M.tile_info[0:1, bass.ds(q, 1)], min_val=0, max_val=EXPERTS - 1)
                    at = sp.value_load(M.ring_at[1:2, bass.ds(q, 1)], min_val=0, max_val=WRING - 1)
                    fresh = sp.value_load(M.tile_info[2:3, bass.ds(q, 1)], min_val=0, max_val=1)
                    if later(i, WRING // 2):
                        sp.wait_ge(sem["y_psum"], q - WRING + 1)
                    if later(i, 1) or p:
                        sp.wait_ge(sem["w_loaded"], 48 * (q - 1) + 48)
                    new = fresh > 0
                    for src, lo in ((w_gate, 0), (w_up, INNER)):
                        sp.dma_start(w_gu[:, bass.ds(at, 1), :, lo:lo + INNER].rearrange("p a k n -> p (a k) n"),
                                     src[bass.ds(expert, 1), :, :, :].rearrange("a p k n -> p (a k) n"), cond=new
                                     ).then_inc(sem["w_loaded"], 16)
                    sp.dma_start(w_dn[0:HALF_IN, bass.ds(at, 1), :, :].rearrange("p a k n -> p (a k) n"),
                                 w_down[bass.ds(expert, 1), :, :, :].rearrange("a p k n -> p (a k) n"), cond=new
                                 ).then_inc(sem["w_loaded"], 16)
                steps(sp, weights)

            @block.tensor
            def _(pe):
                def ring(i, p):
                    return pe.value_load(M.ring_at[1:2, bass.ds(number(i, p), 1)], min_val=0, max_val=WRING - 1)

                def turn_rows(i, p):
                    pe.wait_ge(row_loaded[p], 16 * (i + 1))
                    if later(i, 1):
                        pe.wait_ge(sem["rowT_ready"], number(i, p) - 1)
                    for k in range(KC):
                        last = nc.tensor.transpose(ps[:, p, k * P:(k + 1) * P], rows[:, p, k * P:(k + 1) * P],
                                                   ident[:, :])
                    last.then_inc(sem["row_turned"], 1)

                def gate_up(i, p):
                    at = ring(i, p)
                    pe.wait_ge(sem["w_loaded"], 48 * (number(i, p) + 1))
                    pe.wait_ge(sem["rowT_ready"], number(i, p) + 1)
                    if later(i, 1):
                        pe.wait_ge(sem["h_rows"], number(i, p) - 1)
                    for k in range(KC):
                        last = nc.tensor.matmul(ps[:, 2 + p, 0:2 * INNER], rowsT[:, p, k, :],
                                                w_gu[:, bass.ds(at, 1), k, :].rearrange("p a n -> p (a n)"),
                                                start=(k == 0), stop=(k == KC - 1))
                    last.then_inc(sem["gu_psum"], 1)

                def turn_h(i, p):
                    pe.wait_ge(sem["h_rows"], number(i, p) + 1)
                    if later(i, 1):
                        pe.wait_ge(sem["hT_ready"], number(i, p) - 1)
                    for c in range(2):
                        last = nc.tensor.transpose(ps[0:HALF_IN, 4 + p, c * P:(c + 1) * P],
                                                   h[:, p, c * HALF_IN:(c + 1) * HALF_IN], ident[:, :])
                    last.then_inc(sem["h_turned"], 1)

                def down(i, p):
                    at = ring(i, p)
                    pe.wait_ge(sem["hT_ready"], number(i, p) + 1)
                    if later(i, 1):
                        pe.wait_ge(sem["y_ready"], number(i, p) - 1)
                    for c in range(2):
                        last = nc.tensor.matmul(ps[:, 6 + p, :], hT[:, p, c, :],
                                                w_dn[0:HALF_IN, bass.ds(at, 1), c, :].rearrange("p a n -> p (a n)"),
                                                start=(c == 0), stop=(c == 1))
                    last.then_inc(sem["y_psum"], 1)

                def step(i, p):
                    if after(i, p, -1):
                        down(*after(i, p, -1))
                    if after(i, p, 2):
                        turn_rows(*after(i, p, 2))
                    turn_h(i, p)
                    if after(i, p, 1):
                        gate_up(*after(i, p, 1))

                pe.wait_ge(sem["ident_loaded"], 16)
                turn_rows(0, 0)
                turn_rows(0, 1)
                gate_up(0, 0)
                steps(pe, step)
                down(TILES // 2 - 1, 1)

            @block.vector
            def _(dve):
                def keep_rows(i, p):
                    dve.wait_ge(sem["row_turned"], number(i, p) + 1)
                    if later(i, 1):
                        dve.wait_ge(sem["gu_psum"], number(i, p) - 1)
                    nc.vector.tensor_copy(rowsT[:, p, :, :], ps[:, p, :].rearrange("p (k t) -> p k t", k=KC)
                                          ).then_inc(sem["rowT_ready"], 1)

                def step(i, p):
                    dve.wait_ge(sem["silu_done"], number(i, p) + 1)
                    if later(i, 1):
                        dve.wait_ge(sem["h_turned"], number(i, p) - 1)
                    nc.vector.tensor_tensor(h[:, p, :], silu[:, p, :], ps[:, 2 + p, INNER:2 * INNER], ALU.mult
                                            ).then_inc(sem["h_rows"], 1)
                    dve.wait_ge(sem["h_turned"], number(i, p) + 1)
                    if later(i, 1):
                        dve.wait_ge(sem["y_psum"], number(i, p) - 1)
                    nc.vector.tensor_copy(hT[:, p, :, :], ps[0:HALF_IN, 4 + p, 0:2 * P].rearrange(
                        "p (c t) -> p c t", c=2)).then_inc(sem["hT_ready"], 1)
                    if after(i, p, 2):
                        keep_rows(*after(i, p, 2))

                keep_rows(0, 0)
                keep_rows(0, 1)
                steps(dve, step)

            @block.scalar
            def _(act):
                def out_rows(i, p):
                    act.wait_ge(sem["y_psum"], number(i, p) + 1)
                    if later(i, 1):
                        act.wait_ge(y_stored[p], 16 * i)
                    nc.scalar.activation(y[:, p, :], ps[:, 6 + p, :], ACT.Copy).then_inc(sem["y_ready"], 1)

                def step(i, p):
                    act.wait_ge(sem["gu_psum"], number(i, p) + 1)
                    if later(i, 1):
                        act.wait_ge(sem["h_rows"], number(i, p) - 1)
                    nc.scalar.activation(silu[:, p, :], ps[:, 2 + p, 0:INNER], ACT.Silu).then_inc(sem["silu_done"], 1)
                    if after(i, p, -1):
                        out_rows(*after(i, p, -1))
                steps(act, step)
                out_rows(TILES // 2 - 1, 1)

            @block.gpsimd
            def _(pool):
                def load(i, p):
                    if later(i, 1):
                        pool.wait_ge(sem["row_turned"], number(i, p) - 1)
                    pool.dma_start(rows[:, p, :], T["expert_rows"][bass.ds(number(i, p) * P, P), :]
                                   ).then_inc(row_loaded[p], 16)

                def store(i, p):
                    pool.wait_ge(sem["y_ready"], number(i, p) + 1)
                    pool.dma_start(T["expert_out"][bass.ds(number(i, p) * P, P), :], y[:, p, :]
                                   ).then_inc(y_stored[p], 16)

                def step(i, p):
                    if after(i, p, 3):
                        load(*after(i, p, 3))
                    if after(i, p, -1):
                        store(*after(i, p, -1))
                load(0, 0)
                load(0, 1)
                load(1, 0)
                steps(pool, step)
                store(TILES // 2 - 1, 1)
                for s in y_stored:
                    pool.wait_ge(s, 16 * (TILES // 2))


COMBINE_SIGNALS = """part_ready row_ready stats_ready var_ready rstd_ready x_ready out_stored
hidden_ready gate_psum up_psum silu_ready down_psum shared_ready""".split()
HELD = 8


def combine_pass(nc, T, M, sem, gathered):
    hide_before = {1: 0, 2: 1, 3: 2, 4: 3, 6: 4, 7: 5, 8: 6, 9: 7}
    with ExitStack() as ctx:
        sb = lambda name, shape, dt=F32: ctx.enter_context(nc.sbuf_tensor(name, shape, dt))
        st, sh = Held(), Held()
        sh.gate, sh.up, sh.down, sh.sem = M.ws_gate, M.ws_up, M.ws_down, sem
        sh.ps = ctx.enter_context(nc.psum_tensor("ps_combine", [P, 8, 512], F32))
        sh.silu = sb("silu_last", [P, 2, S])
        sh.hidden = sb("hidden_last", [P, NF, S])
        got = sb("got", [P, HELD, TOP, E])
        part = sb("part", [P, 2, TOP - 1, E])
        st.r = st.x = M.acc
        st.stats = sb("stats_o", [P, TT, 6])
        st.meanvar = sb("meanvar_o", [P, TT, 2])
        st.lnvar = sb("lnvar_o", [P, TT])
        st.rstd = sb("rstd_o", [P, TT])
        st.eps = sb("eps_o", [P, 1])
        with nc.Block() as block:
            @block.vector
            def _(dve):
                nc.vector.memset(st.eps[:, :], LN_EPS)
        with nc.Block() as block:
            @block.gpsimd
            def _(pool):
                for i in range(TT):
                    if i >= HELD:
                        pool.wait_ge(sem["row_ready"], i - HELD + 1)
                    for k in range(TOP):
                        nc.gpsimd.indirect_dma_start(
                            got[:, i % HELD, k, :], None, T["expert_out"],
                            bass.IndirectOffsetOnAxis(ap=M.slots[:, i, k:k + 1], axis=0)
                            ).then_inc(gathered[i % HELD], 16)

            @block.tensor
            def _(pe):
                for f in range(NF):
                    shared_gate_up(nc, pe, sh, 0, f, M.xT_last)
                pe.wait_ge(sem["hidden_ready"], NF + 2)
                for j in range(NT):
                    shared_down(nc, pe, sh, 0, j)

            @block.vector
            def _(dve):
                dve.sem_inc(sem["hidden_ready"], 2)
                dve.sem_inc(sem["shared_ready"], 2)

                def row(i):
                    if i in hide_before:
                        shared_hide(nc, dve, sh, 0, hide_before[i])
                    last_block = i - (TT - NT)
                    if last_block >= 0:
                        shared_add(nc, dve, sh, 0, last_block, M.acc[:, i, :], M.x_last[:, last_block, :])
                        dve.wait_ge(sem["shared_ready"], 2 + last_block + 1)
                    dve.wait_ge(gathered[i % HELD], (i // HELD + 1) * (16 * TOP))
                    for k in range(TOP):
                        if k:
                            dve.wait_ge(sem["part_ready"], (TOP - 1) * i + k)
                            before = part[:, i % 2, k - 1, :]
                        else:
                            before = M.acc[:, i, :]
                        dst, s = ((part[:, i % 2, k, :], sem["part_ready"]) if k < TOP - 1
                                  else (st.r[:, i, :], sem["row_ready"]))
                        nc.vector.scalar_tensor_tensor(dst, got[:, i % HELD, k, :], M.weights[:, i, k:k + 1], before,
                                                       ALU.mult, ALU.add).then_inc(s, 1)
                norm_rows(nc, st, sem, dve, row, TT)

            @block.scalar
            def _(act):
                def first(i):
                    if i in hide_before:
                        shared_silu(nc, act, sh, 0, hide_before[i])
                        load_log_exp(nc)
                load_log_exp(nc)
                norm_scale(nc, st, sem, act, TT, first)

            @block.sync
            def _(sp):
                for b in range(NB):
                    sp.wait_ge(sem["x_ready"], NT * (b + 1))
                    sp.dma_start(T["out"][b].rearrange("(j p) d -> p j d", p=P), st.x[:, b * NT:(b + 1) * NT, :]
                                 ).then_inc(sem["out_stored"], 16)
                sp.wait_ge(sem["out_stored"], 16 * NB)


def mixture(nc, T):
    with ExitStack() as ctx:
        held = lambda name, shape, dt=F32: ctx.enter_context(nc.sbuf_tensor(name, shape, dt))
        M = Held()
        combine_sem = signals(nc, ctx, COMBINE_SIGNALS, "combine_")
        gathered = [ctx.enter_context(nc.semaphore(f"gathered{j}")) for j in range(HELD)]
        M.acc = held("acc", [P, TT, E])
        M.slots = held("slots", [P, TT, TOP], U32)
        M.weights = held("weights", [P, TT, TOP])
        M.tile_info = held("tile_info", [4, P], I32)
        M.ring_at = held("ring_at", [4, P], I32)
        M.ws_gate = held("ws_gate", [P, KC, FF])
        M.ws_up = held("ws_up", [P, KC, FF])
        M.ws_down = held("ws_down", [P, NF, E])
        M.xT_last = held("xT_last", [P, KC, S])
        M.x_last = held("x_last", [P, NT, E])
        dispatch_pass(nc, T, M)
        expert_pass(nc, T, M)
        combine_pass(nc, T, M, combine_sem, gathered)


def program(nc, T):
    layers(nc, T)
    mixture(nc, T)


def layout(inputs):
    import numpy as np
    A = {k: np.asarray(v) for k, v in inputs.items()}
    flat = np.ascontiguousarray
    columns = lambda v, n: flat(v.reshape(n, P).T)
    t = np.arange(S, dtype=np.float32)
    inv_freq = (np.float32(1.0) / np.float32(10000.0) ** (np.arange(0, HD, 2, dtype=np.float32) / np.float32(HD))
                ).astype(np.float32)
    angle = (t[:, None] * inv_freq[None, :]).astype(np.float32)
    tiles = lambda a: flat(a.astype(np.float32).reshape(NT, P, -1).transpose(1, 0, 2))
    w_c = np.zeros((P, E), np.float32)
    for c in range(KC):
        w_c[32 * c:32 * c + STATE] = A["L0_attn_C_w"].T
    bias_rows = np.zeros((P, E), np.float32)
    for at, name in ((0, "L0_attn_proj_out_b"), (96, "L0_xattn_b_k")):
        bias_rows[at, :A[name].shape[0]] = A[name]
    ones_at = np.zeros((P, 64), np.float32)
    ones_at[:, 32] = 1.0
    rows = np.arange(P)
    return {
        "x": flat(A["x"]), "xT": flat(A["x"].transpose(0, 2, 1)),
        "ctx": flat(A["ctx_512"]), "ctxT": flat(A["ctx_512"].transpose(0, 2, 1)),
        "w_in": flat(A["L0_attn_proj_in_w"].T), "w_b": flat(A["L0_attn_B_w"].T), "w_c": w_c,
        "w_o": flat(A["L0_attn_proj_out_w"].T), "w_k": flat(A["L0_xattn_W_k"].T), "w_g": flat(A["L0_ffn_Wg"].T),
        "w_0a": flat(A["L0_ffn_W0a"].T), "w_1a": flat(A["L0_ffn_W1a"].T),
        "w_0b": flat(A["L0_ffn_W0b"].T), "w_1b": flat(A["L0_ffn_W1b"].T),
        "w_qkv": flat(A["L1_attn_w_qkv"]), "w_oatt": flat(A["L1_attn_w_out"]),
        "w_oxatt": flat(A["L1_xattn_w_out"].T), "bias_rows": bias_rows,
        "b_in": columns(A["L0_attn_proj_in_b"], KC), "d_param": columns(A["L0_attn_D_param"], KC),
        "b_0a": columns(A["L0_ffn_b0a"], NF), "b_1a": columns(A["L0_ffn_b1a"], NF),
        "b_0b": flat(A["L0_ffn_b0b"]), "b_1b": flat(A["L0_ffn_b1b"]),
        "b_k": columns(A["L0_xattn_b_k"], 1),
        "head_ln": flat(np.stack([np.tile(A["L1_attn_ln_scale"], HG), np.tile(A["L1_attn_ln_bias"], HG)], 1)),
        "a_in": flat(A["L0_attn_A"].reshape(KC, P, STATE).transpose(1, 0, 2)),
        "gamma": flat(A["L0_xattn_ln_gamma"]), "beta": flat(A["L0_xattn_ln_beta"]),
        "q_norm": flat(A["L1_xattn_q_norm_w"]), "k_norm": flat(A["L1_xattn_k_norm_w"]),
        "ident": np.eye(P, dtype=np.float32),
        "causal": np.where(rows[None, :] > rows[:, None], np.float32(-1e30), np.float32(0.0)),
        "ones_at": ones_at,
        "router": flat(A["L1_ffn_router_w"]), "w_gate": flat(A["L1_ffn_w_gate"]), "w_up": flat(A["L1_ffn_w_up"]),
        "w_down": flat(A["L1_ffn_w_down"]), "ws_gate": flat(A["L1_ffn_ws_gate"]), "ws_up": flat(A["L1_ffn_ws_up"]),
        "ws_down": flat(A["L1_ffn_ws_down"]),
        "before": (rows[:, None] < rows[None, :]).astype(np.float32),
        "iota": np.tile(np.arange(EXPERTS, dtype=np.float32), (P, 1)),
        "tile_no": np.stack([rows, rows - 1, rows == 0], 1).astype(np.float32),
        "cos": tiles(np.concatenate([np.cos(angle), np.cos(angle)], 1)),
        "sin": tiles(np.sin(angle)), "msin": tiles(-np.sin(angle)),
    }


def kernel(**inputs):
    import numpy as _np
    import concourse.bacc as _bacc
    from concourse import mybir as _mybir
    from concourse.bass_utils import run_bass_kernel_spmd as _run

    nc = _bacc.Bacc("TRN2", target_bir_lowering=False, num_devices=1)
    arrays, tensors = {}, {}
    for name, a in layout(inputs).items():
        arrays[f"in_{name}"] = a
        tensors[name] = nc.dram_tensor(f"in_{name}", a.shape, _mybir.dt.from_np(a.dtype), kind="ExternalInput").ap()
    tensors["out"] = nc.dram_tensor("out", (NB, S, E), F32, kind="ExternalOutput").ap()
    for name, shape in (("x5", (NB, S, E)), ("x5T", (NB, E, S)), ("expert_rows", (SLOTS, E)), ("expert_out", (SLOTS, E))):
        tensors[name] = nc.dram_tensor(name, shape, F32, kind="Internal").ap()
    program(nc, tensors)
    r = _run(nc, [arrays], core_ids=[0])
    return r.results[0]["out"]
```
